# Optimizing a Trainium2 kernel written in Bass

```python
import numpy as np
import jax
import jax.numpy as jnp

def _softmax(x, axis=-1):
    return jax.nn.softmax(x, axis=axis)

def _gelu(x):
    return jax.nn.gelu(x, approximate=True)

def _silu(x):
    return jax.nn.silu(x)

def _sigmoid(x):
    return jax.nn.sigmoid(x)

def _layernorm(x, axis=-1, eps=1e-05):
    m = jnp.mean(x, axis=axis, keepdims=True)
    v = jnp.var(x, axis=axis, keepdims=True)
    return (x - m) / jnp.sqrt(v + eps)

def _scatter_add(tgt, idx, src, axis=0):
    return tgt.at[idx].add(src)

def _segment_sum(src, seg, n):
    return jax.ops.segment_sum(src, seg, n)
kernel_name = 'mk_vit_tower_d2_tok_img512_r4_90108b'

def setup_inputs(seed: int=0):
    np.random.seed(seed)
    _w = jnp.asarray

    def _rec_inputs():
        import jax
        import jax.numpy as jnp
        _rk = jax.random.key(seed)
        x = -7.10856e-05 + 0.999911 * jax.random.normal(jax.random.fold_in(_rk, 1), (128, 64, 64, 128), jnp.float32)
        return x
    x = _rec_inputs()

    def _L0_tok_setup():
        import jax, jax.numpy as jnp
        import numpy as np
        from jax import lax
        B, H, W, C = (32, 64, 64, 128)
        POOL = 8
        STRIDE = 8
        key = jax.random.key(seed)
        k1, k2, k3 = jax.random.split(key, 3)
        x = jax.random.normal(k1, (B, H, W, C), dtype=jnp.float32)
        conv_w = jax.random.normal(k2, (3, 3, 1, C), dtype=jnp.float32) * 0.02
        conv_b = jax.random.normal(k3, (C,), dtype=jnp.float32) * 0.02
        return {'x': x, 'conv_w': conv_w, 'conv_b': conv_b}
    _L0_tok_all = _L0_tok_setup()
    _L0_tok_in = {k: v for k, v in _L0_tok_all.items() if k in ('conv_w', 'conv_b')}
    del _L0_tok_all

    def _L0_attn_setup():
        import jax, jax.numpy as jnp
        import numpy as np
        EMBED_DIM = 128
        key = jax.random.key(seed)
        k1, k2, k3 = jax.random.split(key, 3)
        B, T, E = (8, 512, EMBED_DIM)
        x = jax.random.normal(k1, (B, T, E), dtype=jnp.float32)
        Wq = jax.random.normal(k2, (E, E), dtype=jnp.float32) * E ** (-0.5)
        bq = jnp.zeros((E,), dtype=jnp.float32)
        Wk = jax.random.normal(k3, (E, E), dtype=jnp.float32) * E ** (-0.5)
        bk = jnp.zeros((E,), dtype=jnp.float32)
        return {'x': x, 'Wq': Wq, 'bq': bq, 'Wk': Wk, 'bk': bk}
    _L0_attn_all = _L0_attn_setup()
    _L0_attn_in = {k: v for k, v in _L0_attn_all.items() if k in ('Wq', 'bq', 'Wk', 'bk')}
    del _L0_attn_all

    def _L0_ffn_setup():
        import jax, jax.numpy as jnp
        import numpy as np
        B, S, D, F, E, NS, K = (2, 512, 128, 512, 8, 2, 2)
        key = jax.random.key(seed)
        ks = jax.random.split(key, 6)
        scale = 0.02

        def p(k, shape):
            return jax.random.normal(k, shape, jnp.float32) * scale
        return {'x': jax.random.normal(ks[0], (B, S, D), jnp.float32), 'gate_w': p(ks[1], (E, D)), 'gate_b': jnp.zeros((E,), jnp.float32), 'sw1': p(ks[2], (NS, F, D)), 'sb1': jnp.zeros((NS, F), jnp.float32), 'sw2': p(ks[3], (NS, D, F)), 'sb2': jnp.zeros((NS, D), jnp.float32), 'rw1': p(ks[4], (E, F, D)), 'rb1': jnp.zeros((E, F), jnp.float32), 'rw2': p(ks[5], (E, D, F)), 'rb2': jnp.zeros((E, D), jnp.float32)}
    _L0_ffn_all = _L0_ffn_setup()
    _L0_ffn_in = {k: v for k, v in _L0_ffn_all.items() if k in ('gate_w', 'gate_b', 'sw1', 'sb1', 'sw2', 'sb2', 'rw1', 'rb1', 'rw2', 'rb2')}
    del _L0_ffn_all

    def _L1_attn_setup():
        import math
        import jax, jax.numpy as jnp
        import numpy as np
        D_MODEL = 128
        N_HEADS = 8
        HD = D_MODEL // N_HEADS
        RATIO = 8
        STRIDE = 4
        WINDOW = 128
        THETA = 10000.0

        def _rope_freqs(L):
            half = HD // 2
            inv_freq = 1.0 / THETA ** (jnp.arange(half, dtype=jnp.float32) / half)
            t = jnp.arange(L, dtype=jnp.float32)
            f = t[:, None] * inv_freq[None, :]
            return (jnp.cos(f), jnp.sin(f))

        def _apply_rope(x, cos, sin):
            half = x.shape[-1] // 2
            x1, x2 = (x[..., :half], x[..., half:])
            cos = cos[None, None]
            sin = sin[None, None]
            return jnp.concatenate([x1 * cos - x2 * sin, x1 * sin + x2 * cos], axis=-1)
        key = jax.random.key(seed)
        ks = jax.random.split(key, 9)
        B, L, D = (2, 512, D_MODEL)
        s = 0.02
        return {'x': jax.random.normal(ks[0], (B, L, D), dtype=jnp.float32), 'wq': jax.random.normal(ks[1], (D, D), dtype=jnp.float32) * s, 'wk': jax.random.normal(ks[2], (D, D), dtype=jnp.float32) * s, 'wv': jax.random.normal(ks[3], (D, D), dtype=jnp.float32) * s, 'wo': jax.random.normal(ks[4], (D, D), dtype=jnp.float32) * s, 'wk_c': jax.random.normal(ks[5], (D, D), dtype=jnp.float32) * s, 'wv_c': jax.random.normal(ks[6], (D, D), dtype=jnp.float32) * s, 'gate_logits': jax.random.normal(ks[7], (RATIO,), dtype=jnp.float32) * s, 'sink_logit': jnp.zeros((N_HEADS, 1), dtype=jnp.float32)}
    _L1_attn_all = _L1_attn_setup()
    _L1_attn_in = {k: v for k, v in _L1_attn_all.items() if k in ('wq', 'wk', 'wv', 'wo', 'wk_c', 'wv_c', 'gate_logits', 'sink_logit')}
    del _L1_attn_all

    def _L1_ffn_setup():
        import jax, jax.numpy as jnp
        import numpy as np
        T = 128
        B = 64
        C = 256

        def _triu_apply(x, W, b):
            Wm = jnp.tril(W)
            return jnp.einsum('bct,st->bcs', x, Wm) + b
        key = jax.random.key(seed)
        ks = jax.random.split(key, 5)
        x = jax.random.normal(ks[0], (B, C, T), dtype=jnp.float32)
        scale = 1.0 / jnp.sqrt(jnp.arange(1, T + 1, dtype=jnp.float32))[:, None]
        W1 = jax.random.uniform(ks[1], (T, T), jnp.float32, -1.0, 1.0) * scale
        b1 = jax.random.uniform(ks[2], (T,), jnp.float32, -1.0, 1.0) * scale[:, 0]
        W2 = jax.random.uniform(ks[3], (T, T), jnp.float32, -1.0, 1.0) * scale
        b2 = jax.random.uniform(ks[4], (T,), jnp.float32, -1.0, 1.0) * scale[:, 0]
        return {'x': x, 'W1': W1, 'b1': b1, 'W2': W2, 'b2': b2}
    _L1_ffn_all = _L1_ffn_setup()
    _L1_ffn_in = {k: v for k, v in _L1_ffn_all.items() if k in ('W1', 'b1', 'W2', 'b2')}
    del _L1_ffn_all
    return {'x': x, 'L0_tok_conv_w': _L0_tok_in['conv_w'], 'L0_tok_conv_b': _L0_tok_in['conv_b'], 'L0_attn_Wq': _L0_attn_in['Wq'], 'L0_attn_bq': _L0_attn_in['bq'], 'L0_attn_Wk': _L0_attn_in['Wk'], 'L0_attn_bk': _L0_attn_in['bk'], 'L0_ffn_gate_w': _L0_ffn_in['gate_w'], 'L0_ffn_gate_b': _L0_ffn_in['gate_b'], 'L0_ffn_sw1': _L0_ffn_in['sw1'], 'L0_ffn_sb1': _L0_ffn_in['sb1'], 'L0_ffn_sw2': _L0_ffn_in['sw2'], 'L0_ffn_sb2': _L0_ffn_in['sb2'], 'L0_ffn_rw1': _L0_ffn_in['rw1'], 'L0_ffn_rb1': _L0_ffn_in['rb1'], 'L0_ffn_rw2': _L0_ffn_in['rw2'], 'L0_ffn_rb2': _L0_ffn_in['rb2'], 'L1_attn_wq': _L1_attn_in['wq'], 'L1_attn_wk': _L1_attn_in['wk'], 'L1_attn_wv': _L1_attn_in['wv'], 'L1_attn_wo': _L1_attn_in['wo'], 'L1_attn_wk_c': _L1_attn_in['wk_c'], 'L1_attn_wv_c': _L1_attn_in['wv_c'], 'L1_attn_gate_logits': _L1_attn_in['gate_logits'], 'L1_attn_sink_logit': _L1_attn_in['sink_logit'], 'L1_ffn_W1': _L1_ffn_in['W1'], 'L1_ffn_b1': _L1_ffn_in['b1'], 'L1_ffn_W2': _L1_ffn_in['W2'], 'L1_ffn_b2': _L1_ffn_in['b2']}

def reference(x, L0_tok_conv_w, L0_tok_conv_b, L0_attn_Wq, L0_attn_bq, L0_attn_Wk, L0_attn_bk, L0_ffn_gate_w, L0_ffn_gate_b, L0_ffn_sw1, L0_ffn_sb1, L0_ffn_sw2, L0_ffn_sb2, L0_ffn_rw1, L0_ffn_rb1, L0_ffn_rw2, L0_ffn_rb2, L1_attn_wq, L1_attn_wk, L1_attn_wv, L1_attn_wo, L1_attn_wk_c, L1_attn_wv_c, L1_attn_gate_logits, L1_attn_sink_logit, L1_ffn_W1, L1_ffn_b1, L1_ffn_W2, L1_ffn_b2):
    import jax
    import jax.numpy as jnp

    def _L0_tok_ref(x, conv_w, conv_b):
        import jax, jax.numpy as jnp
        import numpy as np
        from jax import lax
        B, H, W, C = (32, 64, 64, 128)
        POOL = 8
        STRIDE = 8
        y = lax.conv_general_dilated(x, conv_w, window_strides=(1, 1), padding=[(1, 1), (1, 1)], dimension_numbers=('NHWC', 'HWIO', 'NHWC'), feature_group_count=C) + conv_b
        y = lax.reduce_window(y, jnp.float32(0.0), lax.add, (1, POOL, POOL, 1), (1, STRIDE, STRIDE, 1), 'VALID') / jnp.float32(POOL * POOL)
        b = y.shape[0]
        ct = y.reshape(b, -1, C)
        return ct

    def _L0_attn_ref(x, Wq, bq, Wk, bk):
        import jax, jax.numpy as jnp
        import numpy as np
        EMBED_DIM = 128
        scaling = jnp.float32(EMBED_DIM ** (-0.5))
        q = (x @ Wq + bq) * scaling
        k = x @ Wk + bk
        scores = jnp.einsum('bqe,bke->bqk', q, k)
        attn = jax.nn.softmax(scores, axis=-1)
        return jnp.einsum('bqk,bke->bqe', attn, x)

    def _L0_ffn_ref(x, gate_w, gate_b, sw1, sb1, sw2, sb2, rw1, rb1, rw2, rb2):
        import jax, jax.numpy as jnp
        import numpy as np
        B, S, D, F, E, NS, K = (2, 512, 128, 512, 8, 2, 2)
        b, s, d = x.shape
        t = x.reshape(-1, d)
        T = t.shape[0]
        hs = jax.nn.gelu(jnp.einsum('td,nfd->ntf', t, sw1) + sb1[:, None, :], approximate=False)
        shared = jnp.einsum('ntf,ndf->td', hs, sw2) + sb2.sum(axis=0)
        logits = t @ gate_w.T + gate_b
        probs = jax.nn.softmax(logits, axis=-1)
        top_v, top_i = jax.lax.top_k(probs, K)
        cw = jnp.zeros_like(probs).at[jnp.arange(T)[:, None], top_i].add(top_v)
        hr = jax.nn.gelu(jnp.einsum('td,efd->etf', t, rw1) + rb1[:, None, :], approximate=False)
        oe = jnp.einsum('etf,edf->etd', hr, rw2) + rb2[:, None, :]
        routed = jnp.einsum('etd,te->td', oe, cw)
        return (shared + routed).reshape(b, s, d)

    def _L1_attn_ref(x, wq, wk, wv, wo, wk_c, wv_c, gate_logits, sink_logit):
        import math
        import jax, jax.numpy as jnp
        import numpy as np
        D_MODEL = 128
        N_HEADS = 8
        HD = D_MODEL // N_HEADS
        RATIO = 8
        STRIDE = 4
        WINDOW = 128
        THETA = 10000.0

        def _rope_freqs(L):
            half = HD // 2
            inv_freq = 1.0 / THETA ** (jnp.arange(half, dtype=jnp.float32) / half)
            t = jnp.arange(L, dtype=jnp.float32)
            f = t[:, None] * inv_freq[None, :]
            return (jnp.cos(f), jnp.sin(f))

        def _apply_rope(x, cos, sin):
            half = x.shape[-1] // 2
            x1, x2 = (x[..., :half], x[..., half:])
            cos = cos[None, None]
            sin = sin[None, None]
            return jnp.concatenate([x1 * cos - x2 * sin, x1 * sin + x2 * cos], axis=-1)
        B, L, D = x.shape
        f32 = jnp.float32

        def heads(t):
            return t.reshape(B, L, N_HEADS, HD).transpose(0, 2, 1, 3)
        q = heads(x @ wq.T)
        k = heads(x @ wk.T)
        v = heads(x @ wv.T)
        cos, sin = _rope_freqs(L)
        q = _apply_rope(q.astype(f32), cos, sin).astype(x.dtype)
        k = _apply_rope(k.astype(f32), cos, sin).astype(x.dtype)
        n_windows = max(1, (L - RATIO) // STRIDE + 1)
        idx = jnp.clip(jnp.arange(RATIO)[None, :] + jnp.arange(n_windows)[:, None] * STRIDE, 0, L - 1)
        windows = x[:, idx, :]
        gate_w = jax.nn.softmax(gate_logits)
        x_c = jnp.einsum('bwrd,r->bwd', windows, gate_w)
        Lc = n_windows
        k_c = x_c @ wk_c.T
        v_c = x_c @ wv_c.T
        k_c = k_c.reshape(B, Lc, N_HEADS, HD).transpose(0, 2, 1, 3)
        v_c = v_c.reshape(B, Lc, N_HEADS, HD).transpose(0, 2, 1, 3)
        scale = math.sqrt(HD)
        pos = jnp.arange(L)
        comp_scores = jnp.einsum('bhqd,bhkd->bhqk', q, k_c) / scale
        entry_end = jnp.arange(Lc) * STRIDE + RATIO - 1
        causal_c = pos[:, None] >= entry_end[None, :]
        comp_scores = jnp.where(causal_c[None, None], comp_scores, -jnp.inf)
        win_scores = jnp.einsum('bhqd,bhkd->bhqk', q, k) / scale
        dist = pos[:, None] - pos[None, :]
        win_mask = (dist >= 0) & (dist < WINDOW)
        win_scores = jnp.where(win_mask[None, None], win_scores, -jnp.inf)
        sink = jnp.broadcast_to(sink_logit[None, :, None, :], (B, N_HEADS, L, 1))
        all_scores = jnp.concatenate([comp_scores.astype(f32), win_scores.astype(f32), sink.astype(f32)], axis=-1)
        attn = jax.nn.softmax(all_scores, axis=-1).astype(x.dtype)
        w_comp = attn[..., :Lc]
        w_win = attn[..., Lc:Lc + L]
        out = jnp.einsum('bhqk,bhkd->bhqd', w_comp, v_c) + jnp.einsum('bhqk,bhkd->bhqd', w_win, v)
        out = out.transpose(0, 2, 1, 3).reshape(B, L, D)
        return out @ wo.T

    def _L1_ffn_ref(x, W1, b1, W2, b2):
        import jax, jax.numpy as jnp
        import numpy as np
        T = 128
        B = 64
        C = 256

        def _triu_apply(x, W, b):
            Wm = jnp.tril(W)
            return jnp.einsum('bct,st->bcs', x, Wm) + b
        h = _triu_apply(x, W1, b1)
        h = jax.nn.gelu(h, approximate=False)
        return _triu_apply(h, W2, b2)
    h = _L0_tok_ref(x, L0_tok_conv_w, L0_tok_conv_b)
    h = h + _L0_attn_ref(_layernorm(h, axis=-1), L0_attn_Wq, L0_attn_bq, L0_attn_Wk, L0_attn_bk)
    h = h + _L0_ffn_ref(_layernorm(h, axis=-1), L0_ffn_gate_w, L0_ffn_gate_b, L0_ffn_sw1, L0_ffn_sb1, L0_ffn_sw2, L0_ffn_sb2, L0_ffn_rw1, L0_ffn_rb1, L0_ffn_rw2, L0_ffn_rb2)
    h = h + _L1_attn_ref(_layernorm(h, axis=-1), L1_attn_wq, L1_attn_wk, L1_attn_wv, L1_attn_wo, L1_attn_wk_c, L1_attn_wv_c, L1_attn_gate_logits, L1_attn_sink_logit)
    h = h + _L1_ffn_ref(_layernorm(h, axis=-1), L1_ffn_W1, L1_ffn_b1, L1_ffn_W2, L1_ffn_b2)
    return h

_drawn_inputs = setup_inputs


def setup_inputs(seed=0):
    import zlib

    import numpy as np

    out = dict(_drawn_inputs(seed))
    spreads = {'L0_attn_bq': (0.0, 2.0),
     'L0_attn_bk': (0.0, 2.0),
     'L0_ffn_gate_b': (0.0, 0.8),
     'L0_ffn_sb1': (0.0, 0.294),
     'L0_ffn_sb2': (0.0, 0.1),
     'L0_ffn_rb1': (0.0, 0.8),
     'L0_ffn_rb2': (0.0, 0.1),
     'L1_attn_sink_logit': (0.0, 2.0)}
    factors = {'L0_ffn_rw1': 3.944,
     'L0_ffn_rw2': 3.51,
     'L1_attn_wq': 8.0,
     'L1_attn_wk': 8.0,
     'L1_attn_wk_c': 8.0,
     'L1_attn_wv_c': 7.513,
     'L1_attn_gate_logits': 64.0,
     'L0_attn_Wq': 2.705}
    for name, (base, spread) in spreads.items():
        noise = np.random.default_rng([zlib.crc32(name.encode()), seed]).standard_normal(out[name].shape)
        drawn = base * np.exp(spread * noise) if base else spread * noise
        out[name] = jnp.asarray(drawn.astype(out[name].dtype))
    for name, factor in factors.items():
        out[name] = (out[name] * factor).astype(out[name].dtype)
    return out
```

```python
import concourse.bass as bass
from concourse import mybir
from contextlib import ExitStack

fp32 = mybir.dt.float32
bf16 = mybir.dt.bfloat16
ALU = mybir.AluOpType
ACT = mybir.ActivationFunctionType
AX = mybir.AxisListType

NI, HW, C = 128, 64, 128
P = 128
BX = 8
L = BX * BX
GI = 8
NG = NI // GI
T = GI * L // P
N = T * P
NS, NE, F = 2, 8, 512
NX = NS + NE
FC = F // P
CH = NX * FC
HEADS, HD = 8, C // 8
RATIO, STRIDE = 8, 4
LC = (L - RATIO) // STRIDE + 1
LK = L + LC
HH = HEADS // 2
PB = 3 * 2 * BX
EPS = 1e-5
RING = 4
SLOTS = CH
KIND_X = (1, 0, 7)

PLAN = {"pe": [], "act": [], "dve": [], "pool": []}


def place(stage, piece, **where):
    for engine, position in where.items():
        PLAN[engine].append((position, stage, piece))


EXPS, RATE, GAP = 21.3, 0.95, 2
for q in range(CH):
    u = RATE * q + (GAP if RATE * q + 1 > EXPS else 0)
    place("ffn", ("up", q), pe=u)
    place("ffn", ("hidden", q), act=u + 1, dve=u + 2)
    place("ffn", ("down", q), pe=u + 3.9)
    if q % FC == FC - 1 and q // FC >= NS - 1:
        place("ffn", ("sum", q), dve=u + 4.25, pool=u + 4.7)

for u in range(T):
    for v in range(2):
        for k, p in enumerate((0.5, 1.5, 1.6)):
            place("tok", ("add", u, 3 * v + k), dve=9 * u + 4 * v + p)
    for k, (p, a) in enumerate(((2.5, 3.4), (3.5, None), (6.5, 7.4), (7.3, 8.3))):
        place("tok", ("pool", u, k), pe=9 * u + p)
        if a:
            place("tok", ("pool", u, k), act=9 * u + a)
for n in range(15):
    place("tok", ("tap", 0, n), dve=18.3 + 0.45 * n)
    place("tok", ("tap", 1, n), dve=35.6 + 0.24 * n)
place("tok", ("out", 0, 0), pe=39.6, act=39.99)

for n, where in enumerate((
        dict(dve=0.3, pool=0.8), dict(dve=1.3, pe=2.3, act=2.8), dict(pe=3.8, act=4.3), dict(pe=5.5, act=6.0),
        dict(pe=7.0, dve=7.8), dict(dve=8.5), dict(act=EXPS), dict(dve=23.9, pe=24.2, act=24.6),
        dict(pe=25.5, dve=26.1), dict(dve=26.7, pool=27.2), dict(dve=27.7, pe=28.4, act=28.9),
        dict(pe=30.1, dve=30.7, pool=31.2), dict(dve=31.9), dict(pe=35, act=35.6))):
    place("att", (n,), **where)
place("att", ("low",), dve=29.8)

for n, where in enumerate((
        dict(pe=5.9, dve=6.4), dict(dve=6.5, pool=6.9), dict(dve=7.4, pe=8.3, act=8.6), dict(pe=9.4, dve=10, pool=10.9),
        dict(pe=10.7, dve=11.4, pool=12), dict(dve=9.6, pe=12.3, act=12.7), dict(pe=12.6, act=13.2, pool=13.5),
        dict(pe=13.4, act=14, pool=14.6))):
    place("sec", ("pre", n), **where)
for n in range(8):
    place("sec", ("score", n), pe=15 + 0.65 * n, dve=15.6 + 0.65 * n)
    if n in (2, 4):
        place("sec", ("score", n), pool=15.6 + 0.65 * n)
place("sec", ("exp", 0), act=EXPS + 0.01)
for n in range(8):
    place("sec", ("turn", n), pe=22.9 + 0.8 * n, act=23.4 + 0.8 * n, dve=22.9 + 0.8 * n)
    place("sec", ("value", n), pe=23.8 + 0.8 * n, dve=24.3 + 0.8 * n)
for n, where in enumerate((
        dict(pe=30.3, act=30.7), dict(pe=31.4, dve=31.8, pool=32.9), dict(dve=31.85, pool=32.4),
        dict(dve=32.8, pe=33.6, act=34), dict(pe=34.7, act=35.3), dict(pe=36, dve=36.5, act=36.9))):
    place("sec", ("post", n), **where)

for pieces in PLAN.values():
    pieces.sort(key=lambda p: (p[0] % SLOTS, p[1], p[2][1:]))
STAGES = ("tok", "att", "ffn", "sec")
assert all(p[1] == "ffn" for pieces in PLAN.values() for p in pieces if p[0] >= SLOTS)


def after(g, n):
    return not isinstance(g, int) or g >= n


def program(nc, x, conv_w, conv_b, wq, bq, wk, bk, gate_w, gate_b, w1, b1, w2, sb2, rb2,
            swq, swqs, swk, swks, swv, swkc, swvc, swo, comp_gate, sink, tw1, tb1, tw2, tb2,
            ident_c, block_c, cos_c, sin_c, mask1_c, mask2_c, heads_c, pick_c, tie_c, out):
    with ExitStack() as ctx:
        per = {}
        kept = []

        def sb(name, shape, dt=fp32):
            return ctx.enter_context(nc.sbuf_tensor(name, shape, dt))

        def pb(name):
            return ctx.enter_context(nc.psum_tensor(name, [P, 512], fp32))

        def sem(name, n=1):
            s = ctx.enter_context(nc.semaphore(name))
            per[id(s)] = n
            kept.append(s)
            return s

        def at(s, g, k):
            return g * per[id(s)] + k

        ident = sb("ident", [P, P])
        ident_b = sb("ident_b", [P, P], bf16)
        block_sum = sb("block_sum", [P, PB])
        cos = sb("cos", [P, L])
        sin = sb("sin", [P, L])
        mask1 = sb("mask1", [P, P])
        mask2 = sb("mask2", [P, LK])
        heads = sb("heads", [P, HEADS])
        pick_b = sb("pick_b", [3 * NE, NE, P], bf16)
        tie = sb("tie", [P, NE, NE])
        cwt = sb("cwt", [P, 9])
        cb = sb("cb", [P, 1])
        tapw = sb("tapw", [P, 15])
        wq_s, wk_s = sb("wq_s", [C, C]), sb("wk_s", [C, C])
        bq_s, bqs_s, bk_s = sb("bq_s", [C, 1]), sb("bqs_s", [C, 1]), sb("bk_s", [C, 1])
        gw = sb("gw", [C, NE])
        gb = sb("gb", [P, NE])
        w1h, w1l = sb("w1h", [P, NX, F], bf16), sb("w1l", [P, NX, F], bf16)
        w2h, w2l = sb("w2h", [P, NX, F], bf16), sb("w2l", [P, NX, F], bf16)
        b1_s = sb("b1_s", [P, CH])
        sb2_s, sb2_sum = sb("sb2_s", [C, NS]), sb("sb2_sum", [C, 1])
        rb2_s = sb("rb2_s", [C, NE])
        second = {}
        for name in ("q", "qs", "k", "ks", "v", "kc", "vc", "o"):
            second[name] = sb("second_" + name, [C, C])
        cg = sb("cg", [P, RATIO])
        cg_max, cg_sum, cg_inv = sb("cg_max", [P, 1]), sb("cg_sum", [P, 1]), sb("cg_inv", [P, 1])
        sink_s = sb("sink_s", [P, HEADS])
        tw1_s, tw2_s = sb("tw1_s", [P, P]), sb("tw2_s", [P, P])
        tb1_s, tb2_s = sb("tb1_s", [P, 1]), sb("tb2_s", [P, P])
        power = sb("power", [P, T])
        euler = sb("euler", [P, T * NE])
        xbuf = [sb(f"xbuf{i}", [P, HW // 2, C]) for i in range(2)]
        blocks = [b[:].rearrange("p (b x) c -> p b x c", x=8) for b in xbuf]
        pooled_s = sb("pooled_s", [P, 3, 3, T, P])
        taps = sb("taps", [C, T, P])
        cols0 = sb("cols0", [C, T, P])
        h0 = [sb(f"h0_{i}", [P, T, C]) for i in range(2)]
        h1 = [sb(f"h1_{i}", [P, T, C]) for i in range(2)]
        x2h = [sb(f"x2h_{i}", [C, N], bf16) for i in range(2)]
        x2l = [sb(f"x2l_{i}", [C, N], bf16) for i in range(2)]
        share_t = [sb(f"share_t{i}", [3 * NE, N], bf16) for i in range(2)]
        mo1, mv1, rs1 = sb("mo1", [P, T, 6]), sb("mv1", [P, T, 2]), sb("rs1", [P, T])
        ve1 = sb("ve1", [P, T])
        mo2, mv2, rs2 = sb("mo2", [P, T, 6]), sb("mv2", [P, T, 2]), sb("rs2", [P, T])
        ve2 = sb("ve2", [P, T])
        x1, x1t = sb("x1", [P, T, C]), sb("x1t", [C, N])
        q1, k1 = sb("q1", [C, N]), sb("k1", [C, N])
        s1 = sb("s1", [P, T, P])
        p1t = q1[:].rearrange("p (t k) -> p t k", t=T)
        nmax1, den1, inv1 = sb("nmax1", [P, T]), sb("den1", [P, T]), sb("inv1", [P, T])
        x2, x2f = k1[:].rearrange("p (t c) -> p t c", t=T), x1t
        lg, lmax, ez = sb("lg", [P, T, NE]), sb("lmax", [P, T]), sb("ez", [P, T, NE])
        esum, einv, prob = sb("esum", [P, T]), sb("einv", [P, T]), sb("prob", [P, T, NE])
        above, equal = [s1[:, 2 * k:2 * k + 2, :].rearrange("p t (a e j) -> p (t a) e j", a=2, e=NE) for k in range(2)]
        rank, share = sb("rank", [P, T, NE]), sb("share", [P, T, NE])
        rest1, rest2 = sb("rest1", [P, T, NE]), sb("rest2", [P, T, NE])
        parts = sb("parts", [P, T, 3, NE], bf16)
        hid = sb("hid", [P, 2, F])
        hid_h, hid_l = sb("hid_h", [P, RING, F], bf16), sb("hid_l", [P, RING, F], bf16)
        share_b = sb("share_b", [P, 2, N])
        pick = share_b[0:3 * NE].rearrange("p a (e q) -> p (a e) q", q=P)
        part = sb("part", [C, 2, N])
        moe = sb("moe", [C, N])
        mo3, mv3, rs3 = sb("mo3", [P, T, 6]), sb("mv3", [P, T, 2]), sb("rs3", [P, T])
        ve3 = sb("ve3", [P, T])
        mo4, mv4, rs4 = sb("mo4", [P, T, 6]), sb("mv4", [P, T, 2]), sb("rs4", [P, T])
        ve4 = sb("ve4", [P, T])
        h2 = sb("h2", [P, T, C])
        x3, x3t = sb("x3", [P, T, C]), sb("x3t", [C, N])
        q3 = sb("q3", [C, N])
        keys = sb("keys", [C, GI, LK])
        xc = sb("xc", [C, GI, LC])
        values = sb("values", [LK, GI, C])
        keys_h = sb("keys_h", [C, 2, 2, HEADS, LK])
        roped = keys_h[:, 0].rearrange("p i h k -> p (i h k)")[:, 0:2 * N].rearrange("p (a n) -> p a n", a=2)
        s3 = sb("s3", [P, 2, HH, LK + 1])
        m3 = sb("m3", [P, 2, HH])
        e3 = sb("e3", [P, 2 * T, HH, LK + 1])
        den3, inv3 = sb("den3", [P, 2 * T, HH]), sb("inv3", [P, 2 * T, HH])
        p3t = sb("p3t", [LK, 2, HH, P])
        o3, h3 = x3, sb("h3", [P, T, C])
        o3t = sb("o3t", [C, N])
        h3b, res = h2, h3

        pool_bank = [pb("pool_bank0"), pb("pool_bank1")]
        hid_bank = [pb("hid_bank0"), pb("hid_bank1")]
        down_bank = pb("down_bank")
        att_bank = pb("att_bank")
        sec_bank = [pb("sec_bank0"), pb("sec_bank1")]

        consts_in = sem("consts_in")
        weight_in = [sem(f"weight_in{i}") for i in range(2)]
        weight_split = sem("weight_split")
        ready_d, ready_a, ready_p = sem("setup_vector"), sem("setup_scalar"), sem("setup_pool")
        x_in = [sem(f"x_in{i}", 16 * T) for i in range(2)]
        x_summed = sem("x_summed", 6 * T)
        pooled = sem("pooled", 4 * T)
        pooled_read = sem("pooled_read", 3 * T)
        tapped = sem("tapped", 32)
        h0_turned, h0_ready = sem("h0_turned"), sem("h0_ready")
        mom1, rstd1, x1_ready = sem("mom1", 10), sem("rstd1"), sem("x1_ready", 4)
        x1_turned, x1t_ready = sem("x1_turned"), sem("x1t_ready")
        q1_done, q1_ready, k1_done, k1_ready = sem("q1_done"), sem("q1_ready"), sem("k1_done"), sem("k1_ready")
        s1_done, s1_masked, s1_max = sem("s1_done"), sem("s1_masked"), sem("s1_max")
        p1_ready, p1_turned, p1t_ready, inv1_ready = sem("p1_ready", 4), sem("p1_turned"), sem("p1t_ready"), sem("inv1_ready")
        o1_done, h1_ready = sem("o1_done"), sem("h1_ready", 4)
        mom2, rstd2, x2_ready = sem("mom2", 10), sem("rstd2"), sem("x2_ready", 4)
        x2_turned, x2_copied, x2l_ready = sem("x2_turned"), sem("x2_copied", 2), sem("x2l_ready")
        gate_done, gate_step, gate_exp = sem("gate_done"), sem("gate_step", 17), sem("gate_exp")
        share_turned, share_ready = sem("share_turned"), sem("share_ready")
        items = CH + NE
        hid_done = sem("hid_done", items)
        hid_made = sem("hid_made", 2 * CH + NE)
        hid_rest = sem("hid_rest", CH)
        hid_used = sem("hid_used", CH)
        down_read = sem("down_read", 1 + NE)
        moe_added = sem("moe_added", NE)
        moe_turned, h2_ready = sem("moe_turned"), sem("h2_ready")
        mom3, rstd3, x3_ready = sem("mom3", 10), sem("rstd3"), sem("x3_ready", 4)
        x3_turned, x3t_ready = sem("x3_turned"), sem("x3t_ready")
        rope_done, rope_read, rope_added = sem("rope_done", 4), sem("rope_read", 4), sem("rope_added", 2)
        xc_step, kc_done, kc_ready = sem("xc_step", 8), sem("kc_done"), sem("kc_ready")
        v_done, v_ready = sem("v_done", 2), sem("v_ready", 2)
        keys_ready, scored, s3_step = sem("keys_ready", 4), sem("scored", 8), sem("s3_step", 24)
        e3_ready, inv3_step = sem("e3_ready", 2), sem("inv3_step", 3)
        p3_turned, p3t_ready = sem("p3_turned", 8), sem("p3t_ready", 8)
        o3_done, o3_ready = sem("o3_done", 8), sem("o3_ready", 8)
        o3_turned, o3t_ready = sem("o3_turned"), sem("o3t_ready")
        wo_done, h3_ready, h3b_ready = sem("wo_done"), sem("h3_ready"), sem("h3b_ready")
        mom4, rstd4, x4_ready = sem("mom4", 10), sem("rstd4"), sem("x4_ready", 4)
        x4_turned, x4t_ready = sem("x4_turned"), sem("x4t_ready")
        up_done, up_ready, mlp_done = sem("up_done"), sem("up_ready"), sem("mlp_done")
        res_ready, res_stored = sem("res_ready"), sem("res_stored", 16)

        first = [q + max(0, q // FC - NS + 1) for q in range(CH)]
        def made(n):
            shares = sum(1 for r in range(NE) if first[(NS + r) * FC] - 1 < n)
            return 2 * (n - shares) + shares

        def schedule(iteration):
            def run(eng):
                for i in range(LAG_ALL + 1):
                    iteration(i, i)
                with eng.Fori(0, (NG - LAG_ALL - 1) // 2) as j:
                    for k in range(2):
                        iteration(j * 2 + (LAG_ALL + 1 + k), LAG_ALL + 1 + k)
                for i in range(NG, NG + LAG_ALL):
                    iteration(i, i)
            return run

        LAG_ALL = 3
        assert (NG - LAG_ALL - 1) % 2 == 0

        def stages(i, where):
            out = []
            for lag in range(4):
                on = 0 <= where - lag < NG or not isinstance(i, int)
                out.append((i - lag, (where - lag) % 2) if on else (None, 0))
            return out

        def pieces(plan, i, where):
            now, before = stages(i, where), stages(i - 1, where - 1)
            for position, stage, piece in plan:
                g, b = (before if position >= SLOTS else now)[STAGES.index(stage)]
                if g is not None:
                    yield g, b, stage, piece

        loads = [(ident, ident_c), (block_sum, block_c), (cos, cos_c), (sin, sin_c), (mask1, mask1_c),
                 (mask2, mask2_c), (heads, heads_c), (pick, pick_c), (tie, tie_c), (cwt, conv_w), (cb, conv_b),
                 (wq_s, wq), (wk_s, wk), (bq_s, bq), (bk_s, bk), (gw, gate_w), (gb, gate_b), (b1_s, b1),
                 (sb2_s, sb2), (rb2_s, rb2), (second["q"], swq), (second["qs"], swqs), (second["k"], swk),
                 (second["ks"], swks), (second["v"], swv), (second["kc"], swkc), (second["vc"], swvc),
                 (second["o"], swo), (cg, comp_gate), (sink_s, sink), (tw1_s, tw1), (tw2_s, tw2),
                 (tb1_s, tb1), (tb2_s, tb2)]
        CONSTS = 16 * len(loads)
        READY_D, READY_A, READY_P = 22, 4, 2

        block = ctx.enter_context(nc.Block())

        @block.sync
        def _(eng):
            def load(g, u, v):
                src = x[bass.ds(g * GI + 2 * u, 2), :, v * (HW // 2):(v + 1) * (HW // 2), :]
                eng.dma_start(xbuf[v][:], src.rearrange("i y x c -> (i y) x c")).then_inc(x_in[v], 16)

            def iteration(i, where):
                g = stages(i, where)[0][0]
                if g is None:
                    return
                for u in range(T):
                    for v in range(2):
                        if u or after(g, 1):
                            eng.wait_ge(pooled, at(pooled, g, 4 * (u - 1) + 2 * (v + 1)))
                        load(g, u, v)

            schedule(iteration)(eng)

        @block.tensor
        def _(eng):
            def turn_tiles(bank, src, eye):
                for t in range(T):
                    mm = nc.tensor.transpose(bank[:, t * P:(t + 1) * P], src(t), eye)
                return mm

            def tokens(g, b, kind, u, k):
                if kind == "pool":
                    v = k // 2
                    m = 3 * u + (0, 1, 1, 2)[k]
                    bank = pool_bank[m % 2]
                    if k % 2 == 0:
                        eng.wait_ge(x_summed, at(x_summed, g, 6 * u + 3 * v + 3))
                    if k != 2:
                        if m >= 2:
                            eng.wait_ge(pooled_read, at(pooled_read, g, m - 1))
                        elif after(g, 1):
                            if m == 0:
                                eng.wait_ge(h0_ready, at(h0_ready, g - 1, 1))
                            else:
                                eng.wait_ge(pooled_read, at(pooled_read, g, 0))
                    if k in (0, 3):
                        view = bank[:, 0:BX * PB].rearrange("p (k d n) -> p k d n", k=2, d=3)
                        views = [(0, view[:, 0]), (1, view[:, 1])]
                    else:
                        view = bank[:, 0:BX * PB].rearrange("p (d v n) -> p d v n", v=2, d=3)
                        views = [(2, view[:, :, v, :])]
                    for kx, cols in views:
                        for bx in range(BX // 2):
                            mm = nc.tensor.matmul(cols[:, :, bx * 2 * BX:(bx + 1) * 2 * BX],
                                                  blocks[v][:, bx, KIND_X[kx], :],
                                                  block_sum[:], start=True, stop=True)
                    mm.then_inc(pooled, 1)
                elif kind == "out":
                    eng.wait_ge(tapped, at(tapped, g, 32))
                    eng.wait_ge(pooled_read, at(pooled_read, g, 3 * T))
                    turn_tiles(pool_bank[0], lambda t: cols0[:, t, :], ident[:]).then_inc(h0_turned, 1)

            def attention(g, b, n):
                bank = att_bank
                if n == 1:
                    eng.wait_ge(x1_ready, at(x1_ready, g, 4))
                    if after(g, 1):
                        eng.wait_ge(share_ready, at(share_ready, g - 1, 1))
                    turn_tiles(bank, lambda t: x1[:, t, :], ident[:]).then_inc(x1_turned, 1)
                elif n == 2:
                    eng.wait_ge(x1t_ready, at(x1t_ready, g, 1))
                    nc.tensor.matmul(bank[:], wq_s[:], x1t[:], start=True, stop=True).then_inc(q1_done, 1)
                elif n == 3:
                    eng.wait_ge(q1_ready, at(q1_ready, g, 1))
                    nc.tensor.matmul(bank[:], wk_s[:], x1t[:], start=True, stop=True).then_inc(k1_done, 1)
                elif n == 4:
                    eng.wait_ge(k1_ready, at(k1_ready, g, 1))
                    for t in range(T):
                        mm = nc.tensor.matmul(bank[:, t * P:(t + 1) * P], q1[:, t * P:(t + 1) * P],
                                              k1[:, t * P:(t + 1) * P], start=True, stop=True)
                    mm.then_inc(s1_done, 1)
                elif n == 7:
                    eng.wait_ge(p1_ready, at(p1_ready, g, 4))
                    turn_tiles(bank, lambda t: s1[:, t, :], ident[:]).then_inc(p1_turned, 1)
                elif n == 8:
                    eng.wait_ge(p1t_ready, at(p1t_ready, g, 1))
                    for t in range(T):
                        mm = nc.tensor.matmul(bank[:, t * P:(t + 1) * P], p1t[:, t, :], x1[:, t, :],
                                              start=True, stop=True)
                    mm.then_inc(o1_done, 1)
                elif n == 10:
                    eng.wait_ge(x2_ready, at(x2_ready, g, 4))
                    turn_tiles(bank, lambda t: x2[:, t, :], ident[:]).then_inc(x2_turned, 1)
                elif n == 11:
                    eng.wait_ge(x2_copied, at(x2_copied, g, 2))
                    for t in range(T):
                        mm = nc.tensor.matmul(bank[:, t * NE:(t + 1) * NE], x2f[:, t * P:(t + 1) * P], gw[:],
                                              start=True, stop=True)
                    mm.then_inc(gate_done, 1)
                elif n == 13:
                    eng.wait_ge(gate_step, at(gate_step, g, 17))
                    bank_b = bank[0:3 * NE, 0:N // 2].bitcast(bf16)
                    for t in range(T):
                        mm = nc.tensor.transpose(bank_b[:, t * P:(t + 1) * P],
                                                 parts[:, t, :, :].rearrange("p a e -> p (a e)"), ident_b[:])
                    mm.then_inc(share_turned, 1)

            def up(g, b, q):
                e, n = q // FC, first[q]
                def bank_free(n):
                    if n >= 2:
                        eng.wait_ge(hid_made, at(hid_made, g, made(n - 1)))
                    elif after(g, 1):
                        eng.wait_ge(hid_made, at(hid_made, g - 1, made(items + n - 1)))
                if q == 0:
                    eng.wait_ge(x2l_ready, at(x2l_ready, g, 1))
                    eng.wait_ge(share_ready, at(share_ready, g, 1))
                if q % FC == 0 and e >= NS:
                    bank_free(n - 1)
                    nc.tensor.matmul(hid_bank[(n - 1) % 2][:], pick_b[:, e - NS, :], share_t[b][:],
                                     start=True, stop=True).then_inc(hid_done, 1)
                bank_free(n)
                cols = slice((q % FC) * P, (q % FC + 1) * P)
                bank = hid_bank[n % 2]
                nc.tensor.matmul(bank[:], w1h[:, e, cols], x2h[b][:], start=True, stop=False)
                nc.tensor.matmul(bank[:], w1l[:, e, cols], x2h[b][:], start=False, stop=False)
                nc.tensor.matmul(bank[:], w1h[:, e, cols], x2l[b][:], start=False, stop=True).then_inc(hid_done, 1)

            def down(g, q):
                e, r = q // FC, q % RING
                cols = slice((q % FC) * P, (q % FC + 1) * P)
                begin = q == 0 or (q % FC == 0 and e >= NS)
                end = q % FC == FC - 1 and e >= NS - 1
                eng.wait_ge(hid_rest, at(hid_rest, g, q + 1))
                if begin and q:
                    eng.wait_ge(down_read, at(down_read, g, e - NS + 1))
                elif begin and after(g, 1):
                    eng.wait_ge(down_read, at(down_read, g - 1, 1 + NE))
                nc.tensor.matmul(down_bank[:], w2h[:, e, cols], hid_h[:, r, :], start=begin, stop=False)
                nc.tensor.matmul(down_bank[:], w2l[:, e, cols], hid_h[:, r, :], start=False, stop=False)
                nc.tensor.matmul(down_bank[:], w2h[:, e, cols], hid_l[:, r, :], start=False, stop=end) \
                  .then_inc(hid_used, 1)

            def layer2(g, b, kind, n):
                b0, b1 = sec_bank
                if kind == "pre" and n == 0:
                    eng.wait_ge(moe_added, at(moe_added, g, NE))
                    if after(g, 1):
                        eng.wait_ge(res_ready, at(res_ready, g - 1, 1))
                    turn_tiles(b0, lambda t: moe[:, t * P:(t + 1) * P], ident[:]).then_inc(moe_turned, 1)
                elif kind == "pre" and n == 2:
                    eng.wait_ge(x3_ready, at(x3_ready, g, 4))
                    if after(g, 1):
                        eng.wait_ge(up_ready, at(up_ready, g - 1, 1))
                    turn_tiles(b1, lambda t: x3[:, t, :], ident[:]).then_inc(x3_turned, 1)
                elif kind == "pre" and n in (3, 4):
                    names = ("q", "qs") if n == 3 else ("k", "ks")
                    eng.wait_ge(x3t_ready, at(x3t_ready, g, 1))
                    for k, name in enumerate(names):
                        if n == 4:
                            eng.wait_ge(rope_read, at(rope_read, g, k + 1))
                        nc.tensor.matmul(sec_bank[k][:], second[name][:], x3t[:], start=True, stop=True) \
                          .then_inc(rope_done, 1)
                elif kind == "pre" and n == 5:
                    eng.wait_ge(xc_step, at(xc_step, g, 8))
                    eng.wait_ge(rope_read, at(rope_read, g, 3))
                    nc.tensor.matmul(b0[:, 0:GI * LC], second["kc"][:], xc[:].rearrange("p i w -> p (i w)"),
                                     start=True, stop=True).then_inc(kc_done, 1)
                elif kind == "pre" and n in (6, 7):
                    half = n - 6
                    bank = sec_bank[1 - half]
                    if half == 0:
                        eng.wait_ge(rope_read, at(rope_read, g, 4))
                    else:
                        eng.wait_ge(kc_ready, at(kc_ready, g, 1))
                    for m in range(4):
                        im = 4 * half + m
                        nc.tensor.matmul(bank[0:L, m * C:(m + 1) * C], x3t[:, im * L:(im + 1) * L], second["v"][:],
                                         start=True, stop=True)
                        mm = nc.tensor.matmul(bank[L:LK, m * C:(m + 1) * C], xc[:, im, :], second["vc"][:],
                                              start=True, stop=True)
                    mm.then_inc(v_done, 1)
                elif kind == "score":
                    t, half = n // 2, n % 2
                    bank = sec_bank[half]
                    if n == 0:
                        eng.wait_ge(rope_added, at(rope_added, g, 2))
                        eng.wait_ge(v_ready, at(v_ready, g, 2))
                    if half == 0:
                        eng.wait_ge(keys_ready, at(keys_ready, g, t + 1))
                    if n >= 2:
                        eng.wait_ge(s3_step, at(s3_step, g, 3 * (n - 2) + 1))
                    for im in range(2):
                        tok = (2 * t + im) * L
                        mm = nc.tensor.matmul(
                            bank[im * L:(im + 1) * L, 0:HH * LK], q3[:, tok:tok + L],
                            keys_h[:, t % 2, im, half * HH:(half + 1) * HH, :].rearrange("p h k -> p (h k)"),
                            start=True, stop=True)
                    mm.then_inc(scored, 1)
                elif kind == "turn":
                    if n == 0:
                        eng.wait_ge(e3_ready, at(e3_ready, g, 2))
                    if n >= 1:
                        eng.wait_ge(p3t_ready, at(p3t_ready, g, n))
                    for h in range(HH):
                        mm = nc.tensor.transpose(b0[0:LK, h * P:(h + 1) * P], e3[:, n, h, 0:LK], ident[:])
                    mm.then_inc(p3_turned, 1)
                elif kind == "value":
                    t, half = n // 2, n % 2
                    eng.wait_ge(p3t_ready, at(p3t_ready, g, n + 1))
                    if n >= 1:
                        eng.wait_ge(o3_ready, at(o3_ready, g, n))
                    for h in range(HH):
                        for im in range(2):
                            ch = (half * HH + h) * HD
                            mm = nc.tensor.matmul(b1[im * L:(im + 1) * L, h * HD:(h + 1) * HD],
                                                  p3t[:, half, h, im * L:(im + 1) * L],
                                                  values[:, 2 * t + im, ch:ch + HD], start=True, stop=True)
                    mm.then_inc(o3_done, 1)
                elif kind == "post" and n == 0:
                    eng.wait_ge(o3_ready, at(o3_ready, g, 8))
                    turn_tiles(b0, lambda t: o3[:, t, :], ident[:]).then_inc(o3_turned, 1)
                elif kind == "post" and n == 1:
                    eng.wait_ge(o3t_ready, at(o3t_ready, g, 1))
                    for t in range(T):
                        mm = nc.tensor.matmul(b1[:, t * P:(t + 1) * P], o3t[:, t * P:(t + 1) * P], second["o"][:],
                                              start=True, stop=True)
                    mm.then_inc(wo_done, 1)
                elif kind == "post" and n == 3:
                    eng.wait_ge(x4_ready, at(x4_ready, g, 4))
                    turn_tiles(b0, lambda t: x3[:, t, :], ident[:]).then_inc(x4_turned, 1)
                elif kind == "post" and n == 4:
                    eng.wait_ge(x4t_ready, at(x4t_ready, g, 1))
                    nc.tensor.matmul(b1[:], tw1_s[:], x3t[:], start=True, stop=True).then_inc(up_done, 1)
                elif kind == "post" and n == 5:
                    eng.wait_ge(up_ready, at(up_ready, g, 1))
                    for t in range(T):
                        mm = nc.tensor.matmul(b0[:, t * P:(t + 1) * P], o3t[:, t * P:(t + 1) * P], tw2_s[:],
                                              start=True, stop=True)
                    mm.then_inc(mlp_done, 1)

            def experts(g, b, kind, q):
                if kind == "up":
                    up(g, b, q)
                else:
                    down(g, q)

            eng.wait_ge(consts_in, CONSTS)
            eng.wait_ge(ready_d, READY_D)
            eng.wait_ge(ready_p, READY_P)

            def iteration(i, where):
                for g, b, stage, piece in pieces(PLAN["pe"], i, where):
                    if where == 2 and piece == ("up", 0):
                        eng.wait_ge(weight_split, 4 * NX)
                    {"tok": tokens, "att": attention, "ffn": experts, "sec": layer2}[stage](g, b, *piece)

            schedule(iteration)(eng)

        @block.scalar
        def _(eng):
            for dst, src in loads:
                eng.dma_start(dst[:] if dst is not pick else dst, src).then_inc(consts_in, 16)
            eng.wait_ge(consts_in, CONSTS)
            nc.scalar.mul(bqs_s[:], bq_s[:], float(C) ** -0.5).then_inc(ready_a, 1)
            eng.wait_ge(ready_d, READY_D - 2)
            nc.scalar.activation(cg[:], cg[:], ACT.Exp, bias=cg_max[:], accum_out=cg_sum[:]).then_inc(ready_a, 1)
            nc.scalar.activation(pick_b[:], pick, ACT.Copy).then_inc(ready_a, 1)
            nc.scalar.activation(ident_b[:], ident[:], ACT.Copy).then_inc(ready_a, 1)
            eng.wait_ge(ready_a, READY_A)

            def tokens(g, b, kind, u, k):
                if kind == "pool" and k != 1:
                    m = (0, None, 1, 2)[k]
                    eng.wait_ge(pooled, at(pooled, g, 4 * u + k + 1))
                    if after(g, 1):
                        eng.wait_ge(tapped, at(tapped, g - 1, 16 * (u // 2 + 1)))
                    side = P // 2
                    if m == 1:
                        dst = pooled_s[:, 2, :, u, :]
                    else:
                        dst = pooled_s[:, 0:2, :, u, (m // 2) * side:(m // 2 + 1) * side].rearrange("p k d n -> p (k d) n")
                    src = pool_bank[(3 * u + m) % 2][:, 0:BX * PB].rearrange("p (r n) -> p r n", r=3 if m == 1 else 6)
                    nc.scalar.activation(dst, src, ACT.Copy).then_inc(pooled_read, 1)
                elif kind == "out":
                    eng.wait_ge(h0_turned, at(h0_turned, g, 1))
                    nc.scalar.activation(h0[b][:].rearrange("p t c -> p (t c)"), pool_bank[0][:], ACT.Copy) \
                      .then_inc(h0_ready, 1)

            def attention(g, b, n):
                bank = att_bank
                if n == 1:
                    eng.wait_ge(x1_turned, at(x1_turned, g, 1))
                    nc.scalar.activation(x1t[:], bank[:], ACT.Copy).then_inc(x1t_ready, 1)
                elif n == 2:
                    eng.wait_ge(q1_done, at(q1_done, g, 1))
                    nc.scalar.activation(q1[:], bank[:], ACT.Identity, bias=bqs_s[:], scale=float(C) ** -0.5) \
                      .then_inc(q1_ready, 1)
                elif n == 3:
                    eng.wait_ge(k1_done, at(k1_done, g, 1))
                    nc.scalar.activation(k1[:], bank[:], ACT.Identity, bias=bk_s[:]).then_inc(k1_ready, 1)
                elif n == 6:
                    eng.wait_ge(s1_max, at(s1_max, g, 1))
                    for t in range(T):
                        nc.scalar.activation(s1[:, t, :], s1[:, t, :], ACT.Exp, bias=nmax1[:, t:t + 1],
                                             accum_out=den1[:, t:t + 1]).then_inc(p1_ready, 1)
                elif n == 7:
                    eng.wait_ge(p1_turned, at(p1_turned, g, 1))
                    nc.scalar.activation(q1[:], bank[:], ACT.Copy) \
                      .then_inc(p1t_ready, 1)
                elif n == 10:
                    eng.wait_ge(x2_turned, at(x2_turned, g, 1))
                    nc.scalar.activation(x2h[b][:], bank[:], ACT.Copy).then_inc(x2_copied, 1)
                    nc.scalar.activation(x2f[:], bank[:], ACT.Copy).then_inc(x2_copied, 1)
                elif n == 13:
                    eng.wait_ge(share_turned, at(share_turned, g, 1))
                    nc.scalar.activation(share_t[b][:], bank[0:3 * NE, 0:N // 2].bitcast(bf16), ACT.Copy) \
                      .then_inc(share_ready, 1)

            def experts(g, b, kind, q):
                e, n = q // FC, first[q]
                if q % FC == 0 and e >= NS:
                    k = e - NS
                    eng.wait_ge(hid_done, at(hid_done, g, n))
                    if k >= 2:
                        eng.wait_ge(down_read, at(down_read, g, k))
                    elif after(g, 1):
                        eng.wait_ge(down_read, at(down_read, g - 1, k + NE))
                    nc.scalar.activation(share_b[:, k % 2, :], hid_bank[(n - 1) % 2][:], ACT.Copy).then_inc(hid_made, 1)
                eng.wait_ge(hid_done, at(hid_done, g, n + 1))
                if q >= RING:
                    eng.wait_ge(hid_used, at(hid_used, g, q - RING + 1))
                elif after(g, 1):
                    eng.wait_ge(hid_used, at(hid_used, g - 1, CH + q - RING + 1))
                if q >= 2:
                    eng.wait_ge(hid_rest, at(hid_rest, g, q - 1))
                elif after(g, 1):
                    eng.wait_ge(hid_rest, at(hid_rest, g - 1, CH + q - 1))
                for dst, r in ((hid_h, q % RING), (hid, q % 2)):
                    nc.scalar.activation(dst[:, r, :], hid_bank[n % 2][:], ACT.Gelu, bias=b1_s[:, q:q + 1]) \
                      .then_inc(hid_made, 1)

            def layer2(g, b, kind, n):
                b0, b1 = sec_bank
                if kind == "pre" and n == 2:
                    eng.wait_ge(x3_turned, at(x3_turned, g, 1))
                    nc.scalar.activation(x3t[:], b1[:], ACT.Copy).then_inc(x3t_ready, 1)
                elif kind == "pre" and n == 5:
                    eng.wait_ge(kc_done, at(kc_done, g, 1))
                    if after(g, 1):
                        eng.wait_ge(keys_ready, at(keys_ready, g - 1, 4))
                    nc.scalar.activation(keys[:, :, L:LK], b0[:, 0:GI * LC].rearrange("p (i w) -> p i w", i=GI),
                                         ACT.Copy).then_inc(kc_ready, 1)
                elif kind == "pre" and n in (6, 7):
                    half = n - 6
                    eng.wait_ge(v_done, at(v_done, g, half + 1))
                    nc.scalar.activation(values[:, 4 * half:4 * half + 4, :].rearrange("p i c -> p (i c)"),
                                         sec_bank[1 - half][0:LK, :], ACT.Copy).then_inc(v_ready, 1)
                elif kind == "exp":
                    for half in range(2):
                        eng.wait_ge(s3_step, at(s3_step, g, 12 * (half + 1)))
                        view = e3[:, T * half:T * half + T].rearrange("p n h k -> p (n h k)")
                        nc.scalar.activation(view, view, ACT.Exp).then_inc(e3_ready, 1)
                elif kind == "turn":
                    eng.wait_ge(p3_turned, at(p3_turned, g, n + 1))
                    if n >= 2:
                        eng.wait_ge(o3_done, at(o3_done, g, n - 1))
                    nc.scalar.activation(p3t[:, n % 2].rearrange("p h q -> p (h q)"), b0[0:LK, :], ACT.Copy) \
                      .then_inc(p3t_ready, 1)
                elif kind == "post" and n == 0:
                    eng.wait_ge(o3_turned, at(o3_turned, g, 1))
                    nc.scalar.activation(o3t[:], b0[:], ACT.Copy).then_inc(o3t_ready, 1)
                elif kind == "post" and n == 3:
                    eng.wait_ge(x4_turned, at(x4_turned, g, 1))
                    nc.scalar.activation(x3t[:], b0[:], ACT.Copy).then_inc(x4t_ready, 1)
                elif kind == "post" and n == 4:
                    eng.wait_ge(up_done, at(up_done, g, 1))
                    nc.scalar.activation(o3t[:], b1[:], ACT.Gelu, bias=tb1_s[:]).then_inc(up_ready, 1)
                elif kind == "post" and n == 5:
                    eng.wait_ge(res_ready, at(res_ready, g, 1))
                    eng.dma_start(out[bass.ds(g * GI, GI)].rearrange("(t i) l c -> (i l) t c", t=T), res[:]) \
                       .then_inc(res_stored, 16)

            def iteration(i, where):
                for g, b, stage, piece in pieces(PLAN["act"], i, where):
                    {"tok": tokens, "att": attention, "ffn": experts, "sec": layer2}[stage](g, b, *piece)

            schedule(iteration)(eng)
            eng.wait_ge(res_stored, at(res_stored, NG, 0))

        @block.vector
        def _(eng):
            step = [0]

            def done(ins):
                ins.then_inc(ready_d, 1)
                step[0] += 1

            done(nc.vector.memset(power[:], -0.5))
            done(nc.vector.memset(euler[:], 2.718281828459045))
            eng.wait_ge(consts_in, CONSTS)
            done(nc.vector.tensor_scalar(cwt[:], cwt[:], 1.0 / (BX * BX), None, ALU.mult))
            eng.wait_ge(ready_d, step[0])
            for dy in range(3):
                w = [cwt[:, 3 * dy + k:3 * dy + k + 1] for k in range(3)]
                t5 = [tapw[:, 5 * dy + k:5 * dy + k + 1] for k in range(5)]
                done(nc.vector.tensor_tensor(t5[1], w[0], w[1], ALU.add))
                done(nc.vector.tensor_tensor(t5[3], w[1], w[2], ALU.add))
                done(nc.vector.tensor_copy(t5[2], w[2]))
                done(nc.vector.tensor_copy(t5[4], w[0]))
                eng.wait_ge(ready_d, step[0])
                done(nc.vector.tensor_tensor(t5[0], t5[1], w[2], ALU.add))
            done(nc.vector.tensor_tensor(sb2_sum[:], sb2_s[:, 0:1], sb2_s[:, 1:2], ALU.add))
            done(nc.vector.tensor_reduce(cg_max[:], cg[:], AX.X, ALU.max, negate=True))
            assert step[0] == READY_D - 2
            eng.wait_ge(ready_a, 2)
            done(nc.vector.reciprocal(cg_inv[:], cg_sum[:]))
            eng.wait_ge(ready_d, step[0])
            done(nc.vector.tensor_scalar(cg[:], cg[:], cg_inv[:], None, ALU.mult))
            for half in range(2):
                nc.vector.tensor_copy(s3[:, half, :, LK:LK + 1],
                                      sink_s[:, half * HH:(half + 1) * HH].unsqueeze(2)).then_inc(ready_d, 1)
            eng.wait_ge(ready_d, step[0] + 2)

            def moments(g, src, ready, need, mo, mv, ve, mom):
                eng.wait_ge(ready, at(ready, g, need))
                for t in range(T):
                    nc.vector.bn_stats(mo[:, t, :], src[:, t, :]).then_inc(mom, 1)
                eng.wait_ge(mom, at(mom, g, T))
                nc.vector.memset(ve[:], EPS).then_inc(mom, 1)
                for t in range(T):
                    nc.vector.bn_aggr(mv[:, t, :], mo[:, t, :]).then_inc(mom, 1)
                eng.wait_ge(mom, at(mom, g, 2 * T + 1))
                nc.vector.tensor_tensor(ve[:], ve[:], mv[:, :, 1], ALU.add).then_inc(mom, 1)

            def normalise(g, dst, src, mv, rs, rstd, ready):
                eng.wait_ge(rstd, at(rstd, g, 1))
                for t in range(T):
                    nc.vector.tensor_scalar(dst[:, t, :], src[:, t, :], mv[:, t, 0:1], rs[:, t:t + 1],
                                            ALU.subtract, ALU.mult).then_inc(ready, 1)

            def tokens(g, b, kind, u, k):
                if kind == "add":
                    half, k = k // 3, k % 3
                    v = blocks[half]
                    if k == 0:
                        eng.wait_ge(x_in[half], at(x_in[half], g, 16 * (u + 1)))
                        nc.vector.tensor_tensor(v[:, :, 1:6:2, :], v[:, :, 1:6:2, :], v[:, :, 2:7:2, :], ALU.add) \
                          .then_inc(x_summed, 1)
                    else:
                        eng.wait_ge(x_summed, at(x_summed, g, 6 * u + 3 * half + k))
                        nc.vector.tensor_tensor(v[:, :, 1, :], v[:, :, 1, :], v[:, :, 2 * k + 1, :], ALU.add) \
                          .then_inc(x_summed, 1)
                elif kind == "tap":
                    pair, n = u, k
                    dy, term = n // 5, (0, 2, 4, 3, 1)[n % 5]
                    src_kind = (0, 1, 1, 2, 2)[term]
                    shift = (0, 0, 1, 0, -1)[term]
                    lo, hi = max(0, -shift), BX - max(0, shift)
                    m, tiles = 2 * BX, slice(2 * pair, 2 * pair + 2)
                    src = pooled_s[:, src_kind, dy, tiles, (lo + shift) * m:(hi + shift) * m]
                    dst = taps[:, tiles, lo * m:hi * m]
                    w = tapw[:, 5 * dy + term:5 * dy + term + 1]
                    if n == 0:
                        eng.wait_ge(pooled_read, at(pooled_read, g, 6 * (pair + 1)))
                        nc.vector.tensor_scalar(dst, src, w, cb[:], ALU.mult, ALU.add).then_inc(tapped, 1)
                    elif n < 14:
                        eng.wait_ge(tapped, at(tapped, g, 16 * pair + n))
                        nc.vector.scalar_tensor_tensor(dst, src, w, dst, ALU.mult, ALU.add).then_inc(tapped, 1)
                    else:
                        eng.wait_ge(tapped, at(tapped, g, 16 * pair + n))
                        if after(g, 1):
                            eng.wait_ge(h0_turned, at(h0_turned, g - 1, 1))
                        for t in (2 * pair, 2 * pair + 1):
                            nc.vector.scalar_tensor_tensor(
                                cols0[:, t, :].rearrange("p (m b) -> p b m", b=BX),
                                pooled_s[:, src_kind, dy, t, :].rearrange("p (b m) -> p b m", b=BX), w,
                                taps[:, t, :].rearrange("p (b m) -> p b m", b=BX), ALU.mult, ALU.add) \
                              .then_inc(tapped, 1)

            def attention(g, b, n):
                bank = att_bank
                tiles = bank[:].rearrange("p (t k) -> p t k", t=T)
                if n == 0:
                    moments(g, h0[b], h0_ready, 1, mo1, mv1, ve1, mom1)
                elif n == 1:
                    normalise(g, x1, h0[b], mv1, rs1, rstd1, x1_ready)
                elif n == 4:
                    eng.wait_ge(s1_done, at(s1_done, g, 1))
                    nc.vector.tensor_tensor(s1[:], tiles, mask1[:].unsqueeze(1).to_broadcast([P, T, P]), ALU.add) \
                      .then_inc(s1_masked, 1)
                elif n == 5:
                    eng.wait_ge(s1_masked, at(s1_masked, g, 1))
                    nc.vector.tensor_reduce(nmax1[:], s1[:], AX.X, ALU.max, negate=True).then_inc(s1_max, 1)
                elif n == 7:
                    eng.wait_ge(p1_ready, at(p1_ready, g, 4))
                    nc.vector.reciprocal(inv1[:], den1[:]).then_inc(inv1_ready, 1)
                elif n == 8:
                    eng.wait_ge(o1_done, at(o1_done, g, 1))
                    eng.wait_ge(inv1_ready, at(inv1_ready, g, 1))
                    for t in range(T):
                        nc.vector.scalar_tensor_tensor(h1[b][:, t, :], tiles[:, t, :], inv1[:, t:t + 1],
                                                       h0[b][:, t, :], ALU.mult, ALU.add).then_inc(h1_ready, 1)
                elif n == 9:
                    moments(g, h1[b], h1_ready, 4, mo2, mv2, ve2, mom2)
                elif n == 10:
                    normalise(g, x2, h1[b], mv2, rs2, rstd2, x2_ready)
                elif n == "low":
                    eng.wait_ge(x2_copied, at(x2_copied, g, 2))
                    nc.vector.tensor_tensor(x2l[b][:], x2f[:], x2h[b][:], ALU.subtract).then_inc(x2l_ready, 1)
                elif n == 11:
                    eng.wait_ge(gate_done, at(gate_done, g, 1))
                    nc.vector.tensor_tensor(lg[:], bank[:, 0:T * NE].rearrange("p (t e) -> p t e", t=T),
                                            gb[:].unsqueeze(1).to_broadcast([P, T, NE]), ALU.add).then_inc(gate_step, 1)
                    eng.wait_ge(gate_step, at(gate_step, g, 1))
                    nc.vector.tensor_reduce(lmax[:], lg[:], AX.X, ALU.max).then_inc(gate_step, 1)
                    eng.wait_ge(gate_step, at(gate_step, g, 2))
                    nc.vector.tensor_tensor(lg[:], lg[:], lmax[:].unsqueeze(2).to_broadcast([P, T, NE]),
                                            ALU.subtract).then_inc(gate_step, 1)
                elif n == 12:
                    four = [P, T, NE, NE]
                    eng.wait_ge(gate_exp, at(gate_exp, g, 1))
                    nc.vector.tensor_reduce(esum[:], ez[:], AX.X, ALU.add).then_inc(gate_step, 1)
                    eng.wait_ge(gate_step, at(gate_step, g, 4))
                    nc.vector.reciprocal(einv[:], esum[:]).then_inc(gate_step, 1)
                    eng.wait_ge(gate_step, at(gate_step, g, 5))
                    nc.vector.tensor_tensor(prob[:], ez[:], einv[:].unsqueeze(2).to_broadcast([P, T, NE]),
                                            ALU.mult).then_inc(gate_step, 1)
                    eng.wait_ge(gate_step, at(gate_step, g, 6))
                    pe_, pj = prob[:].unsqueeze(3).to_broadcast(four), prob[:].unsqueeze(2).to_broadcast(four)
                    nc.vector.tensor_tensor(above, pj, pe_, ALU.is_gt).then_inc(gate_step, 1)
                    nc.vector.tensor_tensor(equal, pj, pe_, ALU.is_equal).then_inc(gate_step, 1)
                    eng.wait_ge(gate_step, at(gate_step, g, 8))
                    nc.vector.tensor_tensor(equal, equal, tie[:].unsqueeze(1).to_broadcast(four),
                                            ALU.mult).then_inc(gate_step, 1)
                    eng.wait_ge(gate_step, at(gate_step, g, 9))
                    nc.vector.tensor_tensor(above, above, equal, ALU.add).then_inc(gate_step, 1)
                    eng.wait_ge(gate_step, at(gate_step, g, 10))
                    nc.vector.tensor_reduce(rank[:], above, AX.X, ALU.add).then_inc(gate_step, 1)
                    eng.wait_ge(gate_step, at(gate_step, g, 11))
                    nc.vector.scalar_tensor_tensor(share[:], rank[:], 1.5, prob[:], ALU.is_lt, ALU.mult) \
                      .then_inc(gate_step, 1)
                    eng.wait_ge(gate_step, at(gate_step, g, 12))
                    nc.vector.tensor_copy(parts[:, :, 0, :], share[:]).then_inc(gate_step, 1)
                    eng.wait_ge(gate_step, at(gate_step, g, 13))
                    nc.vector.tensor_tensor(rest1[:], share[:], parts[:, :, 0, :], ALU.subtract).then_inc(gate_step, 1)
                    eng.wait_ge(gate_step, at(gate_step, g, 14))
                    nc.vector.tensor_copy(parts[:, :, 1, :], rest1[:]).then_inc(gate_step, 1)
                    eng.wait_ge(gate_step, at(gate_step, g, 15))
                    nc.vector.tensor_tensor(rest2[:], rest1[:], parts[:, :, 1, :], ALU.subtract).then_inc(gate_step, 1)
                    eng.wait_ge(gate_step, at(gate_step, g, 16))
                    nc.vector.tensor_copy(parts[:, :, 2, :], rest2[:]).then_inc(gate_step, 1)

            def hidden(g, q):
                eng.wait_ge(hid_made, at(hid_made, g, made(first[q] + 1)))
                nc.vector.tensor_tensor(hid_l[:, q % RING, :], hid[:, q % 2, :], hid_h[:, q % RING, :],
                                        ALU.subtract).then_inc(hid_rest, 1)

            def expert_sum(g, q):
                e = q // FC
                eng.wait_ge(hid_used, at(hid_used, g, q + 1))
                if e == NS - 1:
                    if after(g, 1):
                        eng.wait_ge(moe_turned, at(moe_turned, g - 1, 1))
                    nc.vector.tensor_scalar(moe[:], down_bank[:], sb2_sum[:], None, ALU.add).then_inc(down_read, 1)
                else:
                    r = e - NS
                    if r >= 2:
                        eng.wait_ge(moe_added, at(moe_added, g, r - 1))
                    elif after(g, 1):
                        eng.wait_ge(moe_added, at(moe_added, g - 1, NE + r - 1))
                    nc.vector.scalar_tensor_tensor(part[:, r % 2, :], down_bank[:], rb2_s[:, r:r + 1],
                                                   share_b[:, r % 2, :], ALU.add, ALU.mult).then_inc(down_read, 1)

            def experts(g, b, kind, q):
                if kind == "hidden":
                    hidden(g, q)
                else:
                    expert_sum(g, q)

            def layer2(g, b, kind, n):
                b0, b1 = sec_bank
                if kind == "pre" and n == 0:
                    eng.wait_ge(moe_turned, at(moe_turned, g, 1))
                    nc.vector.tensor_tensor(h2[:].rearrange("p t c -> p (t c)"), b0[:],
                                            h1[b][:].rearrange("p t c -> p (t c)"), ALU.add).then_inc(h2_ready, 1)
                elif kind == "pre" and n == 1:
                    moments(g, h2, h2_ready, 1, mo3, mv3, ve3, mom3)
                elif kind == "pre" and n == 2:
                    normalise(g, x3, h2, mv3, rs3, rstd3, x3_ready)
                elif kind == "pre" and n in (3, 4):
                    for k, table in enumerate((cos, sin)):
                        m = 2 * (n - 3) + k
                        eng.wait_ge(rope_done, at(rope_done, g, m + 1))
                        if n == 4 and k == 0:
                            eng.wait_ge(rope_added, at(rope_added, g, 1))
                        elif n == 3 and k == 0 and after(g, 1):
                            eng.wait_ge(rope_added, at(rope_added, g - 1, 2))
                        nc.vector.tensor_tensor(roped[:, k, :].rearrange("p (i l) -> p i l", i=GI),
                                                sec_bank[k][:].rearrange("p (i l) -> p i l", i=GI),
                                                table[:].unsqueeze(1).to_broadcast([P, GI, L]), ALU.mult) \
                          .then_inc(rope_read, 1)
                elif kind == "pre" and n == 5:
                    eng.wait_ge(x3t_ready, at(x3t_ready, g, 1))
                    tok = x3t[:].rearrange("p (i l) -> p i l", i=GI)
                    for r in range(RATIO):
                        src = tok[:, :, r:r + STRIDE * (LC - 1) + 1:STRIDE]
                        if r == 0:
                            nc.vector.tensor_scalar(xc[:], src, cg[:, 0:1], None, ALU.mult).then_inc(xc_step, 1)
                        else:
                            eng.wait_ge(xc_step, at(xc_step, g, r))
                            nc.vector.scalar_tensor_tensor(xc[:], src, cg[:, r:r + 1], xc[:], ALU.mult, ALU.add) \
                              .then_inc(xc_step, 1)
                elif kind == "score":
                    half = n % 2
                    three = [P, HH, LK]
                    eng.wait_ge(scored, at(scored, g, n + 1))
                    nc.vector.scalar_tensor_tensor(
                        s3[:, half, :, 0:LK], sec_bank[half][:, 0:HH * LK].rearrange("p (h k) -> p h k", h=HH),
                        float(HD) ** -0.5, mask2[:].unsqueeze(1).to_broadcast(three), ALU.mult, ALU.add) \
                      .then_inc(s3_step, 1)
                    eng.wait_ge(s3_step, at(s3_step, g, 3 * n + 1))
                    nc.vector.tensor_reduce(m3[:, half, :], s3[:, half], AX.X, ALU.max).then_inc(s3_step, 1)
                    eng.wait_ge(s3_step, at(s3_step, g, 3 * n + 2))
                    nc.vector.tensor_tensor(e3[:, n], s3[:, half],
                                            m3[:, half, :].unsqueeze(2).to_broadcast([P, HH, LK + 1]),
                                            ALU.subtract).then_inc(s3_step, 1)
                elif kind == "turn" and n < 2:
                    if n == 0:
                        for half in range(2):
                            eng.wait_ge(e3_ready, at(e3_ready, g, half + 1))
                            nc.vector.tensor_reduce(den3[:, T * half:T * half + T], e3[:, T * half:T * half + T],
                                                    AX.X, ALU.add).then_inc(inv3_step, 1)
                        eng.wait_ge(inv3_step, at(inv3_step, g, 2))
                        nc.vector.reciprocal(inv3[:], den3[:]).then_inc(inv3_step, 1)
                elif kind == "value":
                    t, half = n // 2, n % 2
                    eng.wait_ge(o3_done, at(o3_done, g, n + 1))
                    if n == 0:
                        eng.wait_ge(inv3_step, at(inv3_step, g, 3))
                    cols = slice(half * HH * HD, (half + 1) * HH * HD)
                    nc.vector.tensor_tensor(o3[:, t, cols].rearrange("p (h d) -> p h d", h=HH),
                                            b1[:, 0:HH * HD].rearrange("p (h d) -> p h d", h=HH),
                                            inv3[:, n, :].unsqueeze(2).to_broadcast([P, HH, HD]), ALU.mult) \
                      .then_inc(o3_ready, 1)
                elif kind == "post" and n == 1:
                    eng.wait_ge(wo_done, at(wo_done, g, 1))
                    if after(g, 1):
                        eng.wait_ge(res_stored, at(res_stored, g - 1, 16))
                    nc.vector.tensor_tensor(h3[:].rearrange("p t c -> p (t c)"), b1[:],
                                            h2[:].rearrange("p t c -> p (t c)"), ALU.add).then_inc(h3_ready, 1)
                elif kind == "post" and n == 2:
                    moments(g, h3, h3_ready, 1, mo4, mv4, ve4, mom4)
                elif kind == "post" and n == 3:
                    normalise(g, x3, h3, mv4, rs4, rstd4, x4_ready)
                elif kind == "post" and n == 5:
                    eng.wait_ge(mlp_done, at(mlp_done, g, 1))
                    eng.wait_ge(h3b_ready, at(h3b_ready, g, 1))
                    nc.vector.tensor_tensor(res[:].rearrange("p t c -> p (t c)"), b0[:],
                                            h3b[:].rearrange("p t c -> p (t c)"), ALU.add).then_inc(res_ready, 1)

            def iteration(i, where):
                for g, b, stage, piece in pieces(PLAN["dve"], i, where):
                    {"tok": tokens, "att": attention, "ffn": experts, "sec": layer2}[stage](g, b, *piece)

            schedule(iteration)(eng)

        @block.gpsimd
        def _(eng):
            eng.wait_ge(consts_in, CONSTS)
            for w in (tw1_s, tw2_s):
                nc.gpsimd.affine_select(out=w[:], in_=w[:], compare_op=ALU.is_ge, fill=0.0, base=0,
                                        pattern=[[1, P]], channel_multiplier=-1).then_inc(ready_p, 1)
            lots = [(w1, w1h, w1l, e) for e in range(NX)] + [(w2, w2h, w2l, e) for e in range(NX)]

            def load(n):
                src, _, _, e = lots[n]
                eng.dma_start(hid[:, n % 2, :], src[:, e, :]).then_inc(weight_in[n % 2], 16)

            load(0)
            load(1)
            for n, (_, high, low, e) in enumerate(lots):
                eng.wait_ge(weight_in[n % 2], 16 * (n // 2 + 1))
                nc.gpsimd.tensor_copy(high[:, e, :], hid[:, n % 2, :]).then_inc(weight_split, 1)
                eng.wait_ge(weight_split, 2 * n + 1)
                nc.gpsimd.tensor_tensor(low[:, e, :], hid[:, n % 2, :], high[:, e, :], ALU.subtract) \
                  .then_inc(weight_split, 1)
                if n + 2 < len(lots):
                    eng.wait_ge(weight_split, 2 * n + 2)
                    load(n + 2)

            def inverse_root(g, rs, ve, mom, rstd):
                eng.wait_ge(mom, at(mom, g, 10))
                nc.gpsimd.tensor_tensor(rs[:], ve[:], power[:], ALU.pow).then_inc(rstd, 1)

            def attention(g, b, n):
                if n == 0:
                    inverse_root(g, rs1, ve1, mom1, rstd1)
                elif n == 9:
                    inverse_root(g, rs2, ve2, mom2, rstd2)
                elif n == 11:
                    eng.wait_ge(gate_step, at(gate_step, g, 3))
                    nc.gpsimd.tensor_tensor(ez[:].rearrange("p t e -> p (t e)"), euler[:],
                                            lg[:].rearrange("p t e -> p (t e)"), ALU.pow).then_inc(gate_exp, 1)

            def experts(g, b, kind, q):
                r = q // FC - NS
                if r >= 0:
                    eng.wait_ge(down_read, at(down_read, g, 2 + r))
                    if r >= 1:
                        eng.wait_ge(moe_added, at(moe_added, g, r))
                    nc.gpsimd.tensor_tensor(moe[:], moe[:], part[:, r % 2, :], ALU.add).then_inc(moe_added, 1)

            def layer2(g, b, kind, n):
                if kind == "pre" and n == 1:
                    inverse_root(g, rs3, ve3, mom3, rstd3)
                elif kind == "pre" and n == 3:
                    eng.wait_ge(rope_read, at(rope_read, g, 2))
                    if after(g, 1):
                        eng.wait_ge(scored, at(scored, g - 1, 8))
                    nc.gpsimd.tensor_tensor(q3[:], roped[:, 0, :], roped[:, 1, :], ALU.add).then_inc(rope_added, 1)
                elif kind == "pre" and n == 4:
                    eng.wait_ge(rope_read, at(rope_read, g, 4))
                    if after(g, 1):
                        eng.wait_ge(keys_ready, at(keys_ready, g - 1, 4))
                    nc.gpsimd.tensor_tensor(keys[:, :, 0:L], roped[:, 0, :].rearrange("p (i l) -> p i l", i=GI),
                                            roped[:, 1, :].rearrange("p (i l) -> p i l", i=GI), ALU.add) \
                      .then_inc(rope_added, 1)
                elif (kind == "pre" and n in (6, 7)) or (kind == "score" and n in (2, 4)):
                    t = n - 6 if kind == "pre" else n // 2 + 1
                    if t == 0:
                        eng.wait_ge(rope_added, at(rope_added, g, 2))
                        eng.wait_ge(kc_ready, at(kc_ready, g, 1))
                    if t >= 2:
                        eng.wait_ge(scored, at(scored, g, 2 * (t - 1)))
                    for im in range(2):
                        four = [P, HEADS, LK]
                        ins = nc.gpsimd.tensor_tensor(keys_h[:, t % 2, im],
                                                      keys[:, 2 * t + im, :].unsqueeze(1).to_broadcast(four),
                                                      heads[:].unsqueeze(2).to_broadcast(four), ALU.mult)
                    ins.then_inc(keys_ready, 1)
                elif kind == "post" and n == 1:
                    eng.wait_ge(h3_ready, at(h3_ready, g, 1))
                    if after(g, 1):
                        eng.wait_ge(res_ready, at(res_ready, g - 1, 1))
                    nc.gpsimd.tensor_tensor(h3b[:], h3[:], tb2_s[:].unsqueeze(1).to_broadcast([P, T, C]), ALU.add) \
                      .then_inc(h3b_ready, 1)
                elif kind == "post" and n == 2:
                    inverse_root(g, rs4, ve4, mom4, rstd4)

            def iteration(i, where):
                for g, b, stage, piece in pieces(PLAN["pool"], i, where):
                    {"att": attention, "ffn": experts, "sec": layer2}[stage](g, b, *piece)

            schedule(iteration)(eng)


def kernel(**inputs):
    import numpy as _np
    import concourse.bacc as _bacc
    from concourse import mybir as _mybir
    from concourse.bass_utils import run_bass_kernel_spmd as _run

    a = {k: _np.asarray(v) for k, v in inputs.items()}
    f32 = _np.float32

    def rows(v):
        v = v.reshape(1, -1)
        return _np.broadcast_to(v, (P, v.shape[1]))

    def halves(w):
        return w.reshape(HEADS, 2, HD // 2, C)[:, ::-1].reshape(C, C)

    pix, tok = _np.arange(HW), _np.arange(L)
    block = _np.zeros((2, HW, 3, 2, BX), f32)
    for dy in range(3):
        for by in range(BX):
            on = (pix >= by * 8 + dy - 1) & (pix <= by * 8 + 7 + dy - 1)
            for im in range(2):
                block[im, on, dy, im, by] = 1
    half = HD // 2
    freq = (f32(1.0) / _np.power(f32(10000.0), _np.arange(half, dtype=f32) / f32(half))).astype(f32)
    angle = tok.astype(f32)[None, :] * freq[:, None]
    cos = _np.tile(_np.cos(angle), (2 * HEADS, 1)).astype(f32)
    sin = _np.tile(_np.concatenate([-_np.sin(angle), _np.sin(angle)]), (HEADS, 1)).astype(f32)
    image = _np.arange(P) // L
    mask1 = _np.where(image[:, None] == image[None, :], f32(0), f32(-1e30))
    pos = _np.arange(P) % L
    window = (pos[:, None] >= tok[None, :]) & (pos[:, None] - tok[None, :] < 128)
    comp = pos[:, None] >= (_np.arange(LC) * STRIDE + RATIO - 1)[None, :]
    mask2 = _np.where(_np.concatenate([window, comp], 1), f32(0), f32(-1e30))
    heads = (_np.arange(C)[:, None] // HD == _np.arange(HEADS)[None, :]).astype(f32)
    pick = _np.tile(_np.eye(NE, dtype=f32)[:, :, None], (3, 1, P))
    tie = _np.broadcast_to(_np.tril(_np.ones((NE, NE), f32), -1), (P, NE, NE))

    w1 = _np.concatenate([a["L0_ffn_sw1"], a["L0_ffn_rw1"]])
    w2 = _np.concatenate([a["L0_ffn_sw2"], a["L0_ffn_rw2"]])
    b1 = _np.concatenate([a["L0_ffn_sb1"], a["L0_ffn_rb1"]])
    named = dict(
        x=a["x"], conv_w=a["L0_tok_conv_w"].reshape(9, C).T, conv_b=a["L0_tok_conv_b"].reshape(C, 1),
        wq=a["L0_attn_Wq"], bq=a["L0_attn_bq"].reshape(C, 1), wk=a["L0_attn_Wk"], bk=a["L0_attn_bk"].reshape(C, 1),
        gate_w=a["L0_ffn_gate_w"].T, gate_b=rows(a["L0_ffn_gate_b"]),
        w1=w1.transpose(2, 0, 1), b1=b1.reshape(CH, P).T,
        w2=w2.reshape(NX, C, FC, P).transpose(3, 0, 2, 1).reshape(P, NX, F),
        sb2=a["L0_ffn_sb2"].T, rb2=a["L0_ffn_rb2"].T,
        swq=a["L1_attn_wq"].T, swqs=halves(a["L1_attn_wq"]).T, swk=a["L1_attn_wk"].T, swks=halves(a["L1_attn_wk"]).T,
        swv=a["L1_attn_wv"].T, swkc=a["L1_attn_wk_c"].T, swvc=a["L1_attn_wv_c"].T, swo=a["L1_attn_wo"].T,
        comp_gate=rows(a["L1_attn_gate_logits"]), sink=rows(a["L1_attn_sink_logit"]),
        tw1=a["L1_ffn_W1"].T, tb1=a["L1_ffn_b1"].reshape(P, 1), tw2=a["L1_ffn_W2"].T, tb2=rows(a["L1_ffn_b2"]),
        ident_c=_np.eye(P, dtype=f32), block_c=block.reshape(P, PB), cos_c=cos, sin_c=sin, mask1_c=mask1,
        mask2_c=mask2, heads_c=heads, pick_c=pick, tie_c=tie)

    nc = _bacc.Bacc("TRN2", target_bir_lowering=False, num_devices=1)
    arrays, args = {}, {}
    for name, value in named.items():
        value = _np.ascontiguousarray(value)
        arrays[f"in_{name}"] = value
        args[name] = nc.dram_tensor(f"in_{name}", value.shape, _mybir.dt.from_np(value.dtype), kind="ExternalInput").ap()
    args["out"] = nc.dram_tensor("out_0", (NI, L, C), _mybir.dt.float32, kind="ExternalOutput").ap()
    program(nc, **args)
    r = _run(nc, [arrays], core_ids=[0])
    return r.results[0]["out_0"]
```

```python
import concourse.bass as bass
from concourse import mybir
from contextlib import ExitStack

fp32 = mybir.dt.float32
bf16 = mybir.dt.bfloat16
ALU = mybir.AluOpType
ACT = mybir.ActivationFunctionType
AX = mybir.AxisListType

NI, HW, C = 128, 64, 128
P = 128
BX = 8
L = BX * BX
GI = 8
NG = NI // GI
T = GI * L // P
N = T * P
NS, NE, F = 2, 8, 512
NX = NS + NE
FC = F // P
CH = NX * FC
HEADS, HD = 8, C // 8
RATIO, STRIDE = 8, 4
LC = (L - RATIO) // STRIDE + 1
LK = L + LC
HH = HEADS // 2
PB = 3 * 2 * BX
EPS = 1e-5
STAGING = 4
POOL_EVERY = 5
RING = 4
KIND_X = (1, 0, 7)

STAGES = ("tok", "att", "ffn", "sec")
STAGE_OF = dict(pair="tok", add="tok", pool="tok", tap="tok", out="tok", att="att", low="att", up="ffn", hidden="ffn",
                down="ffn", sum="ffn", pre="sec", score="sec", exp="sec", turn="sec", value="sec", post="sec",
                weights="set")

ORDER = dict(
    pe="""
        up.0 up.1 down.38' down.39' up.2 up.3 down.0 up.4 att.1 pool.0.0 pre.0 down.1 pool.0.1 up.5 att.2 down.2
        up.6 up.7 down.3 down.4 down.5 pre.2 pool.0.2 up.8 down.6 pre.3 up.9 pool.0.3 up.10 att.3 down.7 up.11
        att.4 pre.4 up.12 down.8 down.9 pre.5 up.13 pool.1.0 pre.6 pre.7 down.10 down.11 score.0 up.14 score.1
        up.15 pool.1.1 down.12 score.2 score.3 up.16 down.13 up.17 down.14 down.15 score.4 pool.1.2 up.18 up.19
        pool.1.3 down.16 score.5 score.6 up.20 down.17 up.21 down.18 score.7 down.19 up.22 up.23 pool.2.0 turn.0
        pool.2.1 turn.1 down.20 down.21 att.7 value.0 turn.2 att.8 turn.3 value.1 up.24 value.2 turn.4 up.25
        value.3 pool.2.2 down.22 pool.2.3 turn.5 value.4 down.23 turn.6 up.26 up.27 value.5 turn.7 down.24
        value.6 att.10 up.28 value.7 att.11 post.0 up.29 down.25 post.1 up.30 down.26 up.31 down.27 pool.3.0
        pool.3.1 down.28 up.32 down.29 pool.3.2 up.33 pool.3.3 up.34 down.30 post.3 down.31 att.13 up.35 post.4
        down.32 up.36 down.33 post.5 up.37 up.38 down.34 down.35 up.39 out down.36 down.37""",
    act="""
        hidden.39' weights.0 hidden.0 hidden.1 weights.1 hidden.2 hidden.3 att.1 hidden.4 hidden.5 weights.2
        hidden.6 weights.3 pool.0.0 hidden.7 att.2 pre.2 pool.0.2 hidden.8 hidden.9 weights.4 att.3 hidden.10
        weights.5 hidden.11 hidden.12 weights.6 pool.0.3 pre.5 hidden.13 pre.6 weights.7 pre.7 hidden.14
        hidden.15 hidden.16 weights.8 hidden.17 pool.1.0 hidden.18 weights.9 hidden.19 weights.10 pool.1.2
        pool.1.3 hidden.20 hidden.21 weights.11 weights.12 exp att.6 turn.0 hidden.22 weights.13 turn.1 att.7
        turn.2 hidden.23 turn.3 hidden.24 turn.4 pool.2.0 weights.14 hidden.25 turn.5 weights.15 turn.6
        hidden.26 hidden.27 turn.7 weights.16 weights.17 att.10 hidden.28 pool.2.2 post.0 weights.18 pool.2.3
        hidden.29 weights.19 hidden.30 hidden.31 hidden.32 pool.3.0 pool.3.2 hidden.33 pool.3.3 post.3 hidden.34
        hidden.35 post.4 hidden.36 hidden.37 hidden.38 att.13 post.5 out""",
    dve="""
        att.0 pair.0.0 weights.0 weights.1 hidden.0 sum.39' att.1 weights.2 hidden.1 pair.0.1 hidden.2 pre.0
        hidden.3 pre.1 hidden.5 pre.2 weights.3 hidden.6 weights.4 hidden.7 pair.1.0 pre.5 hidden.8 weights.5
        pre.3 sum.7 att.4 weights.6 pre.4 hidden.10 hidden.11 weights.7 hidden.12 att.5 hidden.13 pair.1.1
        weights.8 weights.9 weights.10 sum.11 score.0 score.1 hidden.15 score.2 score.3 hidden.16 sum.15
        hidden.17 score.4 pair.2.0 hidden.18 tap.0.0 weights.11 weights.12 score.5 tap.0.1 score.6 tap.0.2
        score.7 tap.0.3 hidden.20 tap.0.4 hidden.21 tap.0.5 sum.19 turn.0 tap.0.6 value.0 tap.0.7 pair.2.1
        weights.13 tap.0.8 value.1 tap.0.9 tap.0.10 hidden.22 weights.14 turn.1 value.2 hidden.23 turn.2
        tap.0.11 att.7 tap.0.12 att.8 turn.3 value.3 att.9 tap.0.13 turn.4 hidden.25 weights.15 value.4 sum.23
        turn.5 pair.3.0 value.5 att.10 tap.0.14 weights.16 hidden.26 value.6 hidden.27 low value.7 att.11
        weights.17 weights.18 pair.3.1 hidden.28 post.1 turn.6 post.2 sum.27 hidden.30 att.12 hidden.31 turn.7
        post.3 hidden.32 hidden.33 tap.1.0 tap.1.1 weights.19 tap.1.2 sum.31 tap.1.3 tap.1.4 tap.1.5 tap.1.6
        tap.1.7 tap.1.8 tap.1.9 hidden.35 tap.1.10 tap.1.11 hidden.36 tap.1.12 post.5 tap.1.13 tap.1.14 sum.35
        hidden.37 hidden.38""",
    pool="""
        weights.0 sum.35' weights.1 weights.2 hidden.39' att.0 weights.3 add.0.0 weights.4 add.0.1 sum.39' sum.7
        weights.5 hidden.4 weights.6 pre.1 add.0.2 weights.7 add.0.3 weights.8 weights.9 hidden.9 add.1.0
        weights.10 weights.11 pre.3 add.1.1 pre.4 weights.12 pre.6 pre.7 weights.13 add.1.2 score.2 hidden.14
        add.1.3 sum.11 weights.14 score.4 sum.15 hidden.19 weights.15 add.2.0 weights.16 add.2.1 weights.17
        weights.18 sum.19 add.2.2 add.2.3 hidden.24 att.9 add.3.0 sum.23 add.3.1 weights.19 att.11 hidden.29
        add.3.2 add.3.3 post.2 sum.27 hidden.34 post.1 sum.31""")


def read(text):
    for word in text.split():
        name, *numbers = word.rstrip("'").split(".")
        piece = tuple(int(n) for n in numbers)
        yield word[-1] == "'", STAGE_OF[name], piece if name == "att" else (name,) + piece


PLAN = {engine: list(read(text)) for engine, text in ORDER.items()}


def after(g, n):
    return not isinstance(g, int) or g >= n


def program(nc, x, conv_w, conv_b, wq, bq, wk, bk, gate_w, gate_b, w1, b1, w2, sb2, rb2,
            swq, swqs, swk, swks, swv, swkc, swvc, swo, comp_gate, sink, tw1, tb1, tw2, tb2,
            ident_c, block_c, cos_c, sin_c, mask1_c, mask2_c, heads_c, pick_c, tie_c, out):
    with ExitStack() as ctx:
        per = {}
        kept = []

        def sb(name, shape, dt=fp32):
            return ctx.enter_context(nc.sbuf_tensor(name, shape, dt))

        def pb(name):
            return ctx.enter_context(nc.psum_tensor(name, [P, 512], fp32))

        def sem(name, n=1):
            s = ctx.enter_context(nc.semaphore(name))
            per[id(s)] = n
            kept.append(s)
            return s

        def at(s, g, k):
            return g * per[id(s)] + k

        ident = sb("ident", [P, P])
        ident_b = sb("ident_b", [P, P], bf16)
        block_sum = sb("block_sum", [P, PB])
        cos = sb("cos", [P, L])
        sin = sb("sin", [P, L])
        mask1 = sb("mask1", [P, P])
        mask2 = sb("mask2", [P, LK])
        heads = sb("heads", [P, HEADS])
        pick_b = sb("pick_b", [3 * NE, NE, P], bf16)
        tie = sb("tie", [P, NE, NE])
        cwt = sb("cwt", [P, 9])
        cb = sb("cb", [P, 1])
        tapw = sb("tapw", [P, 15])
        wq_s, wk_s = sb("wq_s", [C, C]), sb("wk_s", [C, C])
        bq_s, bqs_s, bk_s = sb("bq_s", [C, 1]), sb("bqs_s", [C, 1]), sb("bk_s", [C, 1])
        gw = sb("gw", [C, NE])
        gb = sb("gb", [P, NE])
        w1h, w1l = sb("w1h", [P, NX, F], bf16), sb("w1l", [P, NX, F], bf16)
        w2h, w2l = sb("w2h", [P, NX, F], bf16), sb("w2l", [P, NX, F], bf16)
        b1_s = sb("b1_s", [P, CH])
        sb2_s, sb2_sum = sb("sb2_s", [C, NS]), sb("sb2_sum", [C, 1])
        rb2_s = sb("rb2_s", [C, NE])
        second = {}
        for name in ("q", "qs", "k", "ks", "v", "kc", "vc", "o"):
            second[name] = sb("second_" + name, [C, C])
        cg = sb("cg", [P, RATIO])
        cg_max, cg_sum, cg_inv = sb("cg_max", [P, 1]), sb("cg_sum", [P, 1]), sb("cg_inv", [P, 1])
        sink_s = sb("sink_s", [P, HEADS])
        tw1_s, tw2_s = sb("tw1_s", [P, P]), sb("tw2_s", [P, P])
        tb1_s, tb2_s = sb("tb1_s", [P, 1]), sb("tb2_s", [P, P])
        power = sb("power", [P, T])
        euler = sb("euler", [P, T * NE])
        xbuf = [sb(f"xbuf{i}", [P, HW // 2, C]) for i in range(2)]
        blocks = [b[:].rearrange("p (b x) c -> p b x c", x=8) for b in xbuf]
        pooled_s = sb("pooled_s", [P, 3, 3, T, P])
        taps = sb("taps", [C, T, P])
        cols0 = sb("cols0", [C, T, P])
        h0 = [sb(f"h0_{i}", [P, T, C]) for i in range(2)]
        h1 = [sb(f"h1_{i}", [P, T, C]) for i in range(2)]
        x2h = [sb(f"x2h_{i}", [C, N], bf16) for i in range(2)]
        x2l = [sb(f"x2l_{i}", [C, N], bf16) for i in range(2)]
        share_t = [sb(f"share_t{i}", [3 * NE, N], bf16) for i in range(2)]
        mo1, mv1, rs1 = sb("mo1", [P, T, 6]), sb("mv1", [P, T, 2]), sb("rs1", [P, T])
        ve1 = sb("ve1", [P, T])
        mo2, mv2, rs2 = sb("mo2", [P, T, 6]), sb("mv2", [P, T, 2]), sb("rs2", [P, T])
        ve2 = sb("ve2", [P, T])
        x1, x1t = sb("x1", [P, T, C]), sb("x1t", [C, N])
        q1, k1 = sb("q1", [C, N]), sb("k1", [C, N])
        s1 = sb("s1", [P, T, P])
        p1t = q1[:].rearrange("p (t k) -> p t k", t=T)
        nmax1, den1, inv1 = sb("nmax1", [P, T]), sb("den1", [P, T]), sb("inv1", [P, T])
        x2, x2f = k1[:].rearrange("p (t c) -> p t c", t=T), x1t
        lg, lmax, ez = sb("lg", [P, T, NE]), sb("lmax", [P, T]), sb("ez", [P, T, NE])
        esum, einv, prob = sb("esum", [P, T]), sb("einv", [P, T]), sb("prob", [P, T, NE])
        above, equal = [s1[:, 2 * k:2 * k + 2, :].rearrange("p t (a e j) -> p (t a) e j", a=2, e=NE) for k in range(2)]
        rank, share = sb("rank", [P, T, NE]), sb("share", [P, T, NE])
        rest1, rest2 = sb("rest1", [P, T, NE]), sb("rest2", [P, T, NE])
        parts = sb("parts", [P, T, 3, NE], bf16)
        hid = sb("hid", [P, 2, F])
        hid_h, hid_l = sb("hid_h", [P, RING, F], bf16), sb("hid_l", [P, RING, F], bf16)
        share_b = sb("share_b", [P, 2, N])
        pick = share_b[0:3 * NE].rearrange("p a (e q) -> p (a e) q", q=P)
        part = sb("part", [C, 2, N])
        moe = sb("moe", [C, N])
        mo3, mv3, rs3 = sb("mo3", [P, T, 6]), sb("mv3", [P, T, 2]), sb("rs3", [P, T])
        ve3 = sb("ve3", [P, T])
        mo4, mv4, rs4 = sb("mo4", [P, T, 6]), sb("mv4", [P, T, 2]), sb("rs4", [P, T])
        ve4 = sb("ve4", [P, T])
        h2 = sb("h2", [P, T, C])
        x3, x3t = sb("x3", [P, T, C]), sb("x3t", [C, N])
        q3 = sb("q3", [C, N])
        keys = sb("keys", [C, GI, LK])
        xc = sb("xc", [C, GI, LC])
        values = sb("values", [LK, GI, C])
        keys_h = sb("keys_h", [C, 2, 2, HEADS, LK])
        roped = keys_h[:, 0].rearrange("p i h k -> p (i h k)")[:, 0:2 * N].rearrange("p (a n) -> p a n", a=2)
        s3 = sb("s3", [P, 2, HH, LK + 1])
        m3 = sb("m3", [P, 2, HH])
        e3 = sb("e3", [P, 2 * T, HH, LK + 1])
        den3, inv3 = sb("den3", [P, 2 * T, HH]), sb("inv3", [P, 2 * T, HH])
        p3t = sb("p3t", [LK, 2, HH, P])
        o3, h3 = x3, sb("h3", [P, T, C])
        o3t = sb("o3t", [C, N])
        h3b, res = h2, h3

        pool_bank = [pb("pool_bank0"), pb("pool_bank1")]
        hid_bank = [pb("hid_bank0"), pb("hid_bank1")]
        down_bank = pb("down_bank")
        att_bank = pb("att_bank")
        sec_bank = [pb("sec_bank0"), pb("sec_bank1")]

        sink_placed = sem("sink_placed")
        early_in, consts_in = sem("early_in"), sem("consts_in")
        weight_in = [sem(f"weight_in{i}") for i in range(STAGING)]
        weight_high, weight_low = sem("weight_high"), sem("weight_low")
        ready_d, ready_a, ready_p = sem("setup_vector"), sem("setup_scalar"), sem("setup_pool")
        x_in = [sem(f"x_in{i}", 16 * T) for i in range(2)]
        x_paired, x_summed = sem("x_paired", 2 * T), sem("x_summed", 4 * T)
        pooled = sem("pooled", 4 * T)
        pooled_read = sem("pooled_read", 3 * T)
        tapped = sem("tapped", 32)
        h0_turned, h0_ready = sem("h0_turned"), sem("h0_ready")
        mom1, rstd1, x1_ready = sem("mom1", 10), sem("rstd1"), sem("x1_ready", 4)
        x1_turned, x1t_ready = sem("x1_turned"), sem("x1t_ready")
        q1_done, q1_ready, k1_done, k1_ready = sem("q1_done"), sem("q1_ready"), sem("k1_done"), sem("k1_ready")
        s1_done, s1_masked, s1_max = sem("s1_done"), sem("s1_masked"), sem("s1_max")
        p1_ready, p1_turned, p1t_ready, inv1_ready = sem("p1_ready", 4), sem("p1_turned"), sem("p1t_ready"), sem("inv1_ready")
        o1_done, h1_ready = sem("o1_done"), sem("h1_ready", 4)
        mom2, rstd2, x2_ready = sem("mom2", 10), sem("rstd2"), sem("x2_ready", 4)
        x2_turned, x2_copied, x2l_ready = sem("x2_turned"), sem("x2_copied", 2), sem("x2l_ready")
        gate_done, gate_step, gate_exp = sem("gate_done"), sem("gate_step", 17), sem("gate_exp")
        share_turned, share_ready = sem("share_turned"), sem("share_ready")
        items = CH + NE
        hid_done = sem("hid_done", items)
        hid_made = sem("hid_made", 2 * CH + NE)
        hid_rest, hid_rest_p = sem("hid_rest", CH - CH // POOL_EVERY), sem("hid_rest_p", CH // POOL_EVERY)
        hid_used = sem("hid_used", CH)
        down_read = sem("down_read", 1 + NE)
        moe_added = sem("moe_added", NE)
        moe_turned, h2_ready = sem("moe_turned"), sem("h2_ready")
        mom3, rstd3, x3_ready = sem("mom3", 10), sem("rstd3"), sem("x3_ready", 4)
        x3_turned, x3t_ready = sem("x3_turned"), sem("x3t_ready")
        rope_done, rope_read, rope_added = sem("rope_done", 4), sem("rope_read", 4), sem("rope_added", 2)
        xc_step, kc_done, kc_ready = sem("xc_step", 8), sem("kc_done"), sem("kc_ready")
        v_done, v_ready = sem("v_done", 2), sem("v_ready", 2)
        keys_ready, scored, s3_step = sem("keys_ready", 4), sem("scored", 8), sem("s3_step", 24)
        e3_ready, inv3_step = sem("e3_ready", 2), sem("inv3_step", 3)
        p3_turned, p3t_ready = sem("p3_turned", 8), sem("p3t_ready", 8)
        o3_done, o3_ready = sem("o3_done", 8), sem("o3_ready", 8)
        o3_turned, o3t_ready = sem("o3_turned"), sem("o3t_ready")
        wo_done, h3_ready, h3b_ready = sem("wo_done"), sem("h3_ready"), sem("h3b_ready")
        mom4, rstd4, x4_ready = sem("mom4", 10), sem("rstd4"), sem("x4_ready", 4)
        x4_turned, x4t_ready = sem("x4_turned"), sem("x4t_ready")
        up_done, up_ready, mlp_done = sem("up_done"), sem("up_ready"), sem("mlp_done")
        res_ready, res_stored = sem("res_ready"), sem("res_stored", 16)

        def rest_taken(g, q):
            if q % POOL_EVERY == POOL_EVERY - 1:
                return hid_rest_p, at(hid_rest_p, g, q // POOL_EVERY + 1)
            return hid_rest, at(hid_rest, g, q + 1 - q // POOL_EVERY)

        first = [q + max(0, q // FC - NS + 1) for q in range(CH)]
        def made(n):
            shares = sum(1 for r in range(NE) if first[(NS + r) * FC] - 1 < n)
            return 2 * (n - shares) + shares

        def schedule(iteration):
            def run(eng):
                for i in range(LAG_ALL + 1):
                    iteration(i, i)
                with eng.Fori(0, (NG - LAG_ALL - 1) // 2) as j:
                    for k in range(2):
                        iteration(j * 2 + (LAG_ALL + 1 + k), LAG_ALL + 1 + k)
                for i in range(NG, NG + LAG_ALL):
                    iteration(i, i)
            return run

        LAG_ALL = 3
        assert (NG - LAG_ALL - 1) % 2 == 0

        def stages(i, where):
            out = []
            for lag in range(4):
                on = 0 <= where - lag < NG or not isinstance(i, int)
                out.append((i - lag, (where - lag) % 2) if on else (None, 0))
            return out

        def pieces(plan, i, where):
            now, before = stages(i, where), stages(i - 1, where - 1)
            for late, stage, piece in plan:
                if stage == "set":
                    g, b = (0 if where == 1 else None), 0
                else:
                    g, b = (before if late else now)[STAGES.index(stage)]
                if g is not None:
                    yield g, b, stage, piece

        early = [(block_sum, block_c), (cwt, conv_w), (cb, conv_b), (ident, ident_c)]
        loads = [(cos, cos_c), (sin, sin_c), (mask1, mask1_c),
                 (mask2, mask2_c), (heads, heads_c), (pick, pick_c), (tie, tie_c),
                 (wq_s, wq), (wk_s, wk), (bq_s, bq), (bk_s, bk), (gw, gate_w), (gb, gate_b), (b1_s, b1),
                 (sb2_s, sb2), (rb2_s, rb2), (second["q"], swq), (second["qs"], swqs), (second["k"], swk),
                 (second["ks"], swks), (second["v"], swv), (second["kc"], swkc), (second["vc"], swvc),
                 (second["o"], swo), (cg, comp_gate), (sink_s, sink), (tw1_s, tw1), (tw2_s, tw2),
                 (tb1_s, tb1), (tb2_s, tb2)]
        EARLY, CONSTS = 16 * len(early), 16 * len(loads)
        READY_D, READY_A, READY_P = 22, 4, 2
        lots = [(w1, w1h, w1l, e) for e in range(NX)] + [(w2, w2h, w2l, e) for e in range(NX)]
        staging = [hid[:, 0, :], hid[:, 1, :], part[:, 0, :], part[:, 1, :]]

        block = ctx.enter_context(nc.Block())

        @block.sync
        def _(eng):
            def load(g, u, v):
                src = x[bass.ds(g * GI + 2 * u, 2), :, v * (HW // 2):(v + 1) * (HW // 2), :]
                eng.dma_start(xbuf[v][:], src.rearrange("i y x c -> (i y) x c")).then_inc(x_in[v], 16)

            def iteration(i, where):
                g = stages(i, where)[0][0]
                if g is None:
                    return
                for u in range(T):
                    for v in range(2):
                        if u or after(g, 1):
                            eng.wait_ge(pooled, at(pooled, g, 4 * (u - 1) + 2 * (v + 1)))
                        load(g, u, v)

            schedule(iteration)(eng)

        @block.tensor
        def _(eng):
            def turn_tiles(bank, src, eye):
                for t in range(T):
                    mm = nc.tensor.transpose(bank[:, t * P:(t + 1) * P], src(t), eye)
                return mm

            def tokens(g, b, kind, u=0, k=0):
                if kind == "pool":
                    v = k // 2
                    m = 3 * u + (0, 1, 1, 2)[k]
                    bank = pool_bank[m % 2]
                    if k % 2 == 0:
                        eng.wait_ge(x_summed, at(x_summed, g, 4 * u + 2 * v + 2))
                    if k != 2:
                        if m >= 2:
                            eng.wait_ge(pooled_read, at(pooled_read, g, m - 1))
                        elif after(g, 1):
                            if m == 0:
                                eng.wait_ge(h0_ready, at(h0_ready, g - 1, 1))
                            else:
                                eng.wait_ge(pooled_read, at(pooled_read, g, 0))
                    if k in (0, 3):
                        view = bank[:, 0:BX * PB].rearrange("p (k d n) -> p k d n", k=2, d=3)
                        views = [(0, view[:, 0]), (1, view[:, 1])]
                    else:
                        view = bank[:, 0:BX * PB].rearrange("p (d v n) -> p d v n", v=2, d=3)
                        views = [(2, view[:, :, v, :])]
                    for kx, cols in views:
                        for bx in range(BX // 2):
                            mm = nc.tensor.matmul(cols[:, :, bx * 2 * BX:(bx + 1) * 2 * BX],
                                                  blocks[v][:, bx, KIND_X[kx], :],
                                                  block_sum[:], start=True, stop=True)
                    mm.then_inc(pooled, 1)
                elif kind == "out":
                    eng.wait_ge(tapped, at(tapped, g, 32))
                    eng.wait_ge(pooled_read, at(pooled_read, g, 3 * T))
                    turn_tiles(pool_bank[0], lambda t: cols0[:, t, :], ident[:]).then_inc(h0_turned, 1)

            def attention(g, b, n):
                bank = att_bank
                if n == 1:
                    eng.wait_ge(x1_ready, at(x1_ready, g, 4))
                    if after(g, 1):
                        eng.wait_ge(share_ready, at(share_ready, g - 1, 1))
                    turn_tiles(bank, lambda t: x1[:, t, :], ident[:]).then_inc(x1_turned, 1)
                elif n == 2:
                    eng.wait_ge(x1t_ready, at(x1t_ready, g, 1))
                    nc.tensor.matmul(bank[:], wq_s[:], x1t[:], start=True, stop=True).then_inc(q1_done, 1)
                elif n == 3:
                    eng.wait_ge(q1_ready, at(q1_ready, g, 1))
                    nc.tensor.matmul(bank[:], wk_s[:], x1t[:], start=True, stop=True).then_inc(k1_done, 1)
                elif n == 4:
                    eng.wait_ge(k1_ready, at(k1_ready, g, 1))
                    for t in range(T):
                        mm = nc.tensor.matmul(bank[:, t * P:(t + 1) * P], q1[:, t * P:(t + 1) * P],
                                              k1[:, t * P:(t + 1) * P], start=True, stop=True)
                    mm.then_inc(s1_done, 1)
                elif n == 7:
                    eng.wait_ge(p1_ready, at(p1_ready, g, 4))
                    turn_tiles(bank, lambda t: s1[:, t, :], ident[:]).then_inc(p1_turned, 1)
                elif n == 8:
                    eng.wait_ge(p1t_ready, at(p1t_ready, g, 1))
                    for t in range(T):
                        mm = nc.tensor.matmul(bank[:, t * P:(t + 1) * P], p1t[:, t, :], x1[:, t, :],
                                              start=True, stop=True)
                    mm.then_inc(o1_done, 1)
                elif n == 10:
                    eng.wait_ge(x2_ready, at(x2_ready, g, 4))
                    turn_tiles(bank, lambda t: x2[:, t, :], ident[:]).then_inc(x2_turned, 1)
                elif n == 11:
                    eng.wait_ge(x2_copied, at(x2_copied, g, 2))
                    for t in range(T):
                        mm = nc.tensor.matmul(bank[:, t * NE:(t + 1) * NE], x2f[:, t * P:(t + 1) * P], gw[:],
                                              start=True, stop=True)
                    mm.then_inc(gate_done, 1)
                elif n == 13:
                    eng.wait_ge(gate_step, at(gate_step, g, 17))
                    bank_b = bank[0:3 * NE, 0:N // 2].bitcast(bf16)
                    for t in range(T):
                        mm = nc.tensor.transpose(bank_b[:, t * P:(t + 1) * P],
                                                 parts[:, t, :, :].rearrange("p a e -> p (a e)"), ident_b[:])
                    mm.then_inc(share_turned, 1)

            def up(g, b, q):
                e, n = q // FC, first[q]
                def bank_free(n):
                    if n >= 2:
                        eng.wait_ge(hid_made, at(hid_made, g, made(n - 1)))
                    elif after(g, 1):
                        eng.wait_ge(hid_made, at(hid_made, g - 1, made(items + n - 1)))
                if q == 0:
                    eng.wait_ge(x2l_ready, at(x2l_ready, g, 1))
                    eng.wait_ge(share_ready, at(share_ready, g, 1))
                if q % FC == 0 and e >= NS:
                    bank_free(n - 1)
                    nc.tensor.matmul(hid_bank[(n - 1) % 2][:], pick_b[:, e - NS, :], share_t[b][:],
                                     start=True, stop=True).then_inc(hid_done, 1)
                bank_free(n)
                cols = slice((q % FC) * P, (q % FC + 1) * P)
                bank = hid_bank[n % 2]
                nc.tensor.matmul(bank[:], w1h[:, e, cols], x2h[b][:], start=True, stop=False)
                nc.tensor.matmul(bank[:], w1l[:, e, cols], x2h[b][:], start=False, stop=False)
                nc.tensor.matmul(bank[:], w1h[:, e, cols], x2l[b][:], start=False, stop=True).then_inc(hid_done, 1)

            def down(g, q):
                e, r = q // FC, q % RING
                cols = slice((q % FC) * P, (q % FC + 1) * P)
                begin = q == 0 or (q % FC == 0 and e >= NS)
                end = q % FC == FC - 1 and e >= NS - 1
                eng.wait_ge(*rest_taken(g, q))
                if begin and q:
                    eng.wait_ge(down_read, at(down_read, g, e - NS + 1))
                elif begin and after(g, 1):
                    eng.wait_ge(down_read, at(down_read, g - 1, 1 + NE))
                nc.tensor.matmul(down_bank[:], w2h[:, e, cols], hid_h[:, r, :], start=begin, stop=False)
                nc.tensor.matmul(down_bank[:], w2l[:, e, cols], hid_h[:, r, :], start=False, stop=False)
                nc.tensor.matmul(down_bank[:], w2h[:, e, cols], hid_l[:, r, :], start=False, stop=end) \
                  .then_inc(hid_used, 1)

            def layer2(g, b, kind, n=0):
                b0, b1 = sec_bank
                if kind == "pre" and n == 0:
                    eng.wait_ge(moe_added, at(moe_added, g, NE))
                    if after(g, 1):
                        eng.wait_ge(res_ready, at(res_ready, g - 1, 1))
                    turn_tiles(b0, lambda t: moe[:, t * P:(t + 1) * P], ident[:]).then_inc(moe_turned, 1)
                elif kind == "pre" and n == 2:
                    eng.wait_ge(x3_ready, at(x3_ready, g, 4))
                    if after(g, 1):
                        eng.wait_ge(up_ready, at(up_ready, g - 1, 1))
                    turn_tiles(b1, lambda t: x3[:, t, :], ident[:]).then_inc(x3_turned, 1)
                elif kind == "pre" and n in (3, 4):
                    names = ("q", "qs") if n == 3 else ("k", "ks")
                    eng.wait_ge(x3t_ready, at(x3t_ready, g, 1))
                    for k, name in enumerate(names):
                        if n == 4:
                            eng.wait_ge(rope_read, at(rope_read, g, k + 1))
                        nc.tensor.matmul(sec_bank[k][:], second[name][:], x3t[:], start=True, stop=True) \
                          .then_inc(rope_done, 1)
                elif kind == "pre" and n == 5:
                    eng.wait_ge(xc_step, at(xc_step, g, 8))
                    eng.wait_ge(rope_read, at(rope_read, g, 3))
                    nc.tensor.matmul(b0[:, 0:GI * LC], second["kc"][:], xc[:].rearrange("p i w -> p (i w)"),
                                     start=True, stop=True).then_inc(kc_done, 1)
                elif kind == "pre" and n in (6, 7):
                    half = n - 6
                    bank = sec_bank[1 - half]
                    if half == 0:
                        eng.wait_ge(rope_read, at(rope_read, g, 4))
                    else:
                        eng.wait_ge(kc_ready, at(kc_ready, g, 1))
                    for m in range(4):
                        im = 4 * half + m
                        nc.tensor.matmul(bank[0:L, m * C:(m + 1) * C], x3t[:, im * L:(im + 1) * L], second["v"][:],
                                         start=True, stop=True)
                        mm = nc.tensor.matmul(bank[L:LK, m * C:(m + 1) * C], xc[:, im, :], second["vc"][:],
                                              start=True, stop=True)
                    mm.then_inc(v_done, 1)
                elif kind == "score":
                    t, half = n // 2, n % 2
                    bank = sec_bank[half]
                    if n == 0:
                        eng.wait_ge(rope_added, at(rope_added, g, 2))
                        eng.wait_ge(v_ready, at(v_ready, g, 2))
                    if half == 0:
                        eng.wait_ge(keys_ready, at(keys_ready, g, t + 1))
                    if n >= 2:
                        eng.wait_ge(s3_step, at(s3_step, g, 3 * (n - 2) + 1))
                    for im in range(2):
                        tok = (2 * t + im) * L
                        mm = nc.tensor.matmul(
                            bank[im * L:(im + 1) * L, 0:HH * LK], q3[:, tok:tok + L],
                            keys_h[:, t % 2, im, half * HH:(half + 1) * HH, :].rearrange("p h k -> p (h k)"),
                            start=True, stop=True)
                    mm.then_inc(scored, 1)
                elif kind == "turn":
                    if n == 0:
                        eng.wait_ge(e3_ready, at(e3_ready, g, 2))
                    if n >= 1:
                        eng.wait_ge(p3t_ready, at(p3t_ready, g, n))
                    for h in range(HH):
                        mm = nc.tensor.transpose(b0[0:LK, h * P:(h + 1) * P], e3[:, n, h, 0:LK], ident[:])
                    mm.then_inc(p3_turned, 1)
                elif kind == "value":
                    t, half = n // 2, n % 2
                    eng.wait_ge(p3t_ready, at(p3t_ready, g, n + 1))
                    if n >= 1:
                        eng.wait_ge(o3_ready, at(o3_ready, g, n))
                    for h in range(HH):
                        for im in range(2):
                            ch = (half * HH + h) * HD
                            mm = nc.tensor.matmul(b1[im * L:(im + 1) * L, h * HD:(h + 1) * HD],
                                                  p3t[:, half, h, im * L:(im + 1) * L],
                                                  values[:, 2 * t + im, ch:ch + HD], start=True, stop=True)
                    mm.then_inc(o3_done, 1)
                elif kind == "post" and n == 0:
                    eng.wait_ge(o3_ready, at(o3_ready, g, 8))
                    turn_tiles(b0, lambda t: o3[:, t, :], ident[:]).then_inc(o3_turned, 1)
                elif kind == "post" and n == 1:
                    eng.wait_ge(o3t_ready, at(o3t_ready, g, 1))
                    for t in range(T):
                        mm = nc.tensor.matmul(b1[:, t * P:(t + 1) * P], o3t[:, t * P:(t + 1) * P], second["o"][:],
                                              start=True, stop=True)
                    mm.then_inc(wo_done, 1)
                elif kind == "post" and n == 3:
                    eng.wait_ge(x4_ready, at(x4_ready, g, 4))
                    turn_tiles(b0, lambda t: x3[:, t, :], ident[:]).then_inc(x4_turned, 1)
                elif kind == "post" and n == 4:
                    eng.wait_ge(x4t_ready, at(x4t_ready, g, 1))
                    nc.tensor.matmul(b1[:], tw1_s[:], x3t[:], start=True, stop=True).then_inc(up_done, 1)
                elif kind == "post" and n == 5:
                    eng.wait_ge(up_ready, at(up_ready, g, 1))
                    for t in range(T):
                        mm = nc.tensor.matmul(b0[:, t * P:(t + 1) * P], o3t[:, t * P:(t + 1) * P], tw2_s[:],
                                              start=True, stop=True)
                    mm.then_inc(mlp_done, 1)

            def experts(g, b, kind, q):
                if kind == "up":
                    up(g, b, q)
                else:
                    down(g, q)

            eng.wait_ge(early_in, EARLY)

            def iteration(i, where):
                if where == 1:
                    eng.wait_ge(consts_in, CONSTS)
                    eng.wait_ge(ready_d, READY_D)
                    eng.wait_ge(ready_a, READY_A)
                    eng.wait_ge(ready_p, READY_P)
                for g, b, stage, piece in pieces(PLAN["pe"], i, where):
                    if where == 2 and piece == ("up", 0):
                        eng.wait_ge(weight_low, len(lots))
                    {"tok": tokens, "att": attention, "ffn": experts, "sec": layer2}[stage](g, b, *piece)

            schedule(iteration)(eng)

        @block.scalar
        def _(eng):
            for dst, src in early:
                eng.dma_start(dst[:], src).then_inc(early_in, 16)
            for dst, src in loads:
                eng.dma_start(dst[:] if dst is not pick else dst, src).then_inc(consts_in, 16)

            def setup():
                eng.wait_ge(consts_in, CONSTS)
                eng.wait_ge(early_in, EARLY)
                nc.scalar.activation(pick_b[:], pick, ACT.Copy).then_inc(ready_a, 1)
                nc.scalar.activation(ident_b[:], ident[:], ACT.Copy).then_inc(ready_a, 1)
                nc.scalar.mul(bqs_s[:], bq_s[:], float(C) ** -0.5).then_inc(ready_a, 1)
                eng.wait_ge(ready_d, READY_D - 2)
                nc.scalar.activation(cg[:], cg[:], ACT.Exp, bias=cg_max[:], accum_out=cg_sum[:]).then_inc(ready_a, 1)
                eng.wait_ge(ready_a, READY_A)

            def weights(g, b, kind, n):
                _, high, _, e = lots[n]
                eng.wait_ge(weight_in[n % STAGING], 16 * (n // STAGING + 1))
                nc.scalar.activation(high[:, e, :], staging[n % STAGING], ACT.Copy).then_inc(weight_high, 1)

            def tokens(g, b, kind, u=0, k=0):
                if kind == "pool" and k != 1:
                    m = (0, None, 1, 2)[k]
                    eng.wait_ge(pooled, at(pooled, g, 4 * u + k + 1))
                    if after(g, 1):
                        eng.wait_ge(tapped, at(tapped, g - 1, 16 * (u // 2 + 1)))
                    side = P // 2
                    if m == 1:
                        dst = pooled_s[:, 2, :, u, :]
                    else:
                        dst = pooled_s[:, 0:2, :, u, (m // 2) * side:(m // 2 + 1) * side].rearrange("p k d n -> p (k d) n")
                    src = pool_bank[(3 * u + m) % 2][:, 0:BX * PB].rearrange("p (r n) -> p r n", r=3 if m == 1 else 6)
                    nc.scalar.activation(dst, src, ACT.Copy).then_inc(pooled_read, 1)
                elif kind == "out":
                    eng.wait_ge(h0_turned, at(h0_turned, g, 1))
                    nc.scalar.activation(h0[b][:].rearrange("p t c -> p (t c)"), pool_bank[0][:], ACT.Copy) \
                      .then_inc(h0_ready, 1)

            def attention(g, b, n):
                bank = att_bank
                if n == 1:
                    eng.wait_ge(x1_turned, at(x1_turned, g, 1))
                    nc.scalar.activation(x1t[:], bank[:], ACT.Copy).then_inc(x1t_ready, 1)
                elif n == 2:
                    eng.wait_ge(q1_done, at(q1_done, g, 1))
                    nc.scalar.activation(q1[:], bank[:], ACT.Identity, bias=bqs_s[:], scale=float(C) ** -0.5) \
                      .then_inc(q1_ready, 1)
                elif n == 3:
                    eng.wait_ge(k1_done, at(k1_done, g, 1))
                    nc.scalar.activation(k1[:], bank[:], ACT.Identity, bias=bk_s[:]).then_inc(k1_ready, 1)
                elif n == 6:
                    eng.wait_ge(s1_max, at(s1_max, g, 1))
                    for t in range(T):
                        nc.scalar.activation(s1[:, t, :], s1[:, t, :], ACT.Exp, bias=nmax1[:, t:t + 1],
                                             accum_out=den1[:, t:t + 1]).then_inc(p1_ready, 1)
                elif n == 7:
                    eng.wait_ge(p1_turned, at(p1_turned, g, 1))
                    nc.scalar.activation(q1[:], bank[:], ACT.Copy) \
                      .then_inc(p1t_ready, 1)
                elif n == 10:
                    eng.wait_ge(x2_turned, at(x2_turned, g, 1))
                    nc.scalar.activation(x2h[b][:], bank[:], ACT.Copy).then_inc(x2_copied, 1)
                    nc.scalar.activation(x2f[:], bank[:], ACT.Copy).then_inc(x2_copied, 1)
                elif n == 13:
                    eng.wait_ge(share_turned, at(share_turned, g, 1))
                    nc.scalar.activation(share_t[b][:], bank[0:3 * NE, 0:N // 2].bitcast(bf16), ACT.Copy) \
                      .then_inc(share_ready, 1)

            def experts(g, b, kind, q):
                e, n = q // FC, first[q]
                if q % FC == 0 and e >= NS:
                    k = e - NS
                    eng.wait_ge(hid_done, at(hid_done, g, n))
                    if k >= 2:
                        eng.wait_ge(down_read, at(down_read, g, k))
                    elif after(g, 1):
                        eng.wait_ge(down_read, at(down_read, g - 1, k + NE))
                    nc.scalar.activation(share_b[:, k % 2, :], hid_bank[(n - 1) % 2][:], ACT.Copy).then_inc(hid_made, 1)
                eng.wait_ge(hid_done, at(hid_done, g, n + 1))
                if q >= RING:
                    eng.wait_ge(hid_used, at(hid_used, g, q - RING + 1))
                elif after(g, 1):
                    eng.wait_ge(hid_used, at(hid_used, g - 1, CH + q - RING + 1))
                if q >= 2:
                    eng.wait_ge(*rest_taken(g, q - 2))
                elif after(g, 1):
                    eng.wait_ge(*rest_taken(g - 1, CH + q - 2))
                for dst, r in ((hid_h, q % RING), (hid, q % 2)):
                    nc.scalar.activation(dst[:, r, :], hid_bank[n % 2][:], ACT.Gelu, bias=b1_s[:, q:q + 1]) \
                      .then_inc(hid_made, 1)

            def layer2(g, b, kind, n=0):
                b0, b1 = sec_bank
                if kind == "pre" and n == 2:
                    eng.wait_ge(x3_turned, at(x3_turned, g, 1))
                    nc.scalar.activation(x3t[:], b1[:], ACT.Copy).then_inc(x3t_ready, 1)
                elif kind == "pre" and n == 5:
                    eng.wait_ge(kc_done, at(kc_done, g, 1))
                    if after(g, 1):
                        eng.wait_ge(keys_ready, at(keys_ready, g - 1, 4))
                    nc.scalar.activation(keys[:, :, L:LK], b0[:, 0:GI * LC].rearrange("p (i w) -> p i w", i=GI),
                                         ACT.Copy).then_inc(kc_ready, 1)
                elif kind == "pre" and n in (6, 7):
                    half = n - 6
                    eng.wait_ge(v_done, at(v_done, g, half + 1))
                    nc.scalar.activation(values[:, 4 * half:4 * half + 4, :].rearrange("p i c -> p (i c)"),
                                         sec_bank[1 - half][0:LK, :], ACT.Copy).then_inc(v_ready, 1)
                elif kind == "exp":
                    for half in range(2):
                        eng.wait_ge(s3_step, at(s3_step, g, 12 * (half + 1)))
                        view = e3[:, T * half:T * half + T].rearrange("p n h k -> p (n h k)")
                        nc.scalar.activation(view, view, ACT.Exp).then_inc(e3_ready, 1)
                elif kind == "turn":
                    eng.wait_ge(p3_turned, at(p3_turned, g, n + 1))
                    if n >= 2:
                        eng.wait_ge(o3_done, at(o3_done, g, n - 1))
                    nc.scalar.activation(p3t[:, n % 2].rearrange("p h q -> p (h q)"), b0[0:LK, :], ACT.Copy) \
                      .then_inc(p3t_ready, 1)
                elif kind == "post" and n == 0:
                    eng.wait_ge(o3_turned, at(o3_turned, g, 1))
                    nc.scalar.activation(o3t[:], b0[:], ACT.Copy).then_inc(o3t_ready, 1)
                elif kind == "post" and n == 3:
                    eng.wait_ge(x4_turned, at(x4_turned, g, 1))
                    nc.scalar.activation(x3t[:], b0[:], ACT.Copy).then_inc(x4t_ready, 1)
                elif kind == "post" and n == 4:
                    eng.wait_ge(up_done, at(up_done, g, 1))
                    nc.scalar.activation(o3t[:], b1[:], ACT.Gelu, bias=tb1_s[:]).then_inc(up_ready, 1)
                elif kind == "post" and n == 5:
                    eng.wait_ge(res_ready, at(res_ready, g, 1))
                    eng.dma_start(out[bass.ds(g * GI, GI)].rearrange("(t i) l c -> (i l) t c", t=T), res[:]) \
                       .then_inc(res_stored, 16)

            def iteration(i, where):
                if where == 1:
                    setup()
                for g, b, stage, piece in pieces(PLAN["act"], i, where):
                    {"tok": tokens, "att": attention, "ffn": experts, "sec": layer2, "set": weights}[stage](g, b, *piece)

            schedule(iteration)(eng)
            eng.wait_ge(res_stored, at(res_stored, NG, 0))

        @block.vector
        def _(eng):
            step = [0]

            def done(ins):
                ins.then_inc(ready_d, 1)
                step[0] += 1

            done(nc.vector.memset(power[:], -0.5))
            done(nc.vector.memset(euler[:], 2.718281828459045))
            eng.wait_ge(early_in, EARLY)
            done(nc.vector.tensor_scalar(cwt[:], cwt[:], 1.0 / (BX * BX), None, ALU.mult))
            eng.wait_ge(ready_d, step[0])
            for dy in range(3):
                w = [cwt[:, 3 * dy + k:3 * dy + k + 1] for k in range(3)]
                t5 = [tapw[:, 5 * dy + k:5 * dy + k + 1] for k in range(5)]
                done(nc.vector.tensor_tensor(t5[1], w[0], w[1], ALU.add))
                done(nc.vector.tensor_tensor(t5[3], w[1], w[2], ALU.add))
                done(nc.vector.tensor_copy(t5[2], w[2]))
                done(nc.vector.tensor_copy(t5[4], w[0]))
                eng.wait_ge(ready_d, step[0])
                done(nc.vector.tensor_tensor(t5[0], t5[1], w[2], ALU.add))
            eng.wait_ge(ready_d, step[0])

            def setup():
                eng.wait_ge(consts_in, CONSTS)
                done(nc.vector.tensor_tensor(sb2_sum[:], sb2_s[:, 0:1], sb2_s[:, 1:2], ALU.add))
                done(nc.vector.tensor_reduce(cg_max[:], cg[:], AX.X, ALU.max, negate=True))
                assert step[0] == READY_D - 2
                for half in range(2):
                    nc.vector.tensor_copy(s3[:, half, :, LK:LK + 1],
                                          sink_s[:, half * HH:(half + 1) * HH].unsqueeze(2)).then_inc(sink_placed, 1)
                eng.wait_ge(ready_a, READY_A)
                done(nc.vector.reciprocal(cg_inv[:], cg_sum[:]))
                eng.wait_ge(ready_d, step[0])
                done(nc.vector.tensor_scalar(cg[:], cg[:], cg_inv[:], None, ALU.mult))
                eng.wait_ge(ready_d, step[0])
                eng.wait_ge(sink_placed, 2)

            def weights(g, b, kind, n):
                _, high, low, e = lots[n]
                eng.wait_ge(weight_high, n + 1)
                nc.vector.tensor_tensor(low[:, e, :], staging[n % STAGING], high[:, e, :], ALU.subtract) \
                  .then_inc(weight_low, 1)

            def moments(g, src, ready, need, mo, mv, ve, mom):
                eng.wait_ge(ready, at(ready, g, need))
                for t in range(T):
                    nc.vector.bn_stats(mo[:, t, :], src[:, t, :]).then_inc(mom, 1)
                eng.wait_ge(mom, at(mom, g, T))
                nc.vector.memset(ve[:], EPS).then_inc(mom, 1)
                for t in range(T):
                    nc.vector.bn_aggr(mv[:, t, :], mo[:, t, :]).then_inc(mom, 1)
                eng.wait_ge(mom, at(mom, g, 2 * T + 1))
                nc.vector.tensor_tensor(ve[:], ve[:], mv[:, :, 1], ALU.add).then_inc(mom, 1)

            def normalise(g, dst, src, mv, rs, rstd, ready):
                eng.wait_ge(rstd, at(rstd, g, 1))
                for t in range(T):
                    nc.vector.tensor_scalar(dst[:, t, :], src[:, t, :], mv[:, t, 0:1], rs[:, t:t + 1],
                                            ALU.subtract, ALU.mult).then_inc(ready, 1)

            def tokens(g, b, kind, u=0, k=0):
                if kind == "pair":
                    v = blocks[k]
                    eng.wait_ge(x_in[k], at(x_in[k], g, 16 * (u + 1)))
                    nc.vector.tensor_tensor(v[:, :, 1:6:2, :], v[:, :, 1:6:2, :], v[:, :, 2:7:2, :], ALU.add) \
                      .then_inc(x_paired, 1)
                elif kind == "tap":
                    pair, n = u, k
                    dy, term = n // 5, (0, 2, 4, 3, 1)[n % 5]
                    src_kind = (0, 1, 1, 2, 2)[term]
                    shift = (0, 0, 1, 0, -1)[term]
                    lo, hi = max(0, -shift), BX - max(0, shift)
                    m, tiles = 2 * BX, slice(2 * pair, 2 * pair + 2)
                    src = pooled_s[:, src_kind, dy, tiles, (lo + shift) * m:(hi + shift) * m]
                    dst = taps[:, tiles, lo * m:hi * m]
                    w = tapw[:, 5 * dy + term:5 * dy + term + 1]
                    if n == 0:
                        eng.wait_ge(pooled_read, at(pooled_read, g, 6 * (pair + 1)))
                        nc.vector.tensor_scalar(dst, src, w, cb[:], ALU.mult, ALU.add).then_inc(tapped, 1)
                    elif n < 14:
                        eng.wait_ge(tapped, at(tapped, g, 16 * pair + n))
                        nc.vector.scalar_tensor_tensor(dst, src, w, dst, ALU.mult, ALU.add).then_inc(tapped, 1)
                    else:
                        eng.wait_ge(tapped, at(tapped, g, 16 * pair + n))
                        if after(g, 1):
                            eng.wait_ge(h0_turned, at(h0_turned, g - 1, 1))
                        for t in (2 * pair, 2 * pair + 1):
                            nc.vector.scalar_tensor_tensor(
                                cols0[:, t, :].rearrange("p (m b) -> p b m", b=BX),
                                pooled_s[:, src_kind, dy, t, :].rearrange("p (b m) -> p b m", b=BX), w,
                                taps[:, t, :].rearrange("p (b m) -> p b m", b=BX), ALU.mult, ALU.add) \
                              .then_inc(tapped, 1)

            def attention(g, b, n):
                bank = att_bank
                tiles = bank[:].rearrange("p (t k) -> p t k", t=T)
                if n == 0:
                    moments(g, h0[b], h0_ready, 1, mo1, mv1, ve1, mom1)
                elif n == 1:
                    normalise(g, x1, h0[b], mv1, rs1, rstd1, x1_ready)
                elif n == 4:
                    eng.wait_ge(s1_done, at(s1_done, g, 1))
                    nc.vector.tensor_tensor(s1[:], tiles, mask1[:].unsqueeze(1).to_broadcast([P, T, P]), ALU.add) \
                      .then_inc(s1_masked, 1)
                elif n == 5:
                    eng.wait_ge(s1_masked, at(s1_masked, g, 1))
                    nc.vector.tensor_reduce(nmax1[:], s1[:], AX.X, ALU.max, negate=True).then_inc(s1_max, 1)
                elif n == 7:
                    eng.wait_ge(p1_ready, at(p1_ready, g, 4))
                    nc.vector.reciprocal(inv1[:], den1[:]).then_inc(inv1_ready, 1)
                elif n == 8:
                    eng.wait_ge(o1_done, at(o1_done, g, 1))
                    eng.wait_ge(inv1_ready, at(inv1_ready, g, 1))
                    for t in range(T):
                        nc.vector.scalar_tensor_tensor(h1[b][:, t, :], tiles[:, t, :], inv1[:, t:t + 1],
                                                       h0[b][:, t, :], ALU.mult, ALU.add).then_inc(h1_ready, 1)
                elif n == 9:
                    moments(g, h1[b], h1_ready, 4, mo2, mv2, ve2, mom2)
                elif n == 10:
                    normalise(g, x2, h1[b], mv2, rs2, rstd2, x2_ready)
                elif n == "low":
                    eng.wait_ge(x2_copied, at(x2_copied, g, 2))
                    nc.vector.tensor_tensor(x2l[b][:], x2f[:], x2h[b][:], ALU.subtract).then_inc(x2l_ready, 1)
                elif n == 11:
                    eng.wait_ge(gate_done, at(gate_done, g, 1))
                    nc.vector.tensor_tensor(lg[:], bank[:, 0:T * NE].rearrange("p (t e) -> p t e", t=T),
                                            gb[:].unsqueeze(1).to_broadcast([P, T, NE]), ALU.add).then_inc(gate_step, 1)
                    eng.wait_ge(gate_step, at(gate_step, g, 1))
                    nc.vector.tensor_reduce(lmax[:], lg[:], AX.X, ALU.max).then_inc(gate_step, 1)
                    eng.wait_ge(gate_step, at(gate_step, g, 2))
                    nc.vector.tensor_tensor(lg[:], lg[:], lmax[:].unsqueeze(2).to_broadcast([P, T, NE]),
                                            ALU.subtract).then_inc(gate_step, 1)
                elif n == 12:
                    four = [P, T, NE, NE]
                    eng.wait_ge(gate_exp, at(gate_exp, g, 1))
                    nc.vector.tensor_reduce(esum[:], ez[:], AX.X, ALU.add).then_inc(gate_step, 1)
                    eng.wait_ge(gate_step, at(gate_step, g, 4))
                    nc.vector.reciprocal(einv[:], esum[:]).then_inc(gate_step, 1)
                    eng.wait_ge(gate_step, at(gate_step, g, 5))
                    nc.vector.tensor_tensor(prob[:], ez[:], einv[:].unsqueeze(2).to_broadcast([P, T, NE]),
                                            ALU.mult).then_inc(gate_step, 1)
                    eng.wait_ge(gate_step, at(gate_step, g, 6))
                    pe_, pj = prob[:].unsqueeze(3).to_broadcast(four), prob[:].unsqueeze(2).to_broadcast(four)
                    nc.vector.tensor_tensor(above, pj, pe_, ALU.is_gt).then_inc(gate_step, 1)
                    nc.vector.tensor_tensor(equal, pj, pe_, ALU.is_equal).then_inc(gate_step, 1)
                    eng.wait_ge(gate_step, at(gate_step, g, 8))
                    nc.vector.tensor_tensor(equal, equal, tie[:].unsqueeze(1).to_broadcast(four),
                                            ALU.mult).then_inc(gate_step, 1)
                    eng.wait_ge(gate_step, at(gate_step, g, 9))
                    nc.vector.tensor_tensor(above, above, equal, ALU.add).then_inc(gate_step, 1)
                    eng.wait_ge(gate_step, at(gate_step, g, 10))
                    nc.vector.tensor_reduce(rank[:], above, AX.X, ALU.add).then_inc(gate_step, 1)
                    eng.wait_ge(gate_step, at(gate_step, g, 11))
                    nc.vector.scalar_tensor_tensor(share[:], rank[:], 1.5, prob[:], ALU.is_lt, ALU.mult) \
                      .then_inc(gate_step, 1)
                    eng.wait_ge(gate_step, at(gate_step, g, 12))
                    nc.vector.tensor_copy(parts[:, :, 0, :], share[:]).then_inc(gate_step, 1)
                    eng.wait_ge(gate_step, at(gate_step, g, 13))
                    nc.vector.tensor_tensor(rest1[:], share[:], parts[:, :, 0, :], ALU.subtract).then_inc(gate_step, 1)
                    eng.wait_ge(gate_step, at(gate_step, g, 14))
                    nc.vector.tensor_copy(parts[:, :, 1, :], rest1[:]).then_inc(gate_step, 1)
                    eng.wait_ge(gate_step, at(gate_step, g, 15))
                    nc.vector.tensor_tensor(rest2[:], rest1[:], parts[:, :, 1, :], ALU.subtract).then_inc(gate_step, 1)
                    eng.wait_ge(gate_step, at(gate_step, g, 16))
                    nc.vector.tensor_copy(parts[:, :, 2, :], rest2[:]).then_inc(gate_step, 1)

            def hidden(g, q):
                eng.wait_ge(hid_made, at(hid_made, g, made(first[q] + 1)))
                nc.vector.tensor_tensor(hid_l[:, q % RING, :], hid[:, q % 2, :], hid_h[:, q % RING, :],
                                        ALU.subtract).then_inc(hid_rest, 1)

            def expert_sum(g, q):
                e = q // FC
                eng.wait_ge(hid_used, at(hid_used, g, q + 1))
                if e == NS - 1:
                    if after(g, 1):
                        eng.wait_ge(moe_turned, at(moe_turned, g - 1, 1))
                    nc.vector.tensor_scalar(moe[:], down_bank[:], sb2_sum[:], None, ALU.add).then_inc(down_read, 1)
                else:
                    r = e - NS
                    if r >= 2:
                        eng.wait_ge(moe_added, at(moe_added, g, r - 1))
                    elif after(g, 1):
                        eng.wait_ge(moe_added, at(moe_added, g - 1, NE + r - 1))
                    nc.vector.scalar_tensor_tensor(part[:, r % 2, :], down_bank[:], rb2_s[:, r:r + 1],
                                                   share_b[:, r % 2, :], ALU.add, ALU.mult).then_inc(down_read, 1)

            def experts(g, b, kind, q):
                if kind == "hidden":
                    hidden(g, q)
                else:
                    expert_sum(g, q)

            def layer2(g, b, kind, n=0):
                b0, b1 = sec_bank
                if kind == "pre" and n == 0:
                    eng.wait_ge(moe_turned, at(moe_turned, g, 1))
                    nc.vector.tensor_tensor(h2[:].rearrange("p t c -> p (t c)"), b0[:],
                                            h1[b][:].rearrange("p t c -> p (t c)"), ALU.add).then_inc(h2_ready, 1)
                elif kind == "pre" and n == 1:
                    moments(g, h2, h2_ready, 1, mo3, mv3, ve3, mom3)
                elif kind == "pre" and n == 2:
                    normalise(g, x3, h2, mv3, rs3, rstd3, x3_ready)
                elif kind == "pre" and n in (3, 4):
                    for k, table in enumerate((cos, sin)):
                        m = 2 * (n - 3) + k
                        eng.wait_ge(rope_done, at(rope_done, g, m + 1))
                        if n == 4 and k == 0:
                            eng.wait_ge(rope_added, at(rope_added, g, 1))
                        elif n == 3 and k == 0 and after(g, 1):
                            eng.wait_ge(rope_added, at(rope_added, g - 1, 2))
                        nc.vector.tensor_tensor(roped[:, k, :].rearrange("p (i l) -> p i l", i=GI),
                                                sec_bank[k][:].rearrange("p (i l) -> p i l", i=GI),
                                                table[:].unsqueeze(1).to_broadcast([P, GI, L]), ALU.mult) \
                          .then_inc(rope_read, 1)
                elif kind == "pre" and n == 5:
                    eng.wait_ge(x3t_ready, at(x3t_ready, g, 1))
                    tok = x3t[:].rearrange("p (i l) -> p i l", i=GI)
                    for r in range(RATIO):
                        src = tok[:, :, r:r + STRIDE * (LC - 1) + 1:STRIDE]
                        if r == 0:
                            nc.vector.tensor_scalar(xc[:], src, cg[:, 0:1], None, ALU.mult).then_inc(xc_step, 1)
                        else:
                            eng.wait_ge(xc_step, at(xc_step, g, r))
                            nc.vector.scalar_tensor_tensor(xc[:], src, cg[:, r:r + 1], xc[:], ALU.mult, ALU.add) \
                              .then_inc(xc_step, 1)
                elif kind == "score":
                    half = n % 2
                    three = [P, HH, LK]
                    eng.wait_ge(scored, at(scored, g, n + 1))
                    nc.vector.scalar_tensor_tensor(
                        s3[:, half, :, 0:LK], sec_bank[half][:, 0:HH * LK].rearrange("p (h k) -> p h k", h=HH),
                        float(HD) ** -0.5, mask2[:].unsqueeze(1).to_broadcast(three), ALU.mult, ALU.add) \
                      .then_inc(s3_step, 1)
                    eng.wait_ge(s3_step, at(s3_step, g, 3 * n + 1))
                    nc.vector.tensor_reduce(m3[:, half, :], s3[:, half], AX.X, ALU.max).then_inc(s3_step, 1)
                    eng.wait_ge(s3_step, at(s3_step, g, 3 * n + 2))
                    nc.vector.tensor_tensor(e3[:, n], s3[:, half],
                                            m3[:, half, :].unsqueeze(2).to_broadcast([P, HH, LK + 1]),
                                            ALU.subtract).then_inc(s3_step, 1)
                elif kind == "turn" and n < 2:
                    if n == 0:
                        for half in range(2):
                            eng.wait_ge(e3_ready, at(e3_ready, g, half + 1))
                            nc.vector.tensor_reduce(den3[:, T * half:T * half + T], e3[:, T * half:T * half + T],
                                                    AX.X, ALU.add).then_inc(inv3_step, 1)
                        eng.wait_ge(inv3_step, at(inv3_step, g, 2))
                        nc.vector.reciprocal(inv3[:], den3[:]).then_inc(inv3_step, 1)
                elif kind == "value":
                    t, half = n // 2, n % 2
                    eng.wait_ge(o3_done, at(o3_done, g, n + 1))
                    if n == 0:
                        eng.wait_ge(inv3_step, at(inv3_step, g, 3))
                    cols = slice(half * HH * HD, (half + 1) * HH * HD)
                    nc.vector.tensor_tensor(o3[:, t, cols].rearrange("p (h d) -> p h d", h=HH),
                                            b1[:, 0:HH * HD].rearrange("p (h d) -> p h d", h=HH),
                                            inv3[:, n, :].unsqueeze(2).to_broadcast([P, HH, HD]), ALU.mult) \
                      .then_inc(o3_ready, 1)
                elif kind == "post" and n == 1:
                    eng.wait_ge(wo_done, at(wo_done, g, 1))
                    if after(g, 1):
                        eng.wait_ge(res_stored, at(res_stored, g - 1, 16))
                    nc.vector.tensor_tensor(h3[:].rearrange("p t c -> p (t c)"), b1[:],
                                            h2[:].rearrange("p t c -> p (t c)"), ALU.add).then_inc(h3_ready, 1)
                elif kind == "post" and n == 2:
                    moments(g, h3, h3_ready, 1, mo4, mv4, ve4, mom4)
                elif kind == "post" and n == 3:
                    normalise(g, x3, h3, mv4, rs4, rstd4, x4_ready)
                elif kind == "post" and n == 5:
                    eng.wait_ge(mlp_done, at(mlp_done, g, 1))
                    eng.wait_ge(h3b_ready, at(h3b_ready, g, 1))
                    nc.vector.tensor_tensor(res[:].rearrange("p t c -> p (t c)"), b0[:],
                                            h3b[:].rearrange("p t c -> p (t c)"), ALU.add).then_inc(res_ready, 1)

            def iteration(i, where):
                if where == 1:
                    setup()
                for g, b, stage, piece in pieces(PLAN["dve"], i, where):
                    {"tok": tokens, "att": attention, "ffn": experts, "sec": layer2, "set": weights}[stage](g, b, *piece)

            schedule(iteration)(eng)

        @block.gpsimd
        def _(eng):
            def setup():
                eng.wait_ge(consts_in, CONSTS)
                for w in (tw1_s, tw2_s):
                    nc.gpsimd.affine_select(out=w[:], in_=w[:], compare_op=ALU.is_ge, fill=0.0, base=0,
                                            pattern=[[1, P]], channel_multiplier=-1).then_inc(ready_p, 1)

            def weights(g, b, kind, n):
                src, _, _, e = lots[n]
                if n >= STAGING:
                    eng.wait_ge(weight_low, n - STAGING + 1)
                eng.dma_start(staging[n % STAGING], src[:, e, :]).then_inc(weight_in[n % STAGING], 16)

            def inverse_root(g, rs, ve, mom, rstd):
                eng.wait_ge(mom, at(mom, g, 10))
                nc.gpsimd.tensor_tensor(rs[:], ve[:], power[:], ALU.pow).then_inc(rstd, 1)

            def attention(g, b, n):
                if n == 0:
                    inverse_root(g, rs1, ve1, mom1, rstd1)
                elif n == 9:
                    inverse_root(g, rs2, ve2, mom2, rstd2)
                elif n == 11:
                    eng.wait_ge(gate_step, at(gate_step, g, 3))
                    nc.gpsimd.tensor_tensor(ez[:].rearrange("p t e -> p (t e)"), euler[:],
                                            lg[:].rearrange("p t e -> p (t e)"), ALU.pow).then_inc(gate_exp, 1)

            def tokens(g, b, kind, u=0, k=0):
                half, k = k // 2, k % 2
                v = blocks[half]
                if k == 0:
                    eng.wait_ge(x_paired, at(x_paired, g, 2 * u + half + 1))
                else:
                    eng.wait_ge(x_summed, at(x_summed, g, 4 * u + 2 * half + 1))
                nc.gpsimd.tensor_tensor(v[:, :, 1, :], v[:, :, 1, :], v[:, :, 2 * k + 3, :], ALU.add) \
                  .then_inc(x_summed, 1)

            def experts(g, b, kind, q):
                r = q // FC - NS
                if kind == "hidden":
                    eng.wait_ge(hid_made, at(hid_made, g, made(first[q] + 1)))
                    nc.gpsimd.tensor_tensor(hid_l[:, q % RING, :], hid[:, q % 2, :], hid_h[:, q % RING, :],
                                            ALU.subtract).then_inc(hid_rest_p, 1)
                    return
                if r >= 0:
                    eng.wait_ge(down_read, at(down_read, g, 2 + r))
                    if r >= 1:
                        eng.wait_ge(moe_added, at(moe_added, g, r))
                    nc.gpsimd.tensor_tensor(moe[:], moe[:], part[:, r % 2, :], ALU.add).then_inc(moe_added, 1)

            def layer2(g, b, kind, n=0):
                if kind == "pre" and n == 1:
                    inverse_root(g, rs3, ve3, mom3, rstd3)
                elif kind == "pre" and n == 3:
                    eng.wait_ge(rope_read, at(rope_read, g, 2))
                    if after(g, 1):
                        eng.wait_ge(scored, at(scored, g - 1, 8))
                    nc.gpsimd.tensor_tensor(q3[:], roped[:, 0, :], roped[:, 1, :], ALU.add).then_inc(rope_added, 1)
                elif kind == "pre" and n == 4:
                    eng.wait_ge(rope_read, at(rope_read, g, 4))
                    if after(g, 1):
                        eng.wait_ge(keys_ready, at(keys_ready, g - 1, 4))
                    nc.gpsimd.tensor_tensor(keys[:, :, 0:L], roped[:, 0, :].rearrange("p (i l) -> p i l", i=GI),
                                            roped[:, 1, :].rearrange("p (i l) -> p i l", i=GI), ALU.add) \
                      .then_inc(rope_added, 1)
                elif (kind == "pre" and n in (6, 7)) or (kind == "score" and n in (2, 4)):
                    t = n - 6 if kind == "pre" else n // 2 + 1
                    if t == 0:
                        eng.wait_ge(rope_added, at(rope_added, g, 2))
                        eng.wait_ge(kc_ready, at(kc_ready, g, 1))
                    if t >= 2:
                        eng.wait_ge(scored, at(scored, g, 2 * (t - 1)))
                    for im in range(2):
                        four = [P, HEADS, LK]
                        ins = nc.gpsimd.tensor_tensor(keys_h[:, t % 2, im],
                                                      keys[:, 2 * t + im, :].unsqueeze(1).to_broadcast(four),
                                                      heads[:].unsqueeze(2).to_broadcast(four), ALU.mult)
                    ins.then_inc(keys_ready, 1)
                elif kind == "post" and n == 1:
                    eng.wait_ge(h3_ready, at(h3_ready, g, 1))
                    if after(g, 1):
                        eng.wait_ge(res_ready, at(res_ready, g - 1, 1))
                    nc.gpsimd.tensor_tensor(h3b[:], h3[:], tb2_s[:].unsqueeze(1).to_broadcast([P, T, C]), ALU.add) \
                      .then_inc(h3b_ready, 1)
                elif kind == "post" and n == 2:
                    inverse_root(g, rs4, ve4, mom4, rstd4)

            def iteration(i, where):
                if where == 1:
                    setup()
                for g, b, stage, piece in pieces(PLAN["pool"], i, where):
                    {"tok": tokens, "att": attention, "ffn": experts, "sec": layer2, "set": weights}[stage](g, b, *piece)

            schedule(iteration)(eng)


def kernel(**inputs):
    import numpy as _np
    import concourse.bacc as _bacc
    from concourse import mybir as _mybir
    from concourse.bass_utils import run_bass_kernel_spmd as _run

    a = {k: _np.asarray(v) for k, v in inputs.items()}
    f32 = _np.float32

    def rows(v):
        v = v.reshape(1, -1)
        return _np.broadcast_to(v, (P, v.shape[1]))

    def halves(w):
        return w.reshape(HEADS, 2, HD // 2, C)[:, ::-1].reshape(C, C)

    pix, tok = _np.arange(HW), _np.arange(L)
    block = _np.zeros((2, HW, 3, 2, BX), f32)
    for dy in range(3):
        for by in range(BX):
            on = (pix >= by * 8 + dy - 1) & (pix <= by * 8 + 7 + dy - 1)
            for im in range(2):
                block[im, on, dy, im, by] = 1
    half = HD // 2
    freq = (f32(1.0) / _np.power(f32(10000.0), _np.arange(half, dtype=f32) / f32(half))).astype(f32)
    angle = tok.astype(f32)[None, :] * freq[:, None]
    cos = _np.tile(_np.cos(angle), (2 * HEADS, 1)).astype(f32)
    sin = _np.tile(_np.concatenate([-_np.sin(angle), _np.sin(angle)]), (HEADS, 1)).astype(f32)
    image = _np.arange(P) // L
    mask1 = _np.where(image[:, None] == image[None, :], f32(0), f32(-1e30))
    pos = _np.arange(P) % L
    window = (pos[:, None] >= tok[None, :]) & (pos[:, None] - tok[None, :] < 128)
    comp = pos[:, None] >= (_np.arange(LC) * STRIDE + RATIO - 1)[None, :]
    mask2 = _np.where(_np.concatenate([window, comp], 1), f32(0), f32(-1e30))
    heads = (_np.arange(C)[:, None] // HD == _np.arange(HEADS)[None, :]).astype(f32)
    pick = _np.tile(_np.eye(NE, dtype=f32)[:, :, None], (3, 1, P))
    tie = _np.broadcast_to(_np.tril(_np.ones((NE, NE), f32), -1), (P, NE, NE))

    w1 = _np.concatenate([a["L0_ffn_sw1"], a["L0_ffn_rw1"]])
    w2 = _np.concatenate([a["L0_ffn_sw2"], a["L0_ffn_rw2"]])
    b1 = _np.concatenate([a["L0_ffn_sb1"], a["L0_ffn_rb1"]])
    named = dict(
        x=a["x"], conv_w=a["L0_tok_conv_w"].reshape(9, C).T, conv_b=a["L0_tok_conv_b"].reshape(C, 1),
        wq=a["L0_attn_Wq"], bq=a["L0_attn_bq"].reshape(C, 1), wk=a["L0_attn_Wk"], bk=a["L0_attn_bk"].reshape(C, 1),
        gate_w=a["L0_ffn_gate_w"].T, gate_b=rows(a["L0_ffn_gate_b"]),
        w1=w1.transpose(2, 0, 1), b1=b1.reshape(CH, P).T,
        w2=w2.reshape(NX, C, FC, P).transpose(3, 0, 2, 1).reshape(P, NX, F),
        sb2=a["L0_ffn_sb2"].T, rb2=a["L0_ffn_rb2"].T,
        swq=a["L1_attn_wq"].T, swqs=halves(a["L1_attn_wq"]).T, swk=a["L1_attn_wk"].T, swks=halves(a["L1_attn_wk"]).T,
        swv=a["L1_attn_wv"].T, swkc=a["L1_attn_wk_c"].T, swvc=a["L1_attn_wv_c"].T, swo=a["L1_attn_wo"].T,
        comp_gate=rows(a["L1_attn_gate_logits"]), sink=rows(a["L1_attn_sink_logit"]),
        tw1=a["L1_ffn_W1"].T, tb1=a["L1_ffn_b1"].reshape(P, 1), tw2=a["L1_ffn_W2"].T, tb2=rows(a["L1_ffn_b2"]),
        ident_c=_np.eye(P, dtype=f32), block_c=block.reshape(P, PB), cos_c=cos, sin_c=sin, mask1_c=mask1,
        mask2_c=mask2, heads_c=heads, pick_c=pick, tie_c=tie)

    nc = _bacc.Bacc("TRN2", target_bir_lowering=False, num_devices=1)
    arrays, args = {}, {}
    for name, value in named.items():
        value = _np.ascontiguousarray(value)
        arrays[f"in_{name}"] = value
        args[name] = nc.dram_tensor(f"in_{name}", value.shape, _mybir.dt.from_np(value.dtype), kind="ExternalInput").ap()
    args["out"] = nc.dram_tensor("out_0", (NI, L, C), _mybir.dt.float32, kind="ExternalOutput").ap()
    program(nc, **args)
    r = _run(nc, [arrays], core_ids=[0])
    return r.results[0]["out_0"]
```

```python
import concourse.bass as bass
from concourse import mybir
from contextlib import ExitStack

fp32 = mybir.dt.float32
bf16 = mybir.dt.bfloat16
ALU = mybir.AluOpType
ACT = mybir.ActivationFunctionType
AX = mybir.AxisListType

NI, HW, C = 128, 64, 128
P = 128
BX = 8
L = BX * BX
GI = 8
NG = NI // GI
T = GI * L // P
N = T * P
NS, NE, F = 2, 8, 512
NX = NS + NE
FC = F // P
CH = NX * FC
HEADS, HD = 8, C // 8
RATIO, STRIDE = 8, 4
LC = (L - RATIO) // STRIDE + 1
LK = L + LC
HH = HEADS // 2
PB = 3 * 2 * BX
EPS = 1e-5
HIDS = 4
STAGING = 4
POOL_EVERY = 5
RING = 5
KIND_X = (4, 2, 6)

STAGES = ("tok", "att", "ffn", "sec")
STAGE_OF = dict(pair="tok", add="tok", ends="tok", inner="tok", pool="tok", tap="tok", out="tok",
                att="att", low="att", up="ffn", hidden="ffn", down="ffn", sum="ffn", pre="sec",
                score="sec", exp="sec", turn="sec", value="sec", post="sec", weights="set")

ORDER = dict(
    pe="""
        up.0 up.1 down.38' down.39' up.2 up.3 down.0 down.1 up.4 att.1 pool.0.0 pool.0.1 up.5 pre.0 down.2 up.6
        att.2 down.3 up.7 down.4 att.3 down.5 up.8 down.6 pre.2 pool.0.2 pool.0.3 up.9 up.10 att.4 pre.3 up.11
        down.7 pre.4 up.12 down.8 pre.5 pre.6 pool.1.0 up.13 pool.1.1 down.9 pre.7 up.14 up.15 score.0 score.1
        down.10 down.11 score.2 score.3 up.16 down.12 up.17 pool.1.2 down.13 up.18 down.14 up.19 pool.1.3
        down.15 score.4 up.20 score.5 score.6 down.16 score.7 down.17 up.21 down.18 down.19 up.22 pool.2.0
        pool.2.1 att.7 turn.0 down.20 up.23 turn.1 value.0 att.8 turn.2 value.1 down.21 turn.3 value.2 up.24
        pool.2.2 turn.4 up.25 pool.2.3 down.22 up.26 value.3 down.23 turn.5 att.10 value.4 up.27 turn.6 value.5
        att.11 turn.7 value.6 up.28 value.7 up.29 post.0 down.24 post.1 up.30 down.25 down.26 down.27 up.31
        pool.3.0 down.28 pool.3.1 up.32 up.33 pool.3.2 pool.3.3 down.29 up.34 att.13 down.30 up.35 down.31
        post.3 up.36 post.4 down.32 up.37 up.38 down.33 down.34 down.35 up.39 post.5 down.36 down.37 out""",
    act="""
        weights.0 hidden.0 hidden.1 ends.0.0 weights.1 hidden.2 weights.2 inner.0.0 hidden.3 weights.3 hidden.4
        att.1 hidden.5 weights.4 hidden.6 att.2 ends.0.1 hidden.7 pool.0.0 inner.0.1 weights.5 att.3 hidden.8
        pre.2 hidden.9 ends.1.0 hidden.10 hidden.11 inner.1.0 pool.0.2 pool.0.3 weights.6 pre.5 weights.7
        weights.8 hidden.12 pre.6 pool.1.0 hidden.13 pre.7 hidden.14 weights.9 ends.1.1 hidden.15 inner.1.1
        hidden.16 hidden.17 pool.1.2 hidden.18 hidden.19 pool.1.3 weights.10 weights.11 ends.2.0 hidden.20
        weights.12 inner.2.0 att.6 exp hidden.21 turn.0 weights.13 att.7 weights.14 hidden.22 turn.1 ends.2.1
        turn.2 hidden.23 pool.2.0 inner.2.1 turn.3 hidden.24 hidden.25 turn.4 hidden.26 ends.3.0 turn.5 att.10
        inner.3.0 turn.6 weights.15 hidden.27 turn.7 hidden.28 post.0 weights.16 hidden.29 ends.3.1 weights.17
        hidden.30 pool.2.2 pool.2.3 pool.3.0 hidden.31 inner.3.1 hidden.32 weights.18 pool.3.2 pool.3.3
        hidden.33 hidden.34 hidden.35 post.3 att.13 hidden.36 hidden.37 post.4 weights.19 hidden.38 hidden.39
        post.5 out""",
    dve="""
        pair.0.0 hidden.38' att.0 hidden.0 weights.0 sum.39' hidden.1 att.1 inner.0.0 weights.1 hidden.2
        hidden.3 weights.2 pair.0.1 pre.0 pre.1 hidden.5 hidden.6 pre.2 weights.3 hidden.7 inner.0.1 weights.4
        pair.1.0 pre.5 pre.3 sum.7 weights.5 hidden.8 pre.4 inner.1.0 hidden.10 att.4 pair.1.1 weights.6
        hidden.11 hidden.12 hidden.13 att.5 score.0 weights.7 score.1 sum.11 weights.8 score.2 inner.1.1
        hidden.15 score.3 hidden.16 weights.9 pair.2.0 hidden.17 hidden.18 weights.10 sum.15 tap.0.0 score.4
        tap.0.1 score.5 tap.0.2 score.6 weights.11 tap.0.3 score.7 tap.0.4 inner.2.0 hidden.20 tap.0.5 sum.19
        pair.2.1 tap.0.6 att.7 tap.0.7 hidden.21 tap.0.8 weights.12 value.0 att.8 value.1 hidden.22 att.9
        inner.2.1 value.2 pair.3.0 hidden.23 att.10 value.3 tap.0.9 weights.13 sum.23 weights.14 tap.0.10
        value.4 hidden.25 tap.0.11 hidden.26 value.5 att.11 weights.15 inner.3.0 value.6 weights.16 tap.0.12
        hidden.27 value.7 pair.3.1 hidden.28 tap.0.13 post.1 tap.0.14 post.2 sum.27 att.12 inner.3.1 weights.17
        hidden.30 hidden.31 weights.18 tap.1.0 post.3 tap.1.1 tap.1.2 low tap.1.3 hidden.32 tap.1.4 tap.1.5
        sum.31 tap.1.6 hidden.33 tap.1.7 tap.1.8 hidden.35 tap.1.9 hidden.36 tap.1.10 hidden.37 tap.1.11 sum.35
        tap.1.12 tap.1.13 post.5 tap.1.14 weights.19""",
    pool="""
        sum.27' sum.31' weights.0 weights.1 weights.2 sum.35' weights.3 hidden.39' add.0.0 add.0.1 att.0
        ends.0.0 weights.4 sum.39' hidden.4 add.0.2 add.0.3 pre.1 ends.0.1 weights.5 weights.6 add.1.0 add.1.1
        ends.1.0 pre.3 hidden.9 weights.7 weights.8 pre.4 pre.6 weights.9 weights.10 add.1.2 pre.7 weights.11
        add.1.3 ends.1.1 hidden.14 score.2 weights.12 score.4 weights.13 add.2.0 weights.14 add.2.1 hidden.19
        ends.2.0 sum.7 sum.11 sum.15 sum.19 add.2.2 add.2.3 ends.2.1 weights.15 att.9 hidden.24 add.3.0 add.3.1
        weights.16 weights.17 ends.3.0 att.11 add.3.2 weights.18 add.3.3 ends.3.1 post.2 post.1 weights.19
        hidden.29 sum.23 hidden.34""")


def read(text):
    for word in text.split():
        name, *numbers = word.rstrip("'").split(".")
        piece = tuple(int(n) for n in numbers)
        yield word[-1] == "'", STAGE_OF[name], piece if name == "att" else (name,) + piece


PLAN = {engine: list(read(text)) for engine, text in ORDER.items()}


def after(g, n):
    return not isinstance(g, int) or g >= n


def program(nc, x, conv_w, conv_b, wq, bq, wk, bk, gate_w, gate_b, w1, b1, w2, sb2, rb2,
            swq, swqs, swk, swks, swv, swkc, swvc, swo, comp_gate, sink, tw1, tb1, tw2, tb2,
            ident_c, block_c, cos_c, sin_c, mask1_c, limit_c, place_c, part_c, heads_c, pick_c, tie_c, out):
    with ExitStack() as ctx:
        per = {}
        kept = []

        def sb(name, shape, dt=fp32):
            return ctx.enter_context(nc.sbuf_tensor(name, shape, dt))

        def pb(name):
            return ctx.enter_context(nc.psum_tensor(name, [P, 512], fp32))

        def sem(name, n=1):
            s = ctx.enter_context(nc.semaphore(name))
            per[id(s)] = n
            kept.append(s)
            return s

        def at(s, g, k):
            return g * per[id(s)] + k

        ident = sb("ident", [P, P])
        ident_b = sb("ident_b", [P, P], bf16)
        block_sum = sb("block_sum", [P, PB])
        block_b = sb("block_b", [P, PB], bf16)
        cos = sb("cos", [P, L])
        sin = sb("sin", [P, L])
        mask1 = sb("mask1", [P, P])
        limit_b = sb("limit_b", [L + 3, 2, HH, LK + 1], bf16)
        place_b = sb("place_b", [L + 3, P], bf16)
        heads = sb("heads", [P, HEADS])
        pick_b = sb("pick_b", [3 * NE, NE, P], bf16)
        tie = sb("tie", [P, NE, NE])
        cwt = sb("cwt", [P, 9])
        cb = sb("cb", [P, 1])
        tapw = sb("tapw", [P, 15])
        wq_s, wk_s = sb("wq_s", [C, C]), sb("wk_s", [C, C])
        bq_s, bqs_s, bk_s = sb("bq_s", [C, 1]), sb("bqs_s", [C, 1]), sb("bk_s", [C, 1])
        gw = sb("gw", [C, NE])
        gb = sb("gb", [P, NE])
        w1h, w1l = sb("w1h", [P, NX, F], bf16), sb("w1l", [P, NX, F], bf16)
        w2h, w2l = sb("w2h", [P, NX, F], bf16), sb("w2l", [P, NX, F], bf16)
        b1_s = sb("b1_s", [P, CH])
        sb2_s, sb2_sum = sb("sb2_s", [C, NS]), sb("sb2_sum", [C, 1])
        rb2_s = sb("rb2_s", [C, NE])
        second = {}
        for name in ("q", "qs", "k", "ks", "v", "kc", "vc", "o"):
            second[name] = sb("second_" + name, [C, C])
        cg = sb("cg", [P, RATIO])
        cg_max, cg_sum, cg_inv = sb("cg_max", [P, 1]), sb("cg_sum", [P, 1]), sb("cg_inv", [P, 1])
        sink_s, sink_sum = sb("sink_s", [P, HEADS]), sb("sink_sum", [P, HEADS])
        sink_rest, sink_part = sb("sink_rest", [P, 2, HEADS]), sb("sink_part", [P, 3, HEADS], bf16)
        part_row = sb("part_row", [P, 3])
        tw1_s, tw2_s = sb("tw1_s", [P, P]), sb("tw2_s", [P, P])
        tb1_s, tb2_s = sb("tb1_s", [P, 1]), sb("tb2_s", [P, P])
        power = sb("power", [P, T])
        euler = sb("euler", [P, T * NE])
        xbuf = [sb(f"xbuf{i}", [P, HW // 2, C]) for i in range(2)]
        blocks = [b[:].rearrange("p (b x) c -> p b x c", x=8) for b in xbuf]
        halves = [b[:].bitcast(bf16).rearrange("p (b x) (h c) -> p b x h c", x=8, h=2) for b in xbuf]
        pooled_s = sb("pooled_s", [P, 3, 3, T, P])
        taps = sb("taps", [C, T, P])
        cols0 = sb("cols0", [C, T, P])
        h0 = [sb(f"h0_{i}", [P, T, C]) for i in range(2)]
        h1 = [sb(f"h1_{i}", [P, T, C]) for i in range(2)]
        x2h = [sb(f"x2h_{i}", [C, N], bf16) for i in range(2)]
        x2l = [sb(f"x2l_{i}", [C, N], bf16) for i in range(2)]
        share_t = [sb(f"share_t{i}", [3 * NE, N], bf16) for i in range(2)]
        mo1, mv1, rs1 = sb("mo1", [P, T, 6]), sb("mv1", [P, T, 2]), sb("rs1", [P, T])
        ve1 = sb("ve1", [P, T])
        mo2, mv2, rs2 = sb("mo2", [P, T, 6]), sb("mv2", [P, T, 2]), sb("rs2", [P, T])
        ve2 = sb("ve2", [P, T])
        x1, x1t = sb("x1", [P, T, C]), sb("x1t", [C, N])
        q1, k1 = sb("q1", [C, N]), sb("k1", [C, N])
        s1 = sb("s1", [P, T, P])
        p1t = q1[:].rearrange("p (t k) -> p t k", t=T)
        nmax1, den1, inv1 = sb("nmax1", [P, T]), sb("den1", [P, T]), sb("inv1", [P, T])
        x2, x2f = k1[:].rearrange("p (t c) -> p t c", t=T), x1t
        lg, lmax, ez = sb("lg", [P, T, NE]), sb("lmax", [P, T]), sb("ez", [P, T, NE])
        esum, einv, prob = sb("esum", [P, T]), sb("einv", [P, T]), sb("prob", [P, T, NE])
        above, equal = [s1[:, 2 * k:2 * k + 2, :].rearrange("p t (a e j) -> p (t a) e j", a=2, e=NE) for k in range(2)]
        rank, share = sb("rank", [P, T, NE]), sb("share", [P, T, NE])
        rest1, rest2 = sb("rest1", [P, T, NE]), sb("rest2", [P, T, NE])
        parts = sb("parts", [P, T, 3, NE], bf16)
        hid = sb("hid", [P, HIDS, F])
        hid_h, hid_l = sb("hid_h", [P, RING, F], bf16), sb("hid_l", [P, RING, F], bf16)
        share_b = sb("share_b", [P, 2, N])
        pick = share_b[0:3 * NE].rearrange("p a (e q) -> p (a e) q", q=P)
        part = sb("part", [C, 2, N])
        moe = sb("moe", [C, N])
        mo3, mv3, rs3 = sb("mo3", [P, T, 6]), sb("mv3", [P, T, 2]), sb("rs3", [P, T])
        ve3 = sb("ve3", [P, T])
        mo4, mv4, rs4 = sb("mo4", [P, T, 6]), sb("mv4", [P, T, 2]), sb("rs4", [P, T])
        ve4 = sb("ve4", [P, T])
        h2 = sb("h2", [P, T, C])
        x3, x3t = sb("x3", [P, T, C]), sb("x3t", [C, N])
        q3 = sb("q3", [C, N])
        keys = sb("keys", [C, GI, LK])
        xc = sb("xc", [C, GI, LC])
        values = sb("values", [LK + 1, GI, HEADS, HD + 1])
        keys_h = sb("keys_h", [C, 2, 2, HEADS, LK])
        roped = keys_h[:, 0].rearrange("p i h k -> p (i h k)")[:, 0:2 * N].rearrange("p (a n) -> p a n", a=2)
        stage = keys_h[:, 0].rearrange("p i h k -> p (i h k)")[0:L + 3]
        limit, place_s = stage[:, 0:HEADS * (LK + 1)], stage[:, HEADS * (LK + 1):HEADS * (LK + 1) + P]
        m3 = sb("m3", [P, 2, HH])
        e3 = sb("e3", [P, 2 * T, HH, LK + 1])
        inv3 = sb("inv3", [P, 2 * T, HH])
        p3t = sb("p3t", [LK + 1, 2, HH, P])
        o3, h3 = x3, sb("h3", [P, T, C])
        o3t = sb("o3t", [C, N])
        h3b, res = h2, h3

        pool_bank = [pb("pool_bank0"), pb("pool_bank1")]
        hid_bank = [pb("hid_bank0"), pb("hid_bank1")]
        down_bank = pb("down_bank")
        att_bank = pb("att_bank")
        sec_bank = [pb("sec_bank0"), pb("sec_bank1")]

        sink_step, block_ready = sem("sink_step"), sem("block_ready")
        early_in, consts_in = sem("early_in"), sem("consts_in")
        weight_in = [sem(f"weight_in{i}") for i in range(STAGING)]
        weight_high, weight_low = sem("weight_high"), sem("weight_low")
        ready_d, ready_a, ready_p = sem("setup_vector"), sem("setup_scalar"), sem("setup_pool")
        x_in = [sem(f"x_in{i}", 16 * T) for i in range(2)]
        x_paired, x_summed = sem("x_paired", 2 * T), sem("x_summed", 4 * T)
        ends_high, ends_low = sem("ends_high", 2 * T), sem("ends_low", 2 * T)
        inner_high, inner_low = sem("inner_high", 2 * T), sem("inner_low", 2 * T)
        pooled = sem("pooled", 4 * T)
        pooled_read = sem("pooled_read", 3 * T)
        tapped = sem("tapped", 32)
        h0_turned, h0_ready = sem("h0_turned"), sem("h0_ready")
        mom1, rstd1, x1_ready = sem("mom1", 10), sem("rstd1"), sem("x1_ready", 4)
        x1_turned, x1t_ready = sem("x1_turned"), sem("x1t_ready")
        q1_done, q1_ready, k1_done, k1_ready = sem("q1_done"), sem("q1_ready"), sem("k1_done"), sem("k1_ready")
        s1_done, s1_masked, s1_max = sem("s1_done"), sem("s1_masked"), sem("s1_max")
        p1_ready, p1_turned, p1t_ready, inv1_ready = sem("p1_ready", 4), sem("p1_turned"), sem("p1t_ready"), sem("inv1_ready")
        o1_done, h1_ready = sem("o1_done"), sem("h1_ready", 4)
        mom2, rstd2, x2_ready = sem("mom2", 10), sem("rstd2"), sem("x2_ready", 4)
        x2_turned, x2_copied, x2l_ready = sem("x2_turned"), sem("x2_copied", 2), sem("x2l_ready")
        gate_done, gate_step, gate_exp = sem("gate_done"), sem("gate_step", 17), sem("gate_exp")
        share_turned, share_ready = sem("share_turned"), sem("share_ready")
        items = CH + NE
        hid_done = sem("hid_done", items)
        hid_made = sem("hid_made", 2 * CH + NE)
        hid_rest, hid_rest_p = sem("hid_rest", CH - CH // POOL_EVERY), sem("hid_rest_p", CH // POOL_EVERY)
        hid_used = sem("hid_used", CH)
        down_read = sem("down_read", 1 + NE)
        moe_added = sem("moe_added", NE)
        moe_turned, h2_ready = sem("moe_turned"), sem("h2_ready")
        mom3, rstd3, x3_ready = sem("mom3", 10), sem("rstd3"), sem("x3_ready", 4)
        x3_turned, x3t_ready = sem("x3_turned"), sem("x3t_ready")
        rope_done, rope_read, rope_added = sem("rope_done", 4), sem("rope_read", 4), sem("rope_added", 2)
        xc_step, kc_done, kc_ready = sem("xc_step", 8), sem("kc_done"), sem("kc_ready")
        v_done, v_ready = sem("v_done", 2), sem("v_ready", 2)
        keys_ready, scored, s3_step = sem("keys_ready", 4), sem("scored", 8), sem("s3_step", 16)
        e3_ready, inv3_ready = sem("e3_ready", 2), sem("inv3_ready", 8)
        p3_turned, p3t_ready = sem("p3_turned", 8), sem("p3t_ready", 8)
        o3_done, o3_ready = sem("o3_done", 8), sem("o3_ready", 8)
        o3_turned, o3t_ready = sem("o3_turned"), sem("o3t_ready")
        wo_done, h3_ready, h3b_ready = sem("wo_done"), sem("h3_ready"), sem("h3b_ready")
        mom4, rstd4, x4_ready = sem("mom4", 10), sem("rstd4"), sem("x4_ready", 4)
        x4_turned, x4t_ready = sem("x4_turned"), sem("x4t_ready")
        up_done, up_ready, mlp_done = sem("up_done"), sem("up_ready"), sem("mlp_done")
        res_ready, res_stored = sem("res_ready"), sem("res_stored", 16)

        def rest_taken(g, q):
            if q % POOL_EVERY == POOL_EVERY - 1:
                return hid_rest_p, at(hid_rest_p, g, q // POOL_EVERY + 1)
            return hid_rest, at(hid_rest, g, q + 1 - q // POOL_EVERY)

        first = [q + max(0, q // FC - NS + 1) for q in range(CH)]
        def made(n):
            shares = sum(1 for r in range(NE) if first[(NS + r) * FC] - 1 < n)
            return 2 * (n - shares) + shares

        def schedule(iteration):
            def run(eng):
                for i in range(LAG_ALL + 1):
                    iteration(i, i)
                with eng.Fori(0, (NG - LAG_ALL - 1) // 2) as j:
                    for k in range(2):
                        iteration(j * 2 + (LAG_ALL + 1 + k), LAG_ALL + 1 + k)
                for i in range(NG, NG + LAG_ALL):
                    iteration(i, i)
            return run

        LAG_ALL = 3
        assert (NG - LAG_ALL - 1) % 2 == 0

        def stages(i, where):
            out = []
            for lag in range(4):
                on = 0 <= where - lag < NG or not isinstance(i, int)
                out.append((i - lag, (where - lag) % 2) if on else (None, 0))
            return out

        def pieces(plan, i, where):
            now, before = stages(i, where), stages(i - 1, where - 1)
            for late, stage, piece in plan:
                if stage == "set":
                    g, b = (0 if where == 1 else None), 0
                else:
                    g, b = (before if late else now)[STAGES.index(stage)]
                if g is not None:
                    yield g, b, stage, piece

        early = [(block_sum, block_c), (cwt, conv_w), (cb, conv_b), (ident, ident_c)]
        loads = [(cos, cos_c), (sin, sin_c), (mask1, mask1_c),
                 (limit, limit_c), (place_s, place_c), (part_row, part_c),
                 (heads, heads_c), (pick, pick_c), (tie, tie_c),
                 (wq_s, wq), (wk_s, wk), (bq_s, bq), (bk_s, bk), (gw, gate_w), (gb, gate_b), (b1_s, b1),
                 (sb2_s, sb2), (rb2_s, rb2), (second["q"], swq), (second["qs"], swqs), (second["k"], swk),
                 (second["ks"], swks), (second["v"], swv), (second["kc"], swkc), (second["vc"], swvc),
                 (second["o"], swo), (cg, comp_gate), (sink_s, sink), (tw1_s, tw1), (tw2_s, tw2),
                 (tb1_s, tb1), (tb2_s, tb2)]
        EARLY, CONSTS = 16 * len(early), 16 * len(loads)
        READY_D, READY_A, READY_P = 22, 6, 4
        lots = [(w1, w1h, w1l, e) for e in range(NX)] + [(w2, w2h, w2l, e) for e in range(NX)]
        staging = [hid[:, 0, :], hid[:, 1, :], part[:, 0, :], part[:, 1, :]]

        block = ctx.enter_context(nc.Block())

        @block.sync
        def _(eng):
            def load(g, u, v):
                src = x[bass.ds(g * GI + 2 * u, 2), :, v * (HW // 2):(v + 1) * (HW // 2), :]
                eng.dma_start(xbuf[v][:], src.rearrange("i y x c -> (i y) x c")).then_inc(x_in[v], 16)

            def iteration(i, where):
                g = stages(i, where)[0][0]
                if g is None:
                    return
                for u in range(T):
                    for v in range(2):
                        if u or after(g, 1):
                            eng.wait_ge(pooled, at(pooled, g, 4 * (u - 1) + 2 * (v + 1)))
                        load(g, u, v)

            schedule(iteration)(eng)

        @block.tensor
        def _(eng):
            def turn_tiles(bank, src, eye):
                for t in range(T):
                    mm = nc.tensor.transpose(bank[:, t * P:(t + 1) * P], src(t), eye)
                return mm

            def tokens(g, b, kind, u=0, k=0):
                if kind == "pool":
                    v = k // 2
                    m = 3 * u + (0, 1, 1, 2)[k]
                    bank = pool_bank[m % 2]
                    if k in (0, 2):
                        eng.wait_ge(ends_low, at(ends_low, g, 2 * u + v + 1))
                    if k in (0, 3):
                        eng.wait_ge(inner_low, at(inner_low, g, 2 * u + v + 1))
                    if k != 2:
                        if m >= 2:
                            eng.wait_ge(pooled_read, at(pooled_read, g, m - 1))
                        elif after(g, 1):
                            if m == 0:
                                eng.wait_ge(h0_ready, at(h0_ready, g - 1, 1))
                            else:
                                eng.wait_ge(pooled_read, at(pooled_read, g, 0))
                    if k in (0, 3):
                        view = bank[:, 0:BX * PB].rearrange("p (k d n) -> p k d n", k=2, d=3)
                        views = [(0, view[:, 0]), (1, view[:, 1])]
                    else:
                        view = bank[:, 0:BX * PB].rearrange("p (d v n) -> p d v n", v=2, d=3)
                        views = [(2, view[:, :, v, :])]
                    for kx, cols in views:
                        for bx in range(BX // 2):
                            for h in range(2):
                                mm = nc.tensor.matmul(cols[:, :, bx * 2 * BX:(bx + 1) * 2 * BX],
                                                      halves[v][:, bx, KIND_X[kx], h, :],
                                                      block_b[:], start=h == 0, stop=h == 1)
                    mm.then_inc(pooled, 1)
                elif kind == "out":
                    eng.wait_ge(tapped, at(tapped, g, 32))
                    eng.wait_ge(pooled_read, at(pooled_read, g, 3 * T))
                    turn_tiles(pool_bank[0], lambda t: cols0[:, t, :], ident[:]).then_inc(h0_turned, 1)

            def attention(g, b, n):
                bank = att_bank
                if n == 1:
                    eng.wait_ge(x1_ready, at(x1_ready, g, 4))
                    if after(g, 1):
                        eng.wait_ge(share_ready, at(share_ready, g - 1, 1))
                    turn_tiles(bank, lambda t: x1[:, t, :], ident[:]).then_inc(x1_turned, 1)
                elif n == 2:
                    eng.wait_ge(x1t_ready, at(x1t_ready, g, 1))
                    nc.tensor.matmul(bank[:], wq_s[:], x1t[:], start=True, stop=True).then_inc(q1_done, 1)
                elif n == 3:
                    eng.wait_ge(q1_ready, at(q1_ready, g, 1))
                    nc.tensor.matmul(bank[:], wk_s[:], x1t[:], start=True, stop=True).then_inc(k1_done, 1)
                elif n == 4:
                    eng.wait_ge(k1_ready, at(k1_ready, g, 1))
                    for t in range(T):
                        mm = nc.tensor.matmul(bank[:, t * P:(t + 1) * P], q1[:, t * P:(t + 1) * P],
                                              k1[:, t * P:(t + 1) * P], start=True, stop=True)
                    mm.then_inc(s1_done, 1)
                elif n == 7:
                    eng.wait_ge(p1_ready, at(p1_ready, g, 4))
                    turn_tiles(bank, lambda t: s1[:, t, :], ident[:]).then_inc(p1_turned, 1)
                elif n == 8:
                    eng.wait_ge(p1t_ready, at(p1t_ready, g, 1))
                    for t in range(T):
                        mm = nc.tensor.matmul(bank[:, t * P:(t + 1) * P], p1t[:, t, :], x1[:, t, :],
                                              start=True, stop=True)
                    mm.then_inc(o1_done, 1)
                elif n == 10:
                    eng.wait_ge(x2_ready, at(x2_ready, g, 4))
                    turn_tiles(bank, lambda t: x2[:, t, :], ident[:]).then_inc(x2_turned, 1)
                elif n == 11:
                    eng.wait_ge(x2_copied, at(x2_copied, g, 2))
                    for t in range(T):
                        mm = nc.tensor.matmul(bank[:, t * NE:(t + 1) * NE], x2f[:, t * P:(t + 1) * P], gw[:],
                                              start=True, stop=True)
                    mm.then_inc(gate_done, 1)
                elif n == 13:
                    eng.wait_ge(gate_step, at(gate_step, g, 17))
                    bank_b = bank[0:3 * NE, 0:N // 2].bitcast(bf16)
                    for t in range(T):
                        mm = nc.tensor.transpose(bank_b[:, t * P:(t + 1) * P],
                                                 parts[:, t, :, :].rearrange("p a e -> p (a e)"), ident_b[:])
                    mm.then_inc(share_turned, 1)

            def up(g, b, q):
                e, n = q // FC, first[q]
                def bank_free(n):
                    if n >= 2:
                        eng.wait_ge(hid_made, at(hid_made, g, made(n - 1)))
                    elif after(g, 1):
                        eng.wait_ge(hid_made, at(hid_made, g - 1, made(items + n - 1)))
                if q == 0:
                    eng.wait_ge(x2l_ready, at(x2l_ready, g, 1))
                    eng.wait_ge(share_ready, at(share_ready, g, 1))
                if q % FC == 0 and e >= NS:
                    bank_free(n - 1)
                    nc.tensor.matmul(hid_bank[(n - 1) % 2][:], pick_b[:, e - NS, :], share_t[b][:],
                                     start=True, stop=True).then_inc(hid_done, 1)
                bank_free(n)
                cols = slice((q % FC) * P, (q % FC + 1) * P)
                bank = hid_bank[n % 2]
                nc.tensor.matmul(bank[:], w1h[:, e, cols], x2h[b][:], start=True, stop=False)
                nc.tensor.matmul(bank[:], w1l[:, e, cols], x2h[b][:], start=False, stop=False)
                nc.tensor.matmul(bank[:], w1h[:, e, cols], x2l[b][:], start=False, stop=True).then_inc(hid_done, 1)

            def down(g, q):
                e, r = q // FC, q % RING
                cols = slice((q % FC) * P, (q % FC + 1) * P)
                begin = q == 0 or (q % FC == 0 and e >= NS)
                end = q % FC == FC - 1 and e >= NS - 1
                eng.wait_ge(*rest_taken(g, q))
                if begin and q:
                    eng.wait_ge(down_read, at(down_read, g, e - NS + 1))
                elif begin and after(g, 1):
                    eng.wait_ge(down_read, at(down_read, g - 1, 1 + NE))
                nc.tensor.matmul(down_bank[:], w2h[:, e, cols], hid_h[:, r, :], start=begin, stop=False)
                nc.tensor.matmul(down_bank[:], w2l[:, e, cols], hid_h[:, r, :], start=False, stop=False)
                nc.tensor.matmul(down_bank[:], w2h[:, e, cols], hid_l[:, r, :], start=False, stop=end) \
                  .then_inc(hid_used, 1)

            def layer2(g, b, kind, n=0):
                b0, b1 = sec_bank
                if kind == "pre" and n == 0:
                    eng.wait_ge(moe_added, at(moe_added, g, NE))
                    if after(g, 1):
                        eng.wait_ge(res_ready, at(res_ready, g - 1, 1))
                    turn_tiles(b0, lambda t: moe[:, t * P:(t + 1) * P], ident[:]).then_inc(moe_turned, 1)
                elif kind == "pre" and n == 2:
                    eng.wait_ge(x3_ready, at(x3_ready, g, 4))
                    if after(g, 1):
                        eng.wait_ge(up_ready, at(up_ready, g - 1, 1))
                    turn_tiles(b1, lambda t: x3[:, t, :], ident[:]).then_inc(x3_turned, 1)
                elif kind == "pre" and n in (3, 4):
                    names = ("q", "qs") if n == 3 else ("k", "ks")
                    eng.wait_ge(x3t_ready, at(x3t_ready, g, 1))
                    for k, name in enumerate(names):
                        if n == 4:
                            eng.wait_ge(rope_read, at(rope_read, g, k + 1))
                        nc.tensor.matmul(sec_bank[k][:], second[name][:], x3t[:], start=True, stop=True) \
                          .then_inc(rope_done, 1)
                elif kind == "pre" and n == 5:
                    eng.wait_ge(xc_step, at(xc_step, g, 8))
                    eng.wait_ge(rope_read, at(rope_read, g, 3))
                    nc.tensor.matmul(b0[:, 0:GI * LC], second["kc"][:], xc[:].rearrange("p i w -> p (i w)"),
                                     start=True, stop=True).then_inc(kc_done, 1)
                elif kind == "pre" and n in (6, 7):
                    half = n - 6
                    bank = sec_bank[1 - half]
                    if half == 0:
                        eng.wait_ge(rope_read, at(rope_read, g, 4))
                    else:
                        eng.wait_ge(kc_ready, at(kc_ready, g, 1))
                    for m in range(4):
                        im = 4 * half + m
                        nc.tensor.matmul(bank[0:L, m * C:(m + 1) * C], x3t[:, im * L:(im + 1) * L], second["v"][:],
                                         start=True, stop=True)
                        mm = nc.tensor.matmul(bank[L:LK, m * C:(m + 1) * C], xc[:, im, :], second["vc"][:],
                                              start=True, stop=True)
                    mm.then_inc(v_done, 1)
                elif kind == "score":
                    t, half = n // 2, n % 2
                    bank = sec_bank[half]
                    if n == 0:
                        eng.wait_ge(rope_added, at(rope_added, g, 2))
                        eng.wait_ge(v_ready, at(v_ready, g, 2))
                    if half == 0:
                        eng.wait_ge(keys_ready, at(keys_ready, g, t + 1))
                    if n >= 2:
                        eng.wait_ge(s3_step, at(s3_step, g, 2 * (n - 2) + 2))
                    wide = bank[:, 0:HH * (LK + 1)]
                    nc.tensor.matmul(wide, place_b[:], limit_b[:, half].rearrange("p h k -> p (h k)"),
                                     start=True, stop=False)
                    for im in range(2):
                        tok = (2 * t + im) * L
                        mm = nc.tensor.matmul(
                            wide[im * L:(im + 1) * L].rearrange("p (h k) -> p h k", h=HH)[:, :, 0:LK],
                            q3[:, tok:tok + L], keys_h[:, t % 2, im, half * HH:(half + 1) * HH, :],
                            start=False, stop=True)
                    mm.then_inc(scored, 1)
                elif kind == "turn":
                    if n == 0:
                        eng.wait_ge(e3_ready, at(e3_ready, g, 2))
                    if n >= 1:
                        eng.wait_ge(p3t_ready, at(p3t_ready, g, n))
                    for h in range(HH):
                        mm = nc.tensor.transpose(b0[0:LK + 1, h * P:(h + 1) * P], e3[:, n, h, :], ident[:])
                    mm.then_inc(p3_turned, 1)
                elif kind == "value":
                    t, half = n // 2, n % 2
                    eng.wait_ge(p3t_ready, at(p3t_ready, g, n + 1))
                    if n >= 1:
                        eng.wait_ge(o3_ready, at(o3_ready, g, n))
                    for h in range(HH):
                        for im in range(2):
                            mm = nc.tensor.matmul(b1[im * L:(im + 1) * L, h * (HD + 1):(h + 1) * (HD + 1)],
                                                  p3t[:, half, h, im * L:(im + 1) * L],
                                                  values[:, 2 * t + im, half * HH + h, :], start=True, stop=True)
                    mm.then_inc(o3_done, 1)
                elif kind == "post" and n == 0:
                    eng.wait_ge(o3_ready, at(o3_ready, g, 8))
                    turn_tiles(b0, lambda t: o3[:, t, :], ident[:]).then_inc(o3_turned, 1)
                elif kind == "post" and n == 1:
                    eng.wait_ge(o3t_ready, at(o3t_ready, g, 1))
                    for t in range(T):
                        mm = nc.tensor.matmul(b1[:, t * P:(t + 1) * P], o3t[:, t * P:(t + 1) * P], second["o"][:],
                                              start=True, stop=True)
                    mm.then_inc(wo_done, 1)
                elif kind == "post" and n == 3:
                    eng.wait_ge(x4_ready, at(x4_ready, g, 4))
                    turn_tiles(b0, lambda t: x3[:, t, :], ident[:]).then_inc(x4_turned, 1)
                elif kind == "post" and n == 4:
                    eng.wait_ge(x4t_ready, at(x4t_ready, g, 1))
                    nc.tensor.matmul(b1[:], tw1_s[:], x3t[:], start=True, stop=True).then_inc(up_done, 1)
                elif kind == "post" and n == 5:
                    eng.wait_ge(up_ready, at(up_ready, g, 1))
                    for t in range(T):
                        mm = nc.tensor.matmul(b0[:, t * P:(t + 1) * P], o3t[:, t * P:(t + 1) * P], tw2_s[:],
                                              start=True, stop=True)
                    mm.then_inc(mlp_done, 1)

            def experts(g, b, kind, q):
                if kind == "up":
                    up(g, b, q)
                else:
                    down(g, q)

            eng.wait_ge(early_in, EARLY)
            eng.wait_ge(block_ready, 1)

            def iteration(i, where):
                if where == 1:
                    eng.wait_ge(consts_in, CONSTS)
                    eng.wait_ge(ready_d, READY_D)
                    eng.wait_ge(sink_step, 9)
                    eng.wait_ge(ready_a, READY_A)
                    eng.wait_ge(ready_p, READY_P)
                for g, b, stage, piece in pieces(PLAN["pe"], i, where):
                    if where == 2 and piece == ("up", 0):
                        eng.wait_ge(weight_low, len(lots))
                    {"tok": tokens, "att": attention, "ffn": experts, "sec": layer2}[stage](g, b, *piece)

            schedule(iteration)(eng)

        @block.scalar
        def _(eng):
            for dst, src in early:
                eng.dma_start(dst[:], src).then_inc(early_in, 16)
            for dst, src in loads:
                eng.dma_start(dst if dst in (pick, limit, place_s) else dst[:], src).then_inc(consts_in, 16)

            def setup():
                eng.wait_ge(consts_in, CONSTS)
                eng.wait_ge(early_in, EARLY)
                nc.scalar.activation(pick_b[:], pick, ACT.Copy).then_inc(ready_a, 1)
                nc.scalar.activation(ident_b[:], ident[:], ACT.Copy).then_inc(ready_a, 1)
                nc.scalar.activation(limit_b[:].rearrange("p a h k -> p (a h k)"), limit, ACT.Copy).then_inc(ready_a, 1)
                nc.scalar.activation(place_b[:], place_s, ACT.Copy).then_inc(ready_a, 1)
                nc.scalar.mul(bqs_s[:], bq_s[:], float(C) ** -0.5).then_inc(ready_a, 1)
                eng.wait_ge(ready_d, READY_D - 2)
                nc.scalar.activation(cg[:], cg[:], ACT.Exp, bias=cg_max[:], accum_out=cg_sum[:]).then_inc(ready_a, 1)
                eng.wait_ge(ready_a, READY_A)

            def weights(g, b, kind, n):
                _, high, _, e = lots[n]
                eng.wait_ge(weight_in[n % STAGING], 16 * (n // STAGING + 1))
                nc.scalar.activation(high[:, e, :], staging[n % STAGING], ACT.Copy).then_inc(weight_high, 1)

            def tokens(g, b, kind, u=0, k=0):
                if kind == "ends":
                    eng.wait_ge(x_paired, at(x_paired, g, 2 * u + k + 1))
                    nc.scalar.activation(halves[k][:, :, 2:7:4, 0, :], blocks[k][:, :, 0:8:7, :], ACT.Copy) \
                      .then_inc(ends_high, 1)
                elif kind == "inner":
                    eng.wait_ge(x_summed, at(x_summed, g, 4 * u + 2 * k + 2))
                    nc.scalar.activation(halves[k][:, :, 4, 0, :], blocks[k][:, :, 1, :], ACT.Copy) \
                      .then_inc(inner_high, 1)
                elif kind == "pool" and k != 1:
                    m = (0, None, 1, 2)[k]
                    eng.wait_ge(pooled, at(pooled, g, 4 * u + k + 1))
                    if after(g, 1):
                        eng.wait_ge(tapped, at(tapped, g - 1, 16 * (u // 2 + 1)))
                    side = P // 2
                    if m == 1:
                        dst = pooled_s[:, 2, :, u, :]
                    else:
                        dst = pooled_s[:, 0:2, :, u, (m // 2) * side:(m // 2 + 1) * side].rearrange("p k d n -> p (k d) n")
                    src = pool_bank[(3 * u + m) % 2][:, 0:BX * PB].rearrange("p (r n) -> p r n", r=3 if m == 1 else 6)
                    nc.scalar.activation(dst, src, ACT.Copy).then_inc(pooled_read, 1)
                elif kind == "out":
                    eng.wait_ge(h0_turned, at(h0_turned, g, 1))
                    nc.scalar.activation(h0[b][:].rearrange("p t c -> p (t c)"), pool_bank[0][:], ACT.Copy) \
                      .then_inc(h0_ready, 1)

            def attention(g, b, n):
                bank = att_bank
                if n == 1:
                    eng.wait_ge(x1_turned, at(x1_turned, g, 1))
                    nc.scalar.activation(x1t[:], bank[:], ACT.Copy).then_inc(x1t_ready, 1)
                elif n == 2:
                    eng.wait_ge(q1_done, at(q1_done, g, 1))
                    nc.scalar.activation(q1[:], bank[:], ACT.Identity, bias=bqs_s[:], scale=float(C) ** -0.5) \
                      .then_inc(q1_ready, 1)
                elif n == 3:
                    eng.wait_ge(k1_done, at(k1_done, g, 1))
                    nc.scalar.activation(k1[:], bank[:], ACT.Identity, bias=bk_s[:]).then_inc(k1_ready, 1)
                elif n == 6:
                    eng.wait_ge(s1_max, at(s1_max, g, 1))
                    for t in range(T):
                        nc.scalar.activation(s1[:, t, :], s1[:, t, :], ACT.Exp, bias=nmax1[:, t:t + 1],
                                             accum_out=den1[:, t:t + 1]).then_inc(p1_ready, 1)
                elif n == 7:
                    eng.wait_ge(p1_turned, at(p1_turned, g, 1))
                    nc.scalar.activation(q1[:], bank[:], ACT.Copy) \
                      .then_inc(p1t_ready, 1)
                elif n == 10:
                    eng.wait_ge(x2_turned, at(x2_turned, g, 1))
                    nc.scalar.activation(x2h[b][:], bank[:], ACT.Copy).then_inc(x2_copied, 1)
                    nc.scalar.activation(x2f[:], bank[:], ACT.Copy).then_inc(x2_copied, 1)
                elif n == 13:
                    eng.wait_ge(share_turned, at(share_turned, g, 1))
                    nc.scalar.activation(share_t[b][:], bank[0:3 * NE, 0:N // 2].bitcast(bf16), ACT.Copy) \
                      .then_inc(share_ready, 1)

            def experts(g, b, kind, q):
                e, n = q // FC, first[q]
                if q % FC == 0 and e >= NS:
                    k = e - NS
                    eng.wait_ge(hid_done, at(hid_done, g, n))
                    if k >= 2:
                        eng.wait_ge(down_read, at(down_read, g, k))
                    elif after(g, 1):
                        eng.wait_ge(down_read, at(down_read, g - 1, k + NE))
                    nc.scalar.activation(share_b[:, k % 2, :], hid_bank[(n - 1) % 2][:], ACT.Copy).then_inc(hid_made, 1)
                eng.wait_ge(hid_done, at(hid_done, g, n + 1))
                if q >= RING:
                    eng.wait_ge(hid_used, at(hid_used, g, q - RING + 1))
                elif after(g, 1):
                    eng.wait_ge(hid_used, at(hid_used, g - 1, CH + q - RING + 1))
                if q >= HIDS:
                    eng.wait_ge(*rest_taken(g, q - HIDS))
                elif after(g, 1):
                    eng.wait_ge(*rest_taken(g - 1, CH + q - HIDS))
                for dst, r in ((hid_h, q % RING), (hid, q % HIDS)):
                    nc.scalar.activation(dst[:, r, :], hid_bank[n % 2][:], ACT.Gelu, bias=b1_s[:, q:q + 1]) \
                      .then_inc(hid_made, 1)

            def layer2(g, b, kind, n=0):
                b0, b1 = sec_bank
                if kind == "pre" and n == 2:
                    eng.wait_ge(x3_turned, at(x3_turned, g, 1))
                    nc.scalar.activation(x3t[:], b1[:], ACT.Copy).then_inc(x3t_ready, 1)
                elif kind == "pre" and n == 5:
                    eng.wait_ge(kc_done, at(kc_done, g, 1))
                    if after(g, 1):
                        eng.wait_ge(keys_ready, at(keys_ready, g - 1, 4))
                    nc.scalar.activation(keys[:, :, L:LK], b0[:, 0:GI * LC].rearrange("p (i w) -> p i w", i=GI),
                                         ACT.Copy).then_inc(kc_ready, 1)
                elif kind == "pre" and n in (6, 7):
                    half = n - 6
                    eng.wait_ge(v_done, at(v_done, g, half + 1))
                    nc.scalar.activation(values[0:LK, 4 * half:4 * half + 4, :, 0:HD].rearrange("p i h d -> p (i h) d"),
                                         sec_bank[1 - half][0:LK, :].rearrange("p (m d) -> p m d", d=HD), ACT.Copy).then_inc(v_ready, 1)
                elif kind == "exp":
                    for half in range(2):
                        eng.wait_ge(s3_step, at(s3_step, g, 8 * (half + 1)))
                        view = e3[:, T * half:T * half + T].rearrange("p n h k -> p (n h k)")
                        nc.scalar.activation(view, view, ACT.Exp, scale=float(HD) ** -0.5).then_inc(e3_ready, 1)
                elif kind == "turn":
                    eng.wait_ge(p3_turned, at(p3_turned, g, n + 1))
                    if n >= 2:
                        eng.wait_ge(o3_done, at(o3_done, g, n - 1))
                    nc.scalar.activation(p3t[:, n % 2].rearrange("p h q -> p (h q)"), b0[0:LK + 1, :], ACT.Copy) \
                      .then_inc(p3t_ready, 1)
                elif kind == "post" and n == 0:
                    eng.wait_ge(o3_turned, at(o3_turned, g, 1))
                    nc.scalar.activation(o3t[:], b0[:], ACT.Copy).then_inc(o3t_ready, 1)
                elif kind == "post" and n == 3:
                    eng.wait_ge(x4_turned, at(x4_turned, g, 1))
                    nc.scalar.activation(x3t[:], b0[:], ACT.Copy).then_inc(x4t_ready, 1)
                elif kind == "post" and n == 4:
                    eng.wait_ge(up_done, at(up_done, g, 1))
                    nc.scalar.activation(o3t[:], b1[:], ACT.Gelu, bias=tb1_s[:]).then_inc(up_ready, 1)
                elif kind == "post" and n == 5:
                    eng.wait_ge(res_ready, at(res_ready, g, 1))
                    eng.dma_start(out[bass.ds(g * GI, GI)].rearrange("(t i) l c -> (i l) t c", t=T), res[:]) \
                       .then_inc(res_stored, 16)

            def iteration(i, where):
                if where == 1:
                    setup()
                for g, b, stage, piece in pieces(PLAN["act"], i, where):
                    {"tok": tokens, "att": attention, "ffn": experts, "sec": layer2, "set": weights}[stage](g, b, *piece)

            schedule(iteration)(eng)
            eng.wait_ge(res_stored, at(res_stored, NG, 0))

        @block.vector
        def _(eng):
            step = [0]

            def done(ins):
                ins.then_inc(ready_d, 1)
                step[0] += 1

            done(nc.vector.memset(power[:], -0.5))
            done(nc.vector.memset(euler[:], 2.718281828459045))
            eng.wait_ge(early_in, EARLY)
            nc.vector.tensor_copy(block_b[:], block_sum[:]).then_inc(block_ready, 1)
            done(nc.vector.tensor_scalar(cwt[:], cwt[:], 1.0 / (BX * BX), None, ALU.mult))
            eng.wait_ge(ready_d, step[0])
            for dy in range(3):
                w = [cwt[:, 3 * dy + k:3 * dy + k + 1] for k in range(3)]
                t5 = [tapw[:, 5 * dy + k:5 * dy + k + 1] for k in range(5)]
                done(nc.vector.tensor_tensor(t5[1], w[0], w[1], ALU.add))
                done(nc.vector.tensor_tensor(t5[3], w[1], w[2], ALU.add))
                done(nc.vector.tensor_copy(t5[2], w[2]))
                done(nc.vector.tensor_copy(t5[4], w[0]))
                eng.wait_ge(ready_d, step[0])
                done(nc.vector.tensor_tensor(t5[0], t5[1], w[2], ALU.add))
            eng.wait_ge(ready_d, step[0])

            def setup():
                eng.wait_ge(consts_in, CONSTS)
                done(nc.vector.tensor_tensor(sb2_sum[:], sb2_s[:, 0:1], sb2_s[:, 1:2], ALU.add))
                done(nc.vector.tensor_reduce(cg_max[:], cg[:], AX.X, ALU.max, negate=True))
                assert step[0] == READY_D - 2
                rows, steps = slice(L, L + 3), [0]

                def sink_done(ins):
                    ins.then_inc(sink_step, 1)
                    steps[0] += 1
                    eng.wait_ge(sink_step, steps[0])

                sink_done(nc.vector.tensor_scalar(sink_s[rows, :], sink_s[rows, :], float(HD) ** 0.5, None, ALU.mult))
                sink_done(nc.vector.tensor_copy(sink_part[rows, 0, :], sink_s[rows, :]))
                sink_done(nc.vector.tensor_tensor(sink_rest[rows, 0, :], sink_s[rows, :], sink_part[rows, 0, :],
                                                  ALU.subtract))
                sink_done(nc.vector.tensor_copy(sink_part[rows, 1, :], sink_rest[rows, 0, :]))
                sink_done(nc.vector.tensor_tensor(sink_rest[rows, 1, :], sink_rest[rows, 0, :], sink_part[rows, 1, :],
                                                  ALU.subtract))
                sink_done(nc.vector.tensor_copy(sink_part[rows, 2, :], sink_rest[rows, 1, :]))
                sink_done(nc.vector.tensor_scalar(sink_sum[rows, :], sink_part[rows, 0, :], part_row[rows, 0:1], None,
                                                  ALU.mult))
                sink_done(nc.vector.scalar_tensor_tensor(sink_sum[rows, :], sink_part[rows, 1, :], part_row[rows, 1:2],
                                                         sink_sum[rows, :], ALU.mult, ALU.add))
                eng.wait_ge(ready_a, READY_A)
                sink_done(nc.vector.scalar_tensor_tensor(
                    limit_b[rows, :, :, LK], sink_part[rows, 2, :].rearrange("p (a h) -> p a h", a=2),
                    part_row[rows, 2:3], sink_sum[rows, :].rearrange("p (a h) -> p a h", a=2), ALU.mult, ALU.add))
                done(nc.vector.reciprocal(cg_inv[:], cg_sum[:]))
                eng.wait_ge(ready_d, step[0])
                done(nc.vector.tensor_scalar(cg[:], cg[:], cg_inv[:], None, ALU.mult))
                eng.wait_ge(ready_d, step[0])

            def weights(g, b, kind, n):
                _, high, low, e = lots[n]
                eng.wait_ge(weight_high, n + 1)
                nc.vector.tensor_tensor(low[:, e, :], staging[n % STAGING], high[:, e, :], ALU.subtract) \
                  .then_inc(weight_low, 1)

            def moments(g, src, ready, need, mo, mv, ve, mom):
                eng.wait_ge(ready, at(ready, g, need))
                for t in range(T):
                    nc.vector.bn_stats(mo[:, t, :], src[:, t, :]).then_inc(mom, 1)
                eng.wait_ge(mom, at(mom, g, T))
                nc.vector.memset(ve[:], EPS).then_inc(mom, 1)
                for t in range(T):
                    nc.vector.bn_aggr(mv[:, t, :], mo[:, t, :]).then_inc(mom, 1)
                eng.wait_ge(mom, at(mom, g, 2 * T + 1))
                nc.vector.tensor_tensor(ve[:], ve[:], mv[:, :, 1], ALU.add).then_inc(mom, 1)

            def normalise(g, dst, src, mv, rs, rstd, ready):
                eng.wait_ge(rstd, at(rstd, g, 1))
                for t in range(T):
                    nc.vector.tensor_scalar(dst[:, t, :], src[:, t, :], mv[:, t, 0:1], rs[:, t:t + 1],
                                            ALU.subtract, ALU.mult).then_inc(ready, 1)

            def tokens(g, b, kind, u=0, k=0):
                if kind == "pair":
                    v = blocks[k]
                    eng.wait_ge(x_in[k], at(x_in[k], g, 16 * (u + 1)))
                    nc.vector.tensor_tensor(v[:, :, 1:6:2, :], v[:, :, 1:6:2, :], v[:, :, 2:7:2, :], ALU.add) \
                      .then_inc(x_paired, 1)
                elif kind == "inner":
                    eng.wait_ge(inner_high, at(inner_high, g, 2 * u + k + 1))
                    nc.vector.tensor_tensor(halves[k][:, :, 4, 1, :], blocks[k][:, :, 1, :], halves[k][:, :, 4, 0, :],
                                            ALU.subtract).then_inc(inner_low, 1)
                elif kind == "tap":
                    pair, n = u, k
                    dy, term = n // 5, (0, 2, 4, 3, 1)[n % 5]
                    src_kind = (0, 1, 1, 2, 2)[term]
                    shift = (0, 0, 1, 0, -1)[term]
                    lo, hi = max(0, -shift), BX - max(0, shift)
                    m, tiles = 2 * BX, slice(2 * pair, 2 * pair + 2)
                    src = pooled_s[:, src_kind, dy, tiles, (lo + shift) * m:(hi + shift) * m]
                    dst = taps[:, tiles, lo * m:hi * m]
                    w = tapw[:, 5 * dy + term:5 * dy + term + 1]
                    if n == 0:
                        eng.wait_ge(pooled_read, at(pooled_read, g, 6 * (pair + 1)))
                        nc.vector.tensor_scalar(dst, src, w, cb[:], ALU.mult, ALU.add).then_inc(tapped, 1)
                    elif n < 14:
                        eng.wait_ge(tapped, at(tapped, g, 16 * pair + n))
                        nc.vector.scalar_tensor_tensor(dst, src, w, dst, ALU.mult, ALU.add).then_inc(tapped, 1)
                    else:
                        eng.wait_ge(tapped, at(tapped, g, 16 * pair + n))
                        if after(g, 1):
                            eng.wait_ge(h0_turned, at(h0_turned, g - 1, 1))
                        for t in (2 * pair, 2 * pair + 1):
                            nc.vector.scalar_tensor_tensor(
                                cols0[:, t, :].rearrange("p (m b) -> p b m", b=BX),
                                pooled_s[:, src_kind, dy, t, :].rearrange("p (b m) -> p b m", b=BX), w,
                                taps[:, t, :].rearrange("p (b m) -> p b m", b=BX), ALU.mult, ALU.add) \
                              .then_inc(tapped, 1)

            def attention(g, b, n):
                bank = att_bank
                tiles = bank[:].rearrange("p (t k) -> p t k", t=T)
                if n == 0:
                    moments(g, h0[b], h0_ready, 1, mo1, mv1, ve1, mom1)
                elif n == 1:
                    normalise(g, x1, h0[b], mv1, rs1, rstd1, x1_ready)
                elif n == 4:
                    eng.wait_ge(s1_done, at(s1_done, g, 1))
                    nc.vector.tensor_tensor(s1[:], tiles, mask1[:].unsqueeze(1).to_broadcast([P, T, P]), ALU.add) \
                      .then_inc(s1_masked, 1)
                elif n == 5:
                    eng.wait_ge(s1_masked, at(s1_masked, g, 1))
                    nc.vector.tensor_reduce(nmax1[:], s1[:], AX.X, ALU.max, negate=True).then_inc(s1_max, 1)
                elif n == 7:
                    eng.wait_ge(p1_ready, at(p1_ready, g, 4))
                    nc.vector.reciprocal(inv1[:], den1[:]).then_inc(inv1_ready, 1)
                elif n == 8:
                    eng.wait_ge(o1_done, at(o1_done, g, 1))
                    eng.wait_ge(inv1_ready, at(inv1_ready, g, 1))
                    for t in range(T):
                        nc.vector.scalar_tensor_tensor(h1[b][:, t, :], tiles[:, t, :], inv1[:, t:t + 1],
                                                       h0[b][:, t, :], ALU.mult, ALU.add).then_inc(h1_ready, 1)
                elif n == 9:
                    moments(g, h1[b], h1_ready, 4, mo2, mv2, ve2, mom2)
                elif n == 10:
                    normalise(g, x2, h1[b], mv2, rs2, rstd2, x2_ready)
                elif n == "low":
                    eng.wait_ge(x2_copied, at(x2_copied, g, 2))
                    nc.vector.tensor_tensor(x2l[b][:], x2f[:], x2h[b][:], ALU.subtract).then_inc(x2l_ready, 1)
                elif n == 11:
                    eng.wait_ge(gate_done, at(gate_done, g, 1))
                    nc.vector.tensor_tensor(lg[:], bank[:, 0:T * NE].rearrange("p (t e) -> p t e", t=T),
                                            gb[:].unsqueeze(1).to_broadcast([P, T, NE]), ALU.add).then_inc(gate_step, 1)
                    eng.wait_ge(gate_step, at(gate_step, g, 1))
                    nc.vector.tensor_reduce(lmax[:], lg[:], AX.X, ALU.max).then_inc(gate_step, 1)
                    eng.wait_ge(gate_step, at(gate_step, g, 2))
                    nc.vector.tensor_tensor(lg[:], lg[:], lmax[:].unsqueeze(2).to_broadcast([P, T, NE]),
                                            ALU.subtract).then_inc(gate_step, 1)
                elif n == 12:
                    four = [P, T, NE, NE]
                    eng.wait_ge(gate_exp, at(gate_exp, g, 1))
                    nc.vector.tensor_reduce(esum[:], ez[:], AX.X, ALU.add).then_inc(gate_step, 1)
                    eng.wait_ge(gate_step, at(gate_step, g, 4))
                    nc.vector.reciprocal(einv[:], esum[:]).then_inc(gate_step, 1)
                    eng.wait_ge(gate_step, at(gate_step, g, 5))
                    nc.vector.tensor_tensor(prob[:], ez[:], einv[:].unsqueeze(2).to_broadcast([P, T, NE]),
                                            ALU.mult).then_inc(gate_step, 1)
                    eng.wait_ge(gate_step, at(gate_step, g, 6))
                    pe_, pj = prob[:].unsqueeze(3).to_broadcast(four), prob[:].unsqueeze(2).to_broadcast(four)
                    nc.vector.tensor_tensor(above, pj, pe_, ALU.is_gt).then_inc(gate_step, 1)
                    nc.vector.tensor_tensor(equal, pj, pe_, ALU.is_equal).then_inc(gate_step, 1)
                    eng.wait_ge(gate_step, at(gate_step, g, 8))
                    nc.vector.tensor_tensor(equal, equal, tie[:].unsqueeze(1).to_broadcast(four),
                                            ALU.mult).then_inc(gate_step, 1)
                    eng.wait_ge(gate_step, at(gate_step, g, 9))
                    nc.vector.tensor_tensor(above, above, equal, ALU.add).then_inc(gate_step, 1)
                    eng.wait_ge(gate_step, at(gate_step, g, 10))
                    nc.vector.tensor_reduce(rank[:], above, AX.X, ALU.add).then_inc(gate_step, 1)
                    eng.wait_ge(gate_step, at(gate_step, g, 11))
                    nc.vector.scalar_tensor_tensor(share[:], rank[:], 1.5, prob[:], ALU.is_lt, ALU.mult) \
                      .then_inc(gate_step, 1)
                    eng.wait_ge(gate_step, at(gate_step, g, 12))
                    nc.vector.tensor_copy(parts[:, :, 0, :], share[:]).then_inc(gate_step, 1)
                    eng.wait_ge(gate_step, at(gate_step, g, 13))
                    nc.vector.tensor_tensor(rest1[:], share[:], parts[:, :, 0, :], ALU.subtract).then_inc(gate_step, 1)
                    eng.wait_ge(gate_step, at(gate_step, g, 14))
                    nc.vector.tensor_copy(parts[:, :, 1, :], rest1[:]).then_inc(gate_step, 1)
                    eng.wait_ge(gate_step, at(gate_step, g, 15))
                    nc.vector.tensor_tensor(rest2[:], rest1[:], parts[:, :, 1, :], ALU.subtract).then_inc(gate_step, 1)
                    eng.wait_ge(gate_step, at(gate_step, g, 16))
                    nc.vector.tensor_copy(parts[:, :, 2, :], rest2[:]).then_inc(gate_step, 1)

            def hidden(g, q):
                eng.wait_ge(hid_made, at(hid_made, g, made(first[q] + 1)))
                nc.vector.tensor_tensor(hid_l[:, q % RING, :], hid[:, q % HIDS, :], hid_h[:, q % RING, :],
                                        ALU.subtract).then_inc(hid_rest, 1)

            def expert_sum(g, q):
                e = q // FC
                eng.wait_ge(hid_used, at(hid_used, g, q + 1))
                if e == NS - 1:
                    if after(g, 1):
                        eng.wait_ge(moe_turned, at(moe_turned, g - 1, 1))
                    nc.vector.tensor_scalar(moe[:], down_bank[:], sb2_sum[:], None, ALU.add).then_inc(down_read, 1)
                else:
                    r = e - NS
                    if r >= 2:
                        eng.wait_ge(moe_added, at(moe_added, g, r - 1))
                    elif after(g, 1):
                        eng.wait_ge(moe_added, at(moe_added, g - 1, NE + r - 1))
                    nc.vector.scalar_tensor_tensor(part[:, r % 2, :], down_bank[:], rb2_s[:, r:r + 1],
                                                   share_b[:, r % 2, :], ALU.add, ALU.mult).then_inc(down_read, 1)

            def experts(g, b, kind, q):
                if kind == "hidden":
                    hidden(g, q)
                else:
                    expert_sum(g, q)

            def layer2(g, b, kind, n=0):
                b0, b1 = sec_bank
                if kind == "pre" and n == 0:
                    eng.wait_ge(moe_turned, at(moe_turned, g, 1))
                    nc.vector.tensor_tensor(h2[:].rearrange("p t c -> p (t c)"), b0[:],
                                            h1[b][:].rearrange("p t c -> p (t c)"), ALU.add).then_inc(h2_ready, 1)
                elif kind == "pre" and n == 1:
                    moments(g, h2, h2_ready, 1, mo3, mv3, ve3, mom3)
                elif kind == "pre" and n == 2:
                    normalise(g, x3, h2, mv3, rs3, rstd3, x3_ready)
                elif kind == "pre" and n in (3, 4):
                    for k, table in enumerate((cos, sin)):
                        m = 2 * (n - 3) + k
                        eng.wait_ge(rope_done, at(rope_done, g, m + 1))
                        if n == 4 and k == 0:
                            eng.wait_ge(rope_added, at(rope_added, g, 1))
                        elif n == 3 and k == 0 and after(g, 1):
                            eng.wait_ge(rope_added, at(rope_added, g - 1, 2))
                        nc.vector.tensor_tensor(roped[:, k, :].rearrange("p (i l) -> p i l", i=GI),
                                                sec_bank[k][:].rearrange("p (i l) -> p i l", i=GI),
                                                table[:].unsqueeze(1).to_broadcast([P, GI, L]), ALU.mult) \
                          .then_inc(rope_read, 1)
                elif kind == "pre" and n == 5:
                    eng.wait_ge(x3t_ready, at(x3t_ready, g, 1))
                    tok = x3t[:].rearrange("p (i l) -> p i l", i=GI)
                    for r in range(RATIO):
                        src = tok[:, :, r:r + STRIDE * (LC - 1) + 1:STRIDE]
                        if r == 0:
                            nc.vector.tensor_scalar(xc[:], src, cg[:, 0:1], None, ALU.mult).then_inc(xc_step, 1)
                        else:
                            eng.wait_ge(xc_step, at(xc_step, g, r))
                            nc.vector.scalar_tensor_tensor(xc[:], src, cg[:, r:r + 1], xc[:], ALU.mult, ALU.add) \
                              .then_inc(xc_step, 1)
                elif kind == "score":
                    half = n % 2
                    scores = sec_bank[half][:, 0:HH * (LK + 1)].rearrange("p (h k) -> p h k", h=HH)
                    eng.wait_ge(scored, at(scored, g, n + 1))
                    nc.vector.tensor_reduce(m3[:, half, :], scores, AX.X, ALU.max).then_inc(s3_step, 1)
                    eng.wait_ge(s3_step, at(s3_step, g, 2 * n + 1))
                    nc.vector.tensor_tensor(e3[:, n], scores, m3[:, half, :].unsqueeze(2).to_broadcast([P, HH, LK + 1]),
                                            ALU.subtract).then_inc(s3_step, 1)
                elif kind == "value":
                    t, half = n // 2, n % 2
                    eng.wait_ge(o3_done, at(o3_done, g, n + 1))
                    made_o = b1[:, 0:HH * (HD + 1)].rearrange("p (h d) -> p h d", h=HH)
                    nc.vector.reciprocal(inv3[:, n, :], made_o[:, :, HD]).then_inc(inv3_ready, 1)
                    cols = slice(half * HH * HD, (half + 1) * HH * HD)
                    eng.wait_ge(inv3_ready, at(inv3_ready, g, n + 1))
                    nc.vector.tensor_tensor(o3[:, t, cols].rearrange("p (h d) -> p h d", h=HH), made_o[:, :, 0:HD],
                                            inv3[:, n, :].unsqueeze(2).to_broadcast([P, HH, HD]), ALU.mult) \
                      .then_inc(o3_ready, 1)
                elif kind == "post" and n == 1:
                    eng.wait_ge(wo_done, at(wo_done, g, 1))
                    if after(g, 1):
                        eng.wait_ge(res_stored, at(res_stored, g - 1, 16))
                    nc.vector.tensor_tensor(h3[:].rearrange("p t c -> p (t c)"), b1[:],
                                            h2[:].rearrange("p t c -> p (t c)"), ALU.add).then_inc(h3_ready, 1)
                elif kind == "post" and n == 2:
                    moments(g, h3, h3_ready, 1, mo4, mv4, ve4, mom4)
                elif kind == "post" and n == 3:
                    normalise(g, x3, h3, mv4, rs4, rstd4, x4_ready)
                elif kind == "post" and n == 5:
                    eng.wait_ge(mlp_done, at(mlp_done, g, 1))
                    eng.wait_ge(h3b_ready, at(h3b_ready, g, 1))
                    nc.vector.tensor_tensor(res[:].rearrange("p t c -> p (t c)"), b0[:],
                                            h3b[:].rearrange("p t c -> p (t c)"), ALU.add).then_inc(res_ready, 1)

            def iteration(i, where):
                if where == 1:
                    setup()
                for g, b, stage, piece in pieces(PLAN["dve"], i, where):
                    {"tok": tokens, "att": attention, "ffn": experts, "sec": layer2, "set": weights}[stage](g, b, *piece)

            schedule(iteration)(eng)

        @block.gpsimd
        def _(eng):
            def setup():
                nc.gpsimd.memset(values[:], 0.0).then_inc(ready_p, 1)
                eng.wait_ge(ready_p, 1)
                nc.gpsimd.memset(values[:, :, :, HD:HD + 1], 1.0).then_inc(ready_p, 1)
                eng.wait_ge(consts_in, CONSTS)
                for w in (tw1_s, tw2_s):
                    nc.gpsimd.affine_select(out=w[:], in_=w[:], compare_op=ALU.is_ge, fill=0.0, base=0,
                                            pattern=[[1, P]], channel_multiplier=-1).then_inc(ready_p, 1)

            def weights(g, b, kind, n):
                src, _, _, e = lots[n]
                if n >= STAGING:
                    eng.wait_ge(weight_low, n - STAGING + 1)
                eng.dma_start(staging[n % STAGING], src[:, e, :]).then_inc(weight_in[n % STAGING], 16)

            def inverse_root(g, rs, ve, mom, rstd):
                eng.wait_ge(mom, at(mom, g, 10))
                nc.gpsimd.tensor_tensor(rs[:], ve[:], power[:], ALU.pow).then_inc(rstd, 1)

            def attention(g, b, n):
                if n == 0:
                    inverse_root(g, rs1, ve1, mom1, rstd1)
                elif n == 9:
                    inverse_root(g, rs2, ve2, mom2, rstd2)
                elif n == 11:
                    eng.wait_ge(gate_step, at(gate_step, g, 3))
                    nc.gpsimd.tensor_tensor(ez[:].rearrange("p t e -> p (t e)"), euler[:],
                                            lg[:].rearrange("p t e -> p (t e)"), ALU.pow).then_inc(gate_exp, 1)

            def tokens(g, b, kind, u=0, k=0):
                if kind == "ends":
                    eng.wait_ge(ends_high, at(ends_high, g, 2 * u + k + 1))
                    nc.gpsimd.tensor_tensor(halves[k][:, :, 2:7:4, 1, :], blocks[k][:, :, 0:8:7, :],
                                            halves[k][:, :, 2:7:4, 0, :], ALU.subtract).then_inc(ends_low, 1)
                    return
                half, k = k // 2, k % 2
                v = blocks[half]
                if k == 0:
                    eng.wait_ge(x_paired, at(x_paired, g, 2 * u + half + 1))
                else:
                    eng.wait_ge(x_summed, at(x_summed, g, 4 * u + 2 * half + 1))
                nc.gpsimd.tensor_tensor(v[:, :, 1, :], v[:, :, 1, :], v[:, :, 2 * k + 3, :], ALU.add) \
                  .then_inc(x_summed, 1)

            def experts(g, b, kind, q):
                r = q // FC - NS
                if kind == "hidden":
                    eng.wait_ge(hid_made, at(hid_made, g, made(first[q] + 1)))
                    nc.gpsimd.tensor_tensor(hid_l[:, q % RING, :], hid[:, q % HIDS, :], hid_h[:, q % RING, :],
                                            ALU.subtract).then_inc(hid_rest_p, 1)
                    return
                if r >= 0:
                    eng.wait_ge(down_read, at(down_read, g, 2 + r))
                    if r >= 1:
                        eng.wait_ge(moe_added, at(moe_added, g, r))
                    nc.gpsimd.tensor_tensor(moe[:], moe[:], part[:, r % 2, :], ALU.add).then_inc(moe_added, 1)

            def layer2(g, b, kind, n=0):
                if kind == "pre" and n == 1:
                    inverse_root(g, rs3, ve3, mom3, rstd3)
                elif kind == "pre" and n == 3:
                    eng.wait_ge(rope_read, at(rope_read, g, 2))
                    if after(g, 1):
                        eng.wait_ge(scored, at(scored, g - 1, 8))
                    nc.gpsimd.tensor_tensor(q3[:], roped[:, 0, :], roped[:, 1, :], ALU.add).then_inc(rope_added, 1)
                elif kind == "pre" and n == 4:
                    eng.wait_ge(rope_read, at(rope_read, g, 4))
                    if after(g, 1):
                        eng.wait_ge(keys_ready, at(keys_ready, g - 1, 4))
                    nc.gpsimd.tensor_tensor(keys[:, :, 0:L], roped[:, 0, :].rearrange("p (i l) -> p i l", i=GI),
                                            roped[:, 1, :].rearrange("p (i l) -> p i l", i=GI), ALU.add) \
                      .then_inc(rope_added, 1)
                elif (kind == "pre" and n in (6, 7)) or (kind == "score" and n in (2, 4)):
                    t = n - 6 if kind == "pre" else n // 2 + 1
                    if t == 0:
                        eng.wait_ge(rope_added, at(rope_added, g, 2))
                        eng.wait_ge(kc_ready, at(kc_ready, g, 1))
                    if t >= 2:
                        eng.wait_ge(scored, at(scored, g, 2 * (t - 1)))
                    for im in range(2):
                        four = [P, HEADS, LK]
                        ins = nc.gpsimd.tensor_tensor(keys_h[:, t % 2, im],
                                                      keys[:, 2 * t + im, :].unsqueeze(1).to_broadcast(four),
                                                      heads[:].unsqueeze(2).to_broadcast(four), ALU.mult)
                    ins.then_inc(keys_ready, 1)
                elif kind == "post" and n == 1:
                    eng.wait_ge(h3_ready, at(h3_ready, g, 1))
                    if after(g, 1):
                        eng.wait_ge(res_ready, at(res_ready, g - 1, 1))
                    nc.gpsimd.tensor_tensor(h3b[:], h3[:], tb2_s[:].unsqueeze(1).to_broadcast([P, T, C]), ALU.add) \
                      .then_inc(h3b_ready, 1)
                elif kind == "post" and n == 2:
                    inverse_root(g, rs4, ve4, mom4, rstd4)

            def iteration(i, where):
                if where == 1:
                    setup()
                for g, b, stage, piece in pieces(PLAN["pool"], i, where):
                    {"tok": tokens, "att": attention, "ffn": experts, "sec": layer2, "set": weights}[stage](g, b, *piece)

            schedule(iteration)(eng)


def kernel(**inputs):
    import numpy as _np
    import concourse.bacc as _bacc
    from concourse import mybir as _mybir
    from concourse.bass_utils import run_bass_kernel_spmd as _run

    a = {k: _np.asarray(v) for k, v in inputs.items()}
    f32 = _np.float32

    def rows(v):
        v = v.reshape(1, -1)
        return _np.broadcast_to(v, (P, v.shape[1]))

    def halves(w):
        return w.reshape(HEADS, 2, HD // 2, C)[:, ::-1].reshape(C, C)

    pix, tok = _np.arange(HW), _np.arange(L)
    block = _np.zeros((2, HW, 3, 2, BX), f32)
    for dy in range(3):
        for by in range(BX):
            on = (pix >= by * 8 + dy - 1) & (pix <= by * 8 + 7 + dy - 1)
            for im in range(2):
                block[im, on, dy, im, by] = 1
    half = HD // 2
    freq = (f32(1.0) / _np.power(f32(10000.0), _np.arange(half, dtype=f32) / f32(half))).astype(f32)
    angle = tok.astype(f32)[None, :] * freq[:, None]
    cos = _np.tile(_np.cos(angle), (2 * HEADS, 1)).astype(f32)
    sin = _np.tile(_np.concatenate([-_np.sin(angle), _np.sin(angle)]), (HEADS, 1)).astype(f32)
    image = _np.arange(P) // L
    mask1 = _np.where(image[:, None] == image[None, :], f32(0), f32(-1e30))
    window = (tok[:, None] >= tok[None, :]) & (tok[:, None] - tok[None, :] < 128)
    comp = tok[:, None] >= (_np.arange(LC) * STRIDE + RATIO - 1)[None, :]
    limit = _np.zeros((L + 3, HEADS, LK + 1), f32)
    limit[:L, :, :LK] = _np.where(_np.concatenate([window, comp], 1), f32(0), f32(-1e30))[:, None, :]
    place = _np.ones((L + 3, P), f32)
    place[:L] = tok[:, None] == (_np.arange(P) % L)[None, :]
    part = _np.zeros((P, 3), f32)
    part[L:L + 3] = _np.eye(3)
    heads = (_np.arange(C)[:, None] // HD == _np.arange(HEADS)[None, :]).astype(f32)
    pick = _np.tile(_np.eye(NE, dtype=f32)[:, :, None], (3, 1, P))
    tie = _np.broadcast_to(_np.tril(_np.ones((NE, NE), f32), -1), (P, NE, NE))

    w1 = _np.concatenate([a["L0_ffn_sw1"], a["L0_ffn_rw1"]])
    w2 = _np.concatenate([a["L0_ffn_sw2"], a["L0_ffn_rw2"]])
    b1 = _np.concatenate([a["L0_ffn_sb1"], a["L0_ffn_rb1"]])
    named = dict(
        x=a["x"], conv_w=a["L0_tok_conv_w"].reshape(9, C).T, conv_b=a["L0_tok_conv_b"].reshape(C, 1),
        wq=a["L0_attn_Wq"], bq=a["L0_attn_bq"].reshape(C, 1), wk=a["L0_attn_Wk"], bk=a["L0_attn_bk"].reshape(C, 1),
        gate_w=a["L0_ffn_gate_w"].T, gate_b=rows(a["L0_ffn_gate_b"]),
        w1=w1.transpose(2, 0, 1), b1=b1.reshape(CH, P).T,
        w2=w2.reshape(NX, C, FC, P).transpose(3, 0, 2, 1).reshape(P, NX, F),
        sb2=a["L0_ffn_sb2"].T, rb2=a["L0_ffn_rb2"].T,
        swq=a["L1_attn_wq"].T, swqs=halves(a["L1_attn_wq"]).T, swk=a["L1_attn_wk"].T, swks=halves(a["L1_attn_wk"]).T,
        swv=a["L1_attn_wv"].T, swkc=a["L1_attn_wk_c"].T, swvc=a["L1_attn_wv_c"].T, swo=a["L1_attn_wo"].T,
        comp_gate=rows(a["L1_attn_gate_logits"]), sink=rows(a["L1_attn_sink_logit"]),
        tw1=a["L1_ffn_W1"].T, tb1=a["L1_ffn_b1"].reshape(P, 1), tw2=a["L1_ffn_W2"].T, tb2=rows(a["L1_ffn_b2"]),
        ident_c=_np.eye(P, dtype=f32), block_c=block.reshape(P, PB), cos_c=cos, sin_c=sin, mask1_c=mask1,
        limit_c=limit.reshape(L + 3, HEADS * (LK + 1)), place_c=place, part_c=part, heads_c=heads, pick_c=pick, tie_c=tie)

    nc = _bacc.Bacc("TRN2", target_bir_lowering=False, num_devices=1)
    arrays, args = {}, {}
    for name, value in named.items():
        value = _np.ascontiguousarray(value)
        arrays[f"in_{name}"] = value
        args[name] = nc.dram_tensor(f"in_{name}", value.shape, _mybir.dt.from_np(value.dtype), kind="ExternalInput").ap()
    args["out"] = nc.dram_tensor("out_0", (NI, L, C), _mybir.dt.float32, kind="ExternalOutput").ap()
    program(nc, **args)
    r = _run(nc, [arrays], core_ids=[0])
    return r.results[0]["out_0"]
```
